# Optimizing a Trainium2 kernel written in Bass

```python
import numpy as np
import jax
import jax.numpy as jnp

def _softmax(x, axis=-1):
    return jax.nn.softmax(x, axis=axis)

def _gelu(x):
    return jax.nn.gelu(x, approximate=True)

def _silu(x):
    return jax.nn.silu(x)

def _sigmoid(x):
    return jax.nn.sigmoid(x)

def _layernorm(x, axis=-1, eps=1e-05):
    m = jnp.mean(x, axis=axis, keepdims=True)
    v = jnp.var(x, axis=axis, keepdims=True)
    return (x - m) / jnp.sqrt(v + eps)

def _scatter_add(tgt, idx, src, axis=0):
    return tgt.at[idx].add(src)

def _segment_sum(src, seg, n):
    return jax.ops.segment_sum(src, seg, n)
kernel_name = 'mk_gps_d2_gnn_r32_378e4a'

def setup_inputs(seed: int=0):
    np.random.seed(seed)
    _w = jnp.asarray

    def _rec_inputs():
        import jax
        import jax.numpy as jnp
        _gk = jax.random.key(seed)
        x = -0.0002928 + 1 * jax.random.normal(jax.random.fold_in(_gk, 1), (256, 512), jnp.float32)
        _s = jax.random.randint(jax.random.fold_in(_gk, 2), (2048,), 0, 256, jnp.int32)
        _d = jax.random.randint(jax.random.fold_in(_gk, 3), (2048,), 0, 256, jnp.int32)
        _loop = jnp.arange(256, dtype=jnp.int32)
        src = jnp.concatenate([_s, _d, _loop])
        dst = jnp.concatenate([_d, _s, _loop])
        _o = jnp.argsort(dst, stable=True)
        src = src[_o]
        dst = dst[_o]
        edge_weight = jax.random.uniform(jax.random.fold_in(_gk, 13), (4352,), jnp.float32, 0.0, 0.999994)
        edge_weight1 = jax.random.uniform(jax.random.fold_in(_gk, 14), (4352, 1), jnp.float32, 0.0, 0.999994)
        return (x, src, dst, edge_weight, edge_weight1)
    x, src, dst, edge_weight, edge_weight1 = _rec_inputs()

    def _L0_gnn_setup():
        import jax, jax.numpy as jnp
        import numpy as np
        N_NODES = 256
        D_MODEL = 512
        N_LAYERS = 2
        N_EDGES = 8192
        LEAKY_SLOPE = 0.01

        def _normalized_adj(edge_index, edge_weights, num_nodes):
            A = jnp.zeros((num_nodes, num_nodes), dtype=edge_weights.dtype)
            A = A.at[edge_index[0], edge_index[1]].add(edge_weights)
            deg = jnp.sum(A, axis=1)
            dinv = jnp.where(deg > 0, deg ** (-0.5), 0.0)
            return dinv[:, None] * A * dinv[None, :]
        key = jax.random.key(seed)
        ks = jax.random.split(key, 6)
        x = jax.random.normal(ks[0], (N_NODES, D_MODEL), dtype=jnp.float32)
        edge_weights = jax.random.uniform(ks[1], (N_EDGES,), dtype=jnp.float32)
        edge_index = jax.random.randint(ks[2], (2, N_EDGES), 0, N_NODES, dtype=jnp.int64)
        scale = 0.02
        W_gcn = jax.random.normal(ks[3], (N_LAYERS, D_MODEL, D_MODEL), dtype=jnp.float32) * scale
        b_gcn = jnp.zeros((N_LAYERS, D_MODEL), dtype=jnp.float32)
        W_mlp = jax.random.normal(ks[4], (N_LAYERS, D_MODEL, D_MODEL), dtype=jnp.float32) * scale
        b_mlp = jnp.zeros((N_LAYERS, D_MODEL), dtype=jnp.float32)
        return {'x': x, 'edge_weights': edge_weights, 'W_gcn': W_gcn, 'b_gcn': b_gcn, 'W_mlp': W_mlp, 'b_mlp': b_mlp, 'edge_index': edge_index}
    _L0_gnn_all = _L0_gnn_setup()
    _L0_gnn_in = {k: v for k, v in _L0_gnn_all.items() if k in ('W_gcn', 'b_gcn', 'W_mlp', 'b_mlp')}
    del _L0_gnn_all

    def _L0_mix_setup():
        import jax, jax.numpy as jnp
        import numpy as np
        HEADS = 8
        DIM_HEAD = 64
        EPS = 1e-05

        def layer_norm(x, gamma):
            mu = jnp.mean(x, axis=-1, keepdims=True)
            var = jnp.var(x, axis=-1, keepdims=True)
            return (x - mu) * jax.lax.rsqrt(var + EPS) * gamma
        key = jax.random.key(seed)
        k1, k2, k3 = jax.random.split(key, 3)
        b, n, dim = (4, 512, 512)
        hidden = HEADS * DIM_HEAD
        x = jax.random.normal(k1, (b, n, dim), dtype=jnp.float32)
        norm_gamma = jnp.ones((dim,), dtype=jnp.float32)
        w_qkv = jax.random.normal(k2, (hidden * 3, dim), dtype=jnp.float32) * dim ** (-0.5)
        w_out = jax.random.normal(k3, (dim, hidden), dtype=jnp.float32) * hidden ** (-0.5)
        out_gamma = jnp.ones((dim,), dtype=jnp.float32)
        return {'x': x, 'norm_gamma': norm_gamma, 'w_qkv': w_qkv, 'w_out': w_out, 'out_gamma': out_gamma}
    _L0_mix_all = _L0_mix_setup()
    _L0_mix_in = {k: v for k, v in _L0_mix_all.items() if k in ('norm_gamma', 'w_qkv', 'w_out', 'out_gamma')}
    del _L0_mix_all

    def _L0_ffn_setup():
        import jax, jax.numpy as jnp
        import numpy as np
        S, B, D, F, E, K = (1024, 2, 512, 64, 8, 2)
        key = jax.random.key(seed)
        ks = jax.random.split(key, 12)
        s = lambda *sh: 1.0 / np.sqrt(sh[0])
        inp = {'x': jax.random.normal(ks[0], (S, B, D), dtype=jnp.float32), 'Wg': jax.random.normal(ks[1], (D, E), dtype=jnp.float32) * s(D), 'bg': jnp.zeros((E,), dtype=jnp.float32), 'W1': jax.random.normal(ks[2], (E, D, F), dtype=jnp.float32) * s(D), 'b1': jnp.zeros((E, F), dtype=jnp.float32), 'W2': jax.random.normal(ks[3], (E, F, D), dtype=jnp.float32) * s(F), 'b2': jnp.zeros((E, D), dtype=jnp.float32), 'Ws1': jax.random.normal(ks[4], (D, F), dtype=jnp.float32) * s(D), 'bs1': jnp.zeros((F,), dtype=jnp.float32), 'Ws2': jax.random.normal(ks[5], (F, D), dtype=jnp.float32) * s(F), 'bs2': jnp.zeros((D,), dtype=jnp.float32)}
        return inp
    _L0_ffn_all = _L0_ffn_setup()
    _L0_ffn_in = {k: v for k, v in _L0_ffn_all.items() if k in ('Wg', 'bg', 'W1', 'b1', 'W2', 'b2', 'Ws1', 'bs1', 'Ws2', 'bs2')}
    del _L0_ffn_all

    def _L1_gnn_setup():
        import jax, jax.numpy as jnp
        import numpy as np
        N_NODES = 50000
        N_EDGES = 5000
        D_IN = 512
        D_OUT = 512
        key = jax.random.key(seed)
        k1, k2, k3, k4, k5, k6 = jax.random.split(key, 6)
        feature = jax.random.normal(k1, (N_NODES, D_IN), dtype=jnp.float32)
        edge_w = jax.random.uniform(k2, (N_EDGES, 1), dtype=jnp.float32)
        W = jax.random.normal(k3, (D_OUT, D_IN), dtype=jnp.float32) / np.sqrt(D_IN)
        b = jax.random.normal(k4, (D_OUT,), dtype=jnp.float32) * 0.01
        src = jax.random.randint(k5, (N_EDGES,), 0, N_NODES, dtype=jnp.int32)
        dst = jax.random.randint(k6, (N_EDGES,), 0, N_NODES, dtype=jnp.int32)
        return {'feature': feature, 'edge_w': edge_w, 'W': W, 'b': b, 'src': src, 'dst': dst}
    _L1_gnn_all = _L1_gnn_setup()
    _L1_gnn_in = {k: v for k, v in _L1_gnn_all.items() if k in ('W', 'b')}
    del _L1_gnn_all

    def _L1_mix_setup():
        import jax, jax.numpy as jnp
        import numpy as np
        HEADS = 8
        DIM_HEAD = 64
        key = jax.random.key(seed)
        k1, k2, k3 = jax.random.split(key, 3)
        B, L, D = (8, 128, 512)
        hidden = HEADS * DIM_HEAD
        x = jax.random.normal(k1, (B, L, D), dtype=jnp.float32)
        Wqkv = jax.random.normal(k2, (3 * hidden, D), dtype=jnp.float32) * (1.0 / np.sqrt(D))
        Wout = jax.random.normal(k3, (D, hidden), dtype=jnp.float32) * (1.0 / np.sqrt(hidden))
        bout = jnp.zeros((D,), dtype=jnp.float32)
        return {'x': x, 'Wqkv': Wqkv, 'Wout': Wout, 'bout': bout}
    _L1_mix_all = _L1_mix_setup()
    _L1_mix_in = {k: v for k, v in _L1_mix_all.items() if k in ('Wqkv', 'Wout', 'bout')}
    del _L1_mix_all

    def _L1_ffn_setup():
        import jax, jax.numpy as jnp
        import numpy as np
        E, TOPK, H, DK, DV, D = (4, 2, 8, 64, 64, 512)
        B, L = (4, 1024)
        VDIM = H * DV

        def _silu(x):
            return x * jax.nn.sigmoid(x)

        def _l2norm(x):
            return x * jax.lax.rsqrt(jnp.sum(x * x, axis=-1, keepdims=True) + 1e-06)

        def _forward(h, Wq, Wgate, Wk, Wv, Wb, Wa, A_log, dt_bias, Wg, o_norm_weight, Wo):
            Bs, Ls, _ = h.shape
            scores = jax.nn.softmax((h @ Wgate).astype(jnp.float32), axis=-1)
            rw, sel = jax.lax.top_k(scores, TOPK)
            rw = rw / jnp.sum(rw, axis=-1, keepdims=True)
            bi = jnp.arange(Bs)[:, None, None]
            li = jnp.arange(Ls)[None, :, None]
            w_full = jnp.zeros((Bs, Ls, E), jnp.float32).at[bi, li, sel].set(rw)
            m = jnp.transpose(w_full > 0, (2, 0, 1))
            q = _l2norm(_silu(h @ Wq).reshape(Bs, Ls, H, DK))
            k = _l2norm(_silu(h @ Wk).reshape(Bs, Ls, H, DK))
            v = _silu(h @ Wv).reshape(Bs, Ls, H, DV)
            beta = jax.nn.sigmoid(h @ Wb)
            g = -jnp.exp(A_log) * jax.nn.softplus((h @ Wa).astype(jnp.float32) + dt_bias)
            beta_e = beta[None] * m[..., None]
            g_e = jnp.where(m[..., None], g[None], 0.0)
            scale = DK ** (-0.5)
            xs = (jnp.moveaxis(q, 1, 0), jnp.moveaxis(k, 1, 0), jnp.moveaxis(v, 1, 0), jnp.moveaxis(beta_e, 2, 0), jnp.moveaxis(g_e, 2, 0))

            def step(S, x):
                qt, kt, vt, bt, gt = x
                S = S * jnp.exp(gt)[..., None, None]
                kv = jnp.einsum('bhk,ebhkv->ebhv', kt, S)
                delta = (vt[None] - kv) * bt[..., None]
                S = S + kt[None, :, :, :, None] * delta[..., None, :]
                ot = jnp.einsum('bhk,ebhkv->ebhv', qt * scale, S)
                return (S, ot)
            S0 = jnp.zeros((E, Bs, H, DK, DV), jnp.float32)
            _, o = jax.lax.scan(step, S0, xs)
            o = jnp.moveaxis(o, 0, 2)
            core = jnp.einsum('ble,eblhv->blhv', w_full, o)
            gate = _silu((h @ Wg).reshape(Bs, Ls, H, DV))
            core = core * jax.lax.rsqrt(jnp.mean(core * core, axis=-1, keepdims=True) + 1e-05)
            core = core * o_norm_weight * gate
            return core.reshape(Bs, Ls, VDIM) @ Wo
        key = jax.random.key(seed)
        ks = jax.random.split(key, 12)
        std = 0.02
        h = jax.random.normal(ks[0], (B, L, D), jnp.float32)
        Wq = jax.random.normal(ks[1], (D, H * DK), jnp.float32) * std
        Wgate = jax.random.normal(ks[2], (D, E), jnp.float32) * std
        Wk = jax.random.normal(ks[3], (D, H * DK), jnp.float32) * std
        Wv = jax.random.normal(ks[4], (D, VDIM), jnp.float32) * std
        Wb = jax.random.normal(ks[5], (D, H), jnp.float32) * std
        Wa = jax.random.normal(ks[6], (D, H), jnp.float32) * std
        Wg = jax.random.normal(ks[7], (D, VDIM), jnp.float32) * std
        Wo = jax.random.normal(ks[8], (VDIM, D), jnp.float32) * std
        A = jax.random.uniform(ks[9], (H,), jnp.float32, 0.0001, 16.0)
        A_log = jnp.log(A)
        dt = jnp.exp(jax.random.uniform(ks[10], (H,), jnp.float32) * (np.float32(np.log(0.1)) - np.float32(np.log(0.001))) + np.float32(np.log(0.001)))
        dt = jnp.maximum(dt, 0.0001)
        dt_bias = dt + jnp.log(-jnp.expm1(-dt))
        o_norm_weight = jnp.ones((DV,), jnp.float32)
        return {'hidden_states': h, 'Wq': Wq, 'Wgate': Wgate, 'Wk': Wk, 'Wv': Wv, 'Wb': Wb, 'Wa': Wa, 'A_log': A_log, 'dt_bias': dt_bias, 'Wg': Wg, 'o_norm_weight': o_norm_weight, 'Wo': Wo}
    _L1_ffn_all = _L1_ffn_setup()
    _L1_ffn_in = {k: v for k, v in _L1_ffn_all.items() if k in ('Wq', 'Wgate', 'Wk', 'Wv', 'Wb', 'Wa', 'A_log', 'dt_bias', 'Wg', 'o_norm_weight', 'Wo')}
    del _L1_ffn_all
    return {'x': x, 'src': src, 'dst': dst, 'edge_weight': edge_weight, 'edge_weight1': edge_weight1, 'L0_gnn_W_gcn': _L0_gnn_in['W_gcn'], 'L0_gnn_b_gcn': _L0_gnn_in['b_gcn'], 'L0_gnn_W_mlp': _L0_gnn_in['W_mlp'], 'L0_gnn_b_mlp': _L0_gnn_in['b_mlp'], 'L0_mix_norm_gamma': _L0_mix_in['norm_gamma'], 'L0_mix_w_qkv': _L0_mix_in['w_qkv'], 'L0_mix_w_out': _L0_mix_in['w_out'], 'L0_mix_out_gamma': _L0_mix_in['out_gamma'], 'L0_ffn_Wg': _L0_ffn_in['Wg'], 'L0_ffn_bg': _L0_ffn_in['bg'], 'L0_ffn_W1': _L0_ffn_in['W1'], 'L0_ffn_b1': _L0_ffn_in['b1'], 'L0_ffn_W2': _L0_ffn_in['W2'], 'L0_ffn_b2': _L0_ffn_in['b2'], 'L0_ffn_Ws1': _L0_ffn_in['Ws1'], 'L0_ffn_bs1': _L0_ffn_in['bs1'], 'L0_ffn_Ws2': _L0_ffn_in['Ws2'], 'L0_ffn_bs2': _L0_ffn_in['bs2'], 'L1_gnn_W': _L1_gnn_in['W'], 'L1_gnn_b': _L1_gnn_in['b'], 'L1_mix_Wqkv': _L1_mix_in['Wqkv'], 'L1_mix_Wout': _L1_mix_in['Wout'], 'L1_mix_bout': _L1_mix_in['bout'], 'L1_ffn_Wq': _L1_ffn_in['Wq'], 'L1_ffn_Wgate': _L1_ffn_in['Wgate'], 'L1_ffn_Wk': _L1_ffn_in['Wk'], 'L1_ffn_Wv': _L1_ffn_in['Wv'], 'L1_ffn_Wb': _L1_ffn_in['Wb'], 'L1_ffn_Wa': _L1_ffn_in['Wa'], 'L1_ffn_A_log': _L1_ffn_in['A_log'], 'L1_ffn_dt_bias': _L1_ffn_in['dt_bias'], 'L1_ffn_Wg': _L1_ffn_in['Wg'], 'L1_ffn_o_norm_weight': _L1_ffn_in['o_norm_weight'], 'L1_ffn_Wo': _L1_ffn_in['Wo']}

def reference(x, src, dst, edge_weight, edge_weight1, L0_gnn_W_gcn, L0_gnn_b_gcn, L0_gnn_W_mlp, L0_gnn_b_mlp, L0_mix_norm_gamma, L0_mix_w_qkv, L0_mix_w_out, L0_mix_out_gamma, L0_ffn_Wg, L0_ffn_bg, L0_ffn_W1, L0_ffn_b1, L0_ffn_W2, L0_ffn_b2, L0_ffn_Ws1, L0_ffn_bs1, L0_ffn_Ws2, L0_ffn_bs2, L1_gnn_W, L1_gnn_b, L1_mix_Wqkv, L1_mix_Wout, L1_mix_bout, L1_ffn_Wq, L1_ffn_Wgate, L1_ffn_Wk, L1_ffn_Wv, L1_ffn_Wb, L1_ffn_Wa, L1_ffn_A_log, L1_ffn_dt_bias, L1_ffn_Wg, L1_ffn_o_norm_weight, L1_ffn_Wo):
    import jax
    import jax.numpy as jnp

    def _L0_gnn_ref(x, edge_weights, W_gcn, b_gcn, W_mlp, b_mlp, edge_index):
        import jax, jax.numpy as jnp
        import numpy as np
        N_NODES = 256
        D_MODEL = 512
        N_LAYERS = 2
        N_EDGES = 8192
        LEAKY_SLOPE = 0.01

        def _normalized_adj(edge_index, edge_weights, num_nodes):
            A = jnp.zeros((num_nodes, num_nodes), dtype=edge_weights.dtype)
            A = A.at[edge_index[0], edge_index[1]].add(edge_weights)
            deg = jnp.sum(A, axis=1)
            dinv = jnp.where(deg > 0, deg ** (-0.5), 0.0)
            return dinv[:, None] * A * dinv[None, :]
        N = x.shape[0]
        A_norm = _normalized_adj(edge_index, edge_weights, N)
        h = x
        for l in range(W_gcn.shape[0]):
            h = A_norm @ h
            h = h @ W_gcn[l] + b_gcn[l]
            h = jax.nn.leaky_relu(h @ W_mlp[l] + b_mlp[l], negative_slope=LEAKY_SLOPE)
        return h

    def _L0_mix_ref(x, norm_gamma, w_qkv, w_out, out_gamma):
        import jax, jax.numpy as jnp
        import numpy as np
        HEADS = 8
        DIM_HEAD = 64
        EPS = 1e-05

        def layer_norm(x, gamma):
            mu = jnp.mean(x, axis=-1, keepdims=True)
            var = jnp.var(x, axis=-1, keepdims=True)
            return (x - mu) * jax.lax.rsqrt(var + EPS) * gamma
        b, n, dim = x.shape
        h, d = (HEADS, DIM_HEAD)
        scale = d ** (-0.5)
        x = layer_norm(x, norm_gamma)
        qkv = jnp.einsum('bnc,fc->bnf', x, w_qkv)
        q, k, v = jnp.split(qkv, 3, axis=-1)
        to_bhnd = lambda t: t.reshape(b, n, h, d).transpose(0, 2, 1, 3)
        q, k, v = (to_bhnd(q), to_bhnd(k), to_bhnd(v))
        q = jax.nn.softmax(q, axis=-1) * scale
        k = jax.nn.softmax(k, axis=-2)
        context = jnp.einsum('bhnd,bhne->bhde', k, v)
        out = jnp.einsum('bhde,bhnd->bhne', context, q)
        out = out.transpose(0, 2, 1, 3).reshape(b, n, h * d)
        out = jnp.einsum('bnf,cf->bnc', out, w_out)
        return layer_norm(out, out_gamma)

    def _L0_ffn_ref(x, Wg, bg, W1, b1, W2, b2, Ws1, bs1, Ws2, bs2):
        import jax, jax.numpy as jnp
        import numpy as np
        S, B, D, F, E, K = (1024, 2, 512, 64, 8, 2)
        gate_logits = jnp.einsum('sbd,de->sbe', x, Wg) + bg
        weights, selected = jax.lax.top_k(gate_logits, K)
        weights = jax.nn.softmax(weights.astype(jnp.float32), axis=-1)
        onehot = jax.nn.one_hot(selected, E, dtype=weights.dtype)
        comb = jnp.einsum('sbk,sbke->sbe', weights, onehot)
        h = jax.nn.relu(jnp.einsum('sbd,edf->sbef', x, W1) + b1)
        y = jnp.einsum('sbef,efd->sbed', h, W2) + b2
        out = jnp.einsum('sbe,sbed->sbd', comb, y)
        hs = jax.nn.relu(jnp.einsum('sbd,df->sbf', x, Ws1) + bs1)
        shared = jnp.einsum('sbf,fd->sbd', hs, Ws2) + bs2
        out = out + 1.0 / K * shared
        return out

    def _L1_gnn_ref(feature, edge_w, W, b, src, dst):
        import jax, jax.numpy as jnp
        import numpy as np
        N_NODES = 50000
        N_EDGES = 5000
        D_IN = 512
        D_OUT = 512
        m = feature[src] * edge_w
        agg = jax.ops.segment_sum(m, dst, num_segments=feature.shape[0])
        return agg @ W.T + b

    def _L1_mix_ref(x, Wqkv, Wout, bout):
        import jax, jax.numpy as jnp
        import numpy as np
        HEADS = 8
        DIM_HEAD = 64
        B, L, D = x.shape
        H, C = (HEADS, DIM_HEAD)
        qkv = jnp.einsum('bld,od->bol', x, Wqkv)
        qkv = qkv.reshape(B, 3, H, C, L)
        q, k, v = (qkv[:, 0], qkv[:, 1], qkv[:, 2])
        k = jax.nn.softmax(k, axis=-1)
        q = jax.nn.softmax(q, axis=-2)
        context = jnp.einsum('bhdn,bhen->bhde', k, v)
        out = jnp.einsum('bhde,bhdn->bhen', context, q)
        out = out.reshape(B, H * C, L)
        y = jnp.einsum('bcl,dc->bld', out, Wout) + bout
        return y

    def _L1_ffn_ref(hidden_states, Wq, Wgate, Wk, Wv, Wb, Wa, A_log, dt_bias, Wg, o_norm_weight, Wo):
        import jax, jax.numpy as jnp
        import numpy as np
        E, TOPK, H, DK, DV, D = (4, 2, 8, 64, 64, 512)
        B, L = (4, 1024)
        VDIM = H * DV

        def _silu(x):
            return x * jax.nn.sigmoid(x)

        def _l2norm(x):
            return x * jax.lax.rsqrt(jnp.sum(x * x, axis=-1, keepdims=True) + 1e-06)

        def _forward(h, Wq, Wgate, Wk, Wv, Wb, Wa, A_log, dt_bias, Wg, o_norm_weight, Wo):
            Bs, Ls, _ = h.shape
            scores = jax.nn.softmax((h @ Wgate).astype(jnp.float32), axis=-1)
            rw, sel = jax.lax.top_k(scores, TOPK)
            rw = rw / jnp.sum(rw, axis=-1, keepdims=True)
            bi = jnp.arange(Bs)[:, None, None]
            li = jnp.arange(Ls)[None, :, None]
            w_full = jnp.zeros((Bs, Ls, E), jnp.float32).at[bi, li, sel].set(rw)
            m = jnp.transpose(w_full > 0, (2, 0, 1))
            q = _l2norm(_silu(h @ Wq).reshape(Bs, Ls, H, DK))
            k = _l2norm(_silu(h @ Wk).reshape(Bs, Ls, H, DK))
            v = _silu(h @ Wv).reshape(Bs, Ls, H, DV)
            beta = jax.nn.sigmoid(h @ Wb)
            g = -jnp.exp(A_log) * jax.nn.softplus((h @ Wa).astype(jnp.float32) + dt_bias)
            beta_e = beta[None] * m[..., None]
            g_e = jnp.where(m[..., None], g[None], 0.0)
            scale = DK ** (-0.5)
            xs = (jnp.moveaxis(q, 1, 0), jnp.moveaxis(k, 1, 0), jnp.moveaxis(v, 1, 0), jnp.moveaxis(beta_e, 2, 0), jnp.moveaxis(g_e, 2, 0))

            def step(S, x):
                qt, kt, vt, bt, gt = x
                S = S * jnp.exp(gt)[..., None, None]
                kv = jnp.einsum('bhk,ebhkv->ebhv', kt, S)
                delta = (vt[None] - kv) * bt[..., None]
                S = S + kt[None, :, :, :, None] * delta[..., None, :]
                ot = jnp.einsum('bhk,ebhkv->ebhv', qt * scale, S)
                return (S, ot)
            S0 = jnp.zeros((E, Bs, H, DK, DV), jnp.float32)
            _, o = jax.lax.scan(step, S0, xs)
            o = jnp.moveaxis(o, 0, 2)
            core = jnp.einsum('ble,eblhv->blhv', w_full, o)
            gate = _silu((h @ Wg).reshape(Bs, Ls, H, DV))
            core = core * jax.lax.rsqrt(jnp.mean(core * core, axis=-1, keepdims=True) + 1e-05)
            core = core * o_norm_weight * gate
            return core.reshape(Bs, Ls, VDIM) @ Wo
        return _forward(hidden_states, Wq, Wgate, Wk, Wv, Wb, Wa, A_log, dt_bias, Wg, o_norm_weight, Wo)
    edge_index = jnp.stack([src, dst])
    xn = _layernorm(x, axis=-1)
    x = x + _L0_gnn_ref(xn, edge_weight, L0_gnn_W_gcn, L0_gnn_b_gcn, L0_gnn_W_mlp, L0_gnn_b_mlp, edge_index) + _L0_mix_ref(xn[None], L0_mix_norm_gamma, L0_mix_w_qkv, L0_mix_w_out, L0_mix_out_gamma)[0]
    x = x + _L0_ffn_ref(_layernorm(x, axis=-1)[None], L0_ffn_Wg, L0_ffn_bg, L0_ffn_W1, L0_ffn_b1, L0_ffn_W2, L0_ffn_b2, L0_ffn_Ws1, L0_ffn_bs1, L0_ffn_Ws2, L0_ffn_bs2)[0]
    xn = _layernorm(x, axis=-1)
    x = x + _L1_gnn_ref(xn, edge_weight1, L1_gnn_W, L1_gnn_b, src, dst) + _L1_mix_ref(xn[None], L1_mix_Wqkv, L1_mix_Wout, L1_mix_bout)[0]
    x = x + _L1_ffn_ref(_layernorm(x, axis=-1)[None], L1_ffn_Wq, L1_ffn_Wgate, L1_ffn_Wk, L1_ffn_Wv, L1_ffn_Wb, L1_ffn_Wa, L1_ffn_A_log, L1_ffn_dt_bias, L1_ffn_Wg, L1_ffn_o_norm_weight, L1_ffn_Wo)[0]
    return x

_drawn_inputs = setup_inputs


def setup_inputs(seed=0):
    import zlib

    import numpy as np

    out = dict(_drawn_inputs(seed))
    spreads = {'L0_gnn_b_gcn': (0.0, 0.1),
     'L0_gnn_b_mlp': (0.0, 0.1),
     'L0_mix_norm_gamma': (1.0, 0.2),
     'L0_mix_out_gamma': (1.0, 0.2),
     'L0_ffn_bg': (0.0, 0.1),
     'L0_ffn_b1': (0.0, 0.288),
     'L0_ffn_b2': (0.0, 0.1),
     'L0_ffn_bs1': (0.0, 0.28),
     'L0_ffn_bs2': (0.0, 0.1),
     'L1_mix_bout': (0.0, 0.455),
     'L1_ffn_o_norm_weight': (1.0, 0.6)}
    factors = {'edge_weight': 8.0,
     'L0_gnn_W_gcn': 4.271,
     'L1_gnn_b': 8.0,
     'L1_ffn_Wq': 5.784,
     'L1_ffn_Wgate': 8.0,
     'L1_ffn_Wk': 5.791,
     'L1_ffn_Wv': 5.326,
     'L1_ffn_Wb': 8.0,
     'L1_ffn_Wa': 8.0,
     'L1_ffn_A_log': 8.0,
     'L1_ffn_dt_bias': 8.0,
     'L1_ffn_Wg': 6.193,
     'L1_ffn_Wo': 6.004}
    for name, (base, spread) in spreads.items():
        noise = np.random.default_rng([zlib.crc32(name.encode()), seed]).standard_normal(out[name].shape)
        drawn = base * np.exp(spread * noise) if base else spread * noise
        out[name] = jnp.asarray(drawn.astype(out[name].dtype))
    for name, factor in factors.items():
        out[name] = (out[name] * factor).astype(out[name].dtype)
    return out
```

```python
from contextlib import ExitStack

import concourse.bass as bass
from concourse import mybir

P = 128
N = 256
D = 512
NC = N // P
FC = D // P
HEADS = 8
DH = D // HEADS
UNIT = FC * D
SLOTS = 8
EDGES = 4352
ET = EDGES // P
E0 = 8
E1 = 4
PAIRS = 2 * N
PC = PAIRS // P
LEVELS = [2, 4, 8, 16, 32, 64]
NL = len(LEVELS)
EPS = 1e-5

F32 = mybir.dt.float32
BF16 = mybir.dt.bfloat16
I32 = mybir.dt.int32
ALU = mybir.AluOpType
ACT = mybir.ActivationFunctionType
AX = mybir.AxisListType.X

(U_Q0, U_K0, U_V0, U_O0, U_GCN0, U_MLP0, U_GCN1, U_MLP1, U_W1, U_W2,
 U_Q1, U_K1, U_V1, U_AGG, U_O1, U_DQ, U_DK, U_DV, U_DG, U_DO) = range(20)
UNITS = 20
(R_MLP0, R_MLP1, R_OG, R_B1, R_BOUT, R_ON) = range(6)
ROWS = 6 * D
R_BG, R_ALOG, R_DT = ROWS, ROWS + 8, ROWS + 16
ROWS_ALL = ROWS + 24
C_GCN, C_GAMMA, C_B1, C_BS1 = 0, 8, 12, 16
COLS = 17
G_WG, G_WS1, G_SM = 0, 8, 72
GW = 92


def build(nc, d_x, d_edge, d_ew, d_w, d_rows, d_cols, d_gw, d_b29, d_ws2, d_out):
    with ExitStack() as ctx:
        def sb(name, shape, dt=F32):
            return ctx.enter_context(nc.sbuf_tensor(name, shape, dt))

        def sem(name):
            return ctx.enter_context(nc.semaphore(name))

        class Sems:
            def __init__(self):
                self.made = {}

            def __getitem__(self, name):
                if name not in self.made:
                    self.made[name] = sem("s_" + name)
                return self.made[name]

        S = Sems()

        bank = [ctx.enter_context(nc.psum_tensor(f"bank{i}", [P, 512], F32)) for i in range(8)]

        ring = sb("ring", [P, SLOTS * UNIT])
        xs = sb("xs", [P, NC, D])
        T_n = sb("T_n", [P, NC * D])
        T_a = sb("T_a", [P, NC * D])
        T_b = sb("T_b", [P, NC * D])
        T_c = sb("T_c", [P, NC * D])
        T_d = sb("T_d", [P, NC * D])
        F_a = sb("F_a", [P, FC * N])
        F_b = sb("F_b", [P, FC * N])
        F_c = sb("F_c", [P, FC * N])
        tm = lambda t: t[:, :].rearrange("p (c f) -> p c f", c=NC)
        fm = lambda t: t[:, :].rearrange("p (k n) -> p k n", k=FC)
        rows = sb("rows", [P, ROWS_ALL])
        row = lambda r: rows[:, r * D:(r + 1) * D]
        cols = sb("cols", [P, COLS])
        gw = sb("gw", [P, FC, GW])
        b29 = sb("b29", [E0 + 1, D])
        ws2 = sb("ws2", [DH, D])
        edge_i = sb("edge_i", [P, 2, ET], I32)
        edge_f = sb("edge_f", [P, 2, ET])
        ew = sb("ew", [P, 2, ET])
        ewp = sb("ewp", [P, 3, 2, ET])
        ewb = sb("ewb", [P, 2, ET], BF16)
        iota_b = sb("iota_b", [P, N], BF16)
        iota_f = sb("iota_f", [P, PAIRS])
        ident = sb("ident", [P, P])
        identz = sb("identz", [P, PAIRS])
        ones = sb("ones", [P, P])
        tri = sb("tri", [P, P])
        zer = sb("zer", [P, 512], BF16)
        src1h = sb("src1h", [P, 2, N], BF16)
        dst1h = sb("dst1h", [P, 2, 3, 2, N], BF16)
        A0 = sb("A0", [P, NC, N])
        A1 = sb("A1", [P, NC, N])
        AnT = sb("AnT", [P, NC, N])
        ctxs = sb("ctxs", [P, FC, P])
        blockm = sb("blockm", [P, P])
        st = sb("st", [P, NC, 6])
        mv = sb("mv", [P, NC, 2])
        rstd = sb("rstd", [P, NC, 1])
        mhalf = sb("mhalf", [P, 2])
        deg = sb("deg", [P, 4, NC])
        hmx = sb("hmx", [P, NC * HEADS])
        hsum = sb("hsum", [P, NC * HEADS])
        kmx = sb("kmx", [P, FC])
        ksum = sb("ksum", [P, FC])
        ltri = sb("ltri", [P, E0, E0])
        rk = sb("rk", [P, 2, NC, E0, E0])
        gl = sb("gl", [P, 4, NC, E0])
        sel = sb("sel", [P, NC, E0])
        gmx = sb("gmx", [P, 2, NC])
        comb = sb("comb", [P, NC, E0 + 1])
        combT = sb("combT", [E0 + 1, N])
        spread = sb("spread", [E0 + 1, FC, P])
        hsT = sb("hsT", [DH, N])
        sm = sb("sm", [P, NC, 20])
        dl = sb("dl", [P, 8, NC, HEADS])
        vals = sb("vals", [P, NC, E1, 17])
        pre = sb("pre", [P, NC, E1])
        posm = sb("posm", [P, NC, E1])
        idx = sb("idx", [P, PC])
        ge = sb("ge", [P, PC, E1 + 1])
        oh = sb("oh", [P, PC, E1])
        first = sb("first", [P, PC, E1])
        forget = sb("forget", [P, PC])
        vmask = sb("vmask", [P, PC, E1, 17])
        pv = sb("pv", [P, PC, 17])
        perm = sb("perm", [P, NC, PAIRS])
        permT = sb("permT", [P, PC, N])
        kp = sb("kp", [P, FC, 2, PAIRS])
        vp = sb("vp", [P, PC, D])
        ba = sb("ba", [P, HEADS // 2, 2, PC, 2])
        ba_st = sb("ba_st", [P, 2, PC, 2])
        kq_st = sb("kq_st", [P, 2, PAIRS])
        v_st = sb("v_st", [P, PC, P])
        o_st = sb("o_st", [P, PC, P])
        T1s = sb("T1s", [P, 2, PC, P // 2])
        Rr = sb("Rr", [P, 2, DH])
        Y = sb("Y", [P, 2, PC, DH])
        m0 = sb("m0", [P, P])
        mlev = sb("mlev", [P, NL, P // 2])

        def wslot(u):
            s = u % SLOTS
            return ring[:, s * UNIT:(s + 1) * UNIT].rearrange("p (k o) -> p k o", k=FC)

        dec = ring[:, 0:UNIT]
        XXT = ring[:, UNIT:2 * UNIT].rearrange("p (x h a n) -> p x h a n", x=2, h=2, a=PC)
        X, XT = XXT[:, 0], XXT[:, 1]
        oall = ring[:, 2 * UNIT:3 * UNIT].rearrange("p (a f) -> p a f", a=PC)
        AT = [ring[:, (4 + h) * UNIT:(5 + h) * UNIT] for h in range(2)]
        ATd = [ring[:, (4 + h) * UNIT:(4 + h) * UNIT + PC * 640].rearrange("p (c m) -> p c m", m=640)[:, :, 0:P]
               for h in range(2)]
        MT = [ring[:, (6 + h) * UNIT:(7 + h) * UNIT] for h in range(2)]

        used = {U_Q0: ("q_ps", 2), U_K0: ("k_ps", 2), U_V0: ("v_ps", 2), U_O0: ("mix_ps", 2),
                U_GCN0: ("h2_ps", 2), U_MLP0: ("h3_ps", 2), U_GCN1: ("h2_ps", 4), U_MLP1: ("h3_ps", 4),
                U_W1: ("hid_ps", 2), U_W2: ("y_ps", 2), U_Q1: ("q_ps", 4), U_K1: ("k_ps", 4)}

        block = ctx.enter_context(nc.Block())

        @block.sync
        def _(sp):
            sp.dma_start(xs[:, :, :], d_x).then_inc(S["x_in"], 16)
            sp.dma_start(cols[:, :], d_cols).then_inc(S["cols_in"], 16)
            for u in range(3):
                sp.dma_start(ring[:, u * UNIT:(u + 1) * UNIT], d_w[u]).then_inc(S["w%d" % (u % SLOTS)], 16)
            sp.dma_start(rows[:, :], d_rows[0, :].partition_broadcast(P)).then_inc(S["rows_in"], 16)
            sp.dma_start(gw[:, :, :], d_gw).then_inc(S["gw_in"], 16)
            sp.dma_start(b29[:, :], d_b29).then_inc(S["b29_in"], 16)
            sp.dma_start(ws2[:, :], d_ws2).then_inc(S["ws2_in"], 16)
            for u in range(3, UNITS):
                if u >= SLOTS:
                    sp.wait_ge(S[used[u - SLOTS][0]], used[u - SLOTS][1])
                s = u % SLOTS
                sp.dma_start(ring[:, s * UNIT:(s + 1) * UNIT], d_w[u]).then_inc(S["w%d" % (u % SLOTS)], 16)
            sp.wait_ge(S["kp"], 8)
            sp.dma_start(kq_st[:, :, :], kp[:, 0, :, :]).then_inc(S["kq_in"], 16)
            sp.wait_ge(S["vp"], 4)
            sp.dma_start(v_st[:, :, :], vp[:, :, 0:P]).then_inc(S["v_in"], 16)
            with sp.Fori(1, HEADS // 2) as i:
                sp.wait_ge(S["kq_ps"], i * 16)
                sp.dma_start(kq_st[:, :, :], kp[:, bass.ds(i, 1), :, :]).then_inc(S["kq_in"], 16)
                sp.wait_ge(S["y_mm"], i * 8)
                sp.dma_start(v_st[:, :, :], vp[:, :, bass.ds(i * P, P)]).then_inc(S["v_in"], 16)
                sp.wait_ge(S["o_st"], i)
                sp.dma_start(oall[:, :, bass.ds(i * P - P, P)], o_st[:, :, :]).then_inc(S["o_out"], 16)
            sp.wait_ge(S["o_st"], HEADS // 2)
            sp.dma_start(oall[:, :, D - P:D], o_st[:, :, :]).then_inc(S["o_out"], 16)
            for c in range(NC):
                sp.wait_ge(S["fin"], c + 1)
                sp.dma_start(d_out[:, c, :], xs[:, c, :]).then_inc(S["out"], 16)
            sp.wait_ge(S["out"], 16 * NC)

        @block.gpsimd
        def _(g):
            count = [0]

            def link(ins):
                count[0] += 1
                ins.then_inc(S["pool_step"], 1)
                g.wait_ge(S["pool_step"], count[0])

            g.dma_start(edge_i[:, :, :], d_edge).then_inc(S["edge_in"], 16)
            g.dma_start(ew[:, :, :], d_ew).then_inc(S["ew_in"], 16)
            g.memset(mhalf[:, :], -0.5).then_inc(S["mhalf"], 1)
            g.memset(zer[:, :], 0.0).then_inc(S["zer"], 1)
            link(g.memset(identz[:, :], 0.0))
            link(g.affine_select(out=identz[:, 0:P], in_=identz[:, 0:P], compare_op=ALU.not_equal, fill=1.0,
                                 base=0, pattern=[[-1, P]], channel_multiplier=1))
            g.tensor_copy(ident[:, :], identz[:, 0:P]).then_inc(S["ident"], 1)
            g.iota(iota_f[:, :], [[1, PAIRS]], base=0, channel_multiplier=0,
                   allow_small_or_imprecise_dtypes=True).then_inc(S["iota"], 1)
            g.wait_ge(S["iota"], 1)
            g.tensor_copy(iota_b[:, :], iota_f[:, 0:N]).then_inc(S["iota"], 1)

            def power(n):
                g.wait_ge(S["mhalf"], 1)
                g.wait_ge(S["var"], n + 1)
                g.tensor_tensor(rstd[:, :, 0], mv[:, :, 1], mhalf[:, :], ALU.pow).then_inc(S["rstd"], 1)

            power(0)
            link(g.memset(ones[:, :], 1.0))
            link(g.memset(blockm[:, :], 0.0))
            link(g.memset(blockm[0:DH, 0:DH], 1.0))
            link(g.memset(blockm[DH:P, DH:P], 1.0))
            power(1)
            link(g.affine_select(out=tri[:, :], in_=ones[:, :], compare_op=ALU.is_ge, fill=0.0,
                                 base=-1, pattern=[[1, P]], channel_multiplier=-1))
            link(g.memset(ltri[:, :, :], 1.0))
            link(g.affine_select(out=ltri[:, :, :], in_=ltri[:, :, :], compare_op=ALU.is_ge, fill=0.0,
                                 base=-1, pattern=[[1, E0], [-1, E0]], channel_multiplier=0))
            link(g.memset(spread[:, :, :], 1.0))
            link(g.affine_select(out=spread[:, :, :], in_=spread[:, :, :], compare_op=ALU.is_ge, fill=0.0,
                                 base=0, pattern=[[P, FC], [1, P]], channel_multiplier=-DH))
            link(g.affine_select(out=spread[:, :, :], in_=spread[:, :, :], compare_op=ALU.is_ge, fill=0.0,
                                 base=DH - 1, pattern=[[-P, FC], [-1, P]], channel_multiplier=DH))
            link(g.memset(m0[:, :], -1.0))
            m0v = m0[:, :].rearrange("p (b j) -> p b j", j=2)
            link(g.memset(m0v[:, :, 0], 0.0))
            link(g.affine_select(out=m0v, in_=m0v, compare_op=ALU.is_equal, fill=0.0,
                                 base=0, pattern=[[2, P // 2], [0, 2]], channel_multiplier=-1))
            link(g.memset(mlev[:, :, :], -1.0))
            for l, b in enumerate(LEVELS):
                v = mlev[:, l, :].rearrange("p (n j) -> p n j", j=b)
                link(g.affine_select(out=v, in_=v, compare_op=ALU.is_ge, fill=0.0,
                                     base=-b, pattern=[[-2 * b, P // (2 * b)], [0, b]], channel_multiplier=1))
                link(g.affine_select(out=v, in_=v, compare_op=ALU.is_ge, fill=0.0,
                                     base=2 * b - 1, pattern=[[2 * b, P // (2 * b)], [0, b]], channel_multiplier=-1))
            link(g.iota(idx[:, :], [[P, PC]], base=0, channel_multiplier=1, allow_small_or_imprecise_dtypes=True))
            link(g.memset(ge[:, :, :], 0.0))
            g.memset(comb[:, :, E0:E0 + 1], 0.5).then_inc(S["consts"], 1)
            g.wait_ge(S["deg"], 1)
            g.tensor_tensor(deg[:, 1, :], deg[:, 1, :], mhalf[:, :], ALU.pow).then_inc(S["degp"], 1)
            for n in range(2, 6):
                power(n)

        @block.tensor
        def _(pe):
            mm, tp = nc.tensor.matmul, nc.tensor.transpose

            def weight(u):
                pe.wait_ge(S["w%d" % (u % SLOTS)], 16 * (u // SLOTS + 1))

            def to_fm(src, b0, b1, name):
                for k in range(FC):
                    for c in range(NC):
                        last = tp((b0, b1)[k // 2][:, (k % 2) * N + c * P:(k % 2) * N + (c + 1) * P],
                                  src[:, c, k * P:(k + 1) * P], ident[:, :])
                    if k % 2:
                        last.then_inc(S[name], 1)

            def to_tm(src, b0, b1, name):
                for c in range(NC):
                    for k in range(FC):
                        last = tp((b0, b1)[c][:, k * P:(k + 1) * P], src[:, k, c * P:(c + 1) * P], ident[:, :])
                    last.then_inc(S[name], 1)

            def proj_tm(act, u, b0, b1, name):
                weight(u)
                for c in range(NC):
                    for k in range(FC):
                        last = mm((b0, b1)[c][:, :], act[:, k, c * P:(c + 1) * P], wslot(u)[:, k, :],
                                  start=(k == 0), stop=(k == FC - 1))
                    last.then_inc(S[name], 1)

            def proj_fm(act, u, b0, b1, name):
                weight(u)
                for o in range(FC):
                    for k in range(FC):
                        last = mm((b0, b1)[o // 2][:, (o % 2) * N:(o % 2 + 1) * N], wslot(u)[:, k, o * P:(o + 1) * P],
                                  act[:, k, :], start=(k == 0), stop=(k == FC - 1))
                    if o % 2:
                        last.then_inc(S[name], 1)

            def attention_in(l, uq, uk, uv):
                proj_tm(fm(F_a), uq, bank[2], bank[3], "q_ps")
                proj_fm(fm(F_a), uk, bank[4], bank[5], "k_ps")
                proj_tm(fm(F_a), uv, bank[6], bank[7], "v_ps")

            def attention_core(l):
                pe.wait_ge(S["ek"], l * 4 + 4)
                to_tm(fm(F_c), bank[4], bank[5], "ekt_ps")
                pe.wait_ge(S["qs"], l * 2 + 2)
                to_fm(tm(T_b), bank[2], bank[3], "qT_ps")
                pe.wait_ge(S["v"], l * 2 + 2)
                pe.wait_ge(S["ekt"], l * 2 + 2)
                for j in range(FC):
                    for c in range(NC):
                        last = mm(bank[6][:, j * P:(j + 1) * P], tm(T_c)[:, c, j * P:(j + 1) * P],
                                  tm(T_d)[:, c, j * P:(j + 1) * P], start=(c == 0), stop=(c == NC - 1))
                last.then_inc(S["ctx_ps"], 1)
                pe.wait_ge(S["ctx"], l * 1 + 1)
                pe.wait_ge(S["qT"], l * 2 + 2)
                for j in range(FC):
                    last = mm(bank[4 + j // 2][:, (j % 2) * N:(j % 2 + 1) * N], ctxs[:, j, :], fm(F_b)[:, j, :],
                              start=True, stop=True)
                    if j % 2:
                        last.then_inc(S["oT_ps"], 1)

            pe.wait_ge(S["ident"], 1)
            pe.wait_ge(S["normed"], 4)
            to_fm(tm(T_a), bank[0], bank[1], "yT_ps")
            pe.wait_ge(S["yT"], 2)
            attention_in(0, U_Q0, U_K0, U_V0)

            pe.wait_ge(S["zer"], 1)
            for c in range(NC):
                mm(bank[c][:, :], zer[:, 0:P], zer[:, :], start=True, stop=False, skip_group_check=True)
            with pe.Fori(0, ET // 2) as i:
                for half in range(2):
                    pe.wait_ge(S["onehot"], i * 2 + half + 1)
                    for c in range(NC):
                        for part in range(3):
                            last = mm(bank[c][:, :], src1h[:, half, c * P:(c + 1) * P],
                                      dst1h[:, half, part, :, :], start=False, stop=False, skip_group_check=True)
                    last.then_inc(S["adj_tile"], 1)
            for c in range(NC):
                mm(bank[c][:, :], zer[:, 0:P], zer[:, :], start=False, stop=True,
                   skip_group_check=True).then_inc(S["adj_ps"], 1)

            attention_core(0)
            pe.wait_ge(S["oT"], 2)
            proj_tm(fm(F_a), U_O0, bank[2], bank[3], "mix_ps")

            pe.wait_ge(S["A0s"], 1)
            for dc in range(NC):
                for sc in range(NC):
                    last = tp(bank[7][:, dc * N + sc * P:dc * N + (sc + 1) * P], A0[:, sc, dc * P:(dc + 1) * P], ident[:, :])
            last.then_inc(S["AnT_ps"], 1)
            pe.wait_ge(S["AnT"], 1)
            for l in range(2):
                h = tm(T_n) if l == 0 else tm(T_b)
                if l == 1:
                    pe.wait_ge(S["h"], 2)
                for k in range(FC):
                    for dc in range(NC):
                        last = mm(bank[4 + k // 2][:, (k % 2) * N:(k % 2 + 1) * N], h[:, dc, k * P:(k + 1) * P],
                                  AnT[:, dc, :], start=(dc == 0), stop=(dc == NC - 1))
                    if k % 2:
                        last.then_inc(S["h1_ps"], 1)
                pe.wait_ge(S["h1T"], 2 * l + 2)
                proj_fm(fm(F_b), (U_GCN0, U_GCN1)[l], bank[6], bank[7], "h2_ps")
                pe.wait_ge(S["h2T"], 2 * l + 2)
                proj_tm(fm(F_c), (U_MLP0, U_MLP1)[l], bank[0], bank[1], "h3_ps")

            pe.wait_ge(S["normed"], 8)
            to_fm(tm(T_a), bank[2], bank[3], "zT_ps")
            pe.wait_ge(S["zT"], 2)
            pe.wait_ge(S["gw_in"], 16)
            for c in range(NC):
                for k in range(FC):
                    last = mm(bank[4][:, c * E0:(c + 1) * E0], fm(F_a)[:, k, c * P:(c + 1) * P],
                              gw[:, k, G_WG:G_WG + E0], start=(k == 0), stop=(k == FC - 1))
            last.then_inc(S["gate_ps"], 1)
            proj_fm(fm(F_a), U_W1, bank[6], bank[7], "hid_ps")
            for k in range(FC):
                last = mm(bank[5][0:DH, 0:N], gw[:, k, G_WS1:G_WS1 + DH], fm(F_a)[:, k, :],
                          start=(k == 0), stop=(k == FC - 1))
            last.then_inc(S["hs_ps"], 1)
            pe.wait_ge(S["comb"], 1)
            for c in range(NC):
                last = tp(bank[4][0:E0 + 1, c * P:(c + 1) * P], comb[:, c, :], ident[:, :])
            last.then_inc(S["combT_ps"], 1)
            pe.wait_ge(S["combT"], 1)
            for o in range(FC):
                last = mm(bank[o // 2][:, (o % 2) * N:(o % 2 + 1) * N], spread[:, o, :], combT[:, :],
                          start=True, stop=True)
                if o % 2:
                    last.then_inc(S["combB_ps"], 1)
            pe.wait_ge(S["hw"], 2)
            pe.wait_ge(S["hsT"], 1)
            pe.wait_ge(S["ws2_in"], 16)
            pe.wait_ge(S["b29_in"], 16)
            weight(U_W2)
            for c in range(NC):
                for k in range(FC):
                    mm(bank[2 + c][:, :], fm(F_c)[:, k, c * P:(c + 1) * P], wslot(U_W2)[:, k, :], start=(k == 0), stop=False)
                mm(bank[2 + c][:, :], hsT[:, c * P:(c + 1) * P], ws2[:, :], start=False, stop=False)
                mm(bank[2 + c][:, :], combT[:, c * P:(c + 1) * P], b29[:, :], start=False, stop=True).then_inc(S["y_ps"], 1)

            pe.wait_ge(S["normed"], 10)
            to_fm(tm(T_n), bank[0], bank[1], "xT_ps")
            pe.wait_ge(S["xT"], 2)
            attention_in(1, U_Q1, U_K1, U_V1)
            pe.wait_ge(S["A1"], 1)
            for k in range(FC):
                for c in range(NC):
                    last = mm(bank[k // 2][:, (k % 2) * N:(k % 2 + 1) * N], tm(T_n)[:, c, k * P:(k + 1) * P],
                              A1[:, c, :], start=(c == 0), stop=(c == NC - 1))
                if k % 2:
                    last.then_inc(S["agg_ps"], 1)
            attention_core(1)
            pe.wait_ge(S["oT"], 4)
            pe.wait_ge(S["aggT"], 2)
            weight(U_AGG)
            weight(U_O1)
            for c in range(NC):
                for k in range(FC):
                    mm(bank[2 + c][:, :], fm(T_a)[:, k, c * P:(c + 1) * P], wslot(U_AGG)[:, k, :], start=(k == 0), stop=False)
                for k in range(FC):
                    last = mm(bank[2 + c][:, :], fm(F_a)[:, k, c * P:(c + 1) * P], wslot(U_O1)[:, k, :],
                              start=False, stop=(k == FC - 1))
                last.then_inc(S["mix_ps"], 1)

            pe.wait_ge(S["normed"], 12)
            to_fm(tm(T_n), bank[0], bank[1], "dT_ps")
            pe.wait_ge(S["dT"], 2)
            for c in range(NC):
                for k in range(FC):
                    last = mm(bank[2][:, c * 20:(c + 1) * 20], fm(F_a)[:, k, c * P:(c + 1) * P],
                              gw[:, k, G_SM:G_SM + 20], start=(k == 0), stop=(k == FC - 1))
            last.then_inc(S["sm_ps"], 1)
            proj_tm(fm(F_a), U_DQ, bank[3], bank[4], "dq_ps")
            proj_tm(fm(F_a), U_DK, bank[5], bank[6], "dk_ps")
            proj_tm(fm(F_a), U_DV, bank[7], bank[0], "dv_ps")
            pe.wait_ge(S["sm"], 1)
            proj_tm(fm(F_a), U_DG, bank[1], bank[2], "dg_ps")
            pe.wait_ge(S["dq"], 2)
            pe.wait_ge(S["sel"], 1)
            for c in range(NC):
                for kc in range(NC):
                    mm(bank[3][:, c * E1:(c + 1) * E1], ones[:, :], pre[:, kc, :], start=(kc == 0), stop=False)
                for kc in range(c + 1):
                    mm(bank[3][:, c * E1:(c + 1) * E1], (tri if kc == c else ones)[:, :], sel[:, kc, 0:E1],
                       start=False, stop=(kc == c))
            for kc in range(NC):
                last = mm(bank[3][:, 2 * E1:3 * E1], ones[:, :], pre[:, kc, :], start=(kc == 0), stop=(kc == NC - 1))
            last.then_inc(S["pos_ps"], 1)
            pe.wait_ge(S["perm"], 1)
            pe.wait_ge(S["dv"], 2)
            for p in range(PC):
                for c in range(NC):
                    last = mm(bank[3][:, p * 68:(p + 1) * 68], perm[:, c, p * P:(p + 1) * P],
                              vals[:, c, :, :], start=(c == 0), stop=(c == NC - 1))
            last.then_inc(S["vals_ps"], 1)
            for p in range(PC):
                b = (4, 5, 6, 7)[p]
                if p == 1:
                    pe.wait_ge(S["dk"], 2)
                for c in range(NC):
                    last = mm(bank[b][:, :], perm[:, c, p * P:(p + 1) * P], tm(T_c)[:, c, :],
                              start=(c == 0), stop=(c == NC - 1))
                last.then_inc(S["vp_ps"], 1)
            pe.wait_ge(S["kn"], 2)
            pe.wait_ge(S["dg"], 2)
            for k in range(FC):
                b = (0, 1, 2, 4)[k]
                if k == 3:
                    pe.wait_ge(S["vp"], 1)
                for c in range(NC):
                    last = mm(bank[b][:, :], tm(T_b)[:, c, k * P:(k + 1) * P], perm[:, c, :],
                              start=(c == 0), stop=(c == NC - 1))
                last.then_inc(S["kp_ps"], 1)
            pe.wait_ge(S["qn"], 2)
            for k in range(FC):
                b = (5, 6, 7, 0)[k]
                if k < 3:
                    pe.wait_ge(S["vp"], k + 2)
                else:
                    pe.wait_ge(S["kp"], 1)
                for c in range(NC):
                    last = mm(bank[b][:, :], tm(T_a)[:, c, k * P:(k + 1) * P], perm[:, c, :],
                              start=(c == 0), stop=(c == NC - 1))
                last.then_inc(S["kp_ps"], 1)
            for p in range(PC):
                if p % 2 == 0:
                    pe.wait_ge(S["kp"], 2 + p // 2)
                for c in range(NC):
                    last = tp(bank[1 + p // 2][:, (p % 2) * N + c * P:(p % 2) * N + (c + 1) * P],
                              perm[:, c, p * P:(p + 1) * P], ident[:, :])
                if p % 2:
                    last.then_inc(S["permT_ps"], 1)
            pe.wait_ge(S["kp"], 8)
            pe.wait_ge(S["permT"], 2)
            pe.wait_ge(S["pv"], 1)

            with pe.Fori(0, HEADS // 2) as i:
                pe.wait_ge(S["ba_st"], i + 1)
                pe.wait_ge(S["kq_in"], i * 16 + 16)
                for hh in range(2):
                    r = slice(hh * DH, (hh + 1) * DH)
                    if hh:
                        pe.wait_ge(S["scan"], i * 2 + hh)
                    for p in range(PC):
                        last = tp(bank[0][:, p * P:(p + 1) * P], ba_st[:, 1, p, hh:hh + 1].to_broadcast([P, P]), ident[:, :])
                    last.then_inc(S["arow"], 1)
                    for p in range(PC):
                        for z in range(2):
                            n = hh * 8 + p * 2 + z
                            if n >= 6:
                                pe.wait_ge(S["prod"], i * 16 + n - 5)
                            mm(bank[1 + n % 6][:, 0:PAIRS - p * P], kq_st[r, 0, p * P:(p + 1) * P],
                               kq_st[r, z, p * P:PAIRS], start=True, stop=True).then_inc(S["kq_ps"], 1)
                pe.wait_ge(S["prod"], i * 16 + 16)
                for hh in range(2):
                    pe.wait_ge(S["xt0"], i * 2 + hh + 1)
                    for p in range(PC):
                        last = tp(bank[5 + hh][:, p * P:(p + 1) * P], XT[:, hh, p, :], ident[:, :])
                    last.then_inc(S["x0_ps"], 1)
                for l, b in enumerate(LEVELS):
                    for hh in range(2):
                        if l == 0:
                            pe.wait_ge(S["x0"], i * 2 + hh + 1)
                        else:
                            pe.wait_ge(S["x"], i * 2 * NL + 2 * (l - 1) + hh + 1)
                        for p in range(PC):
                            even = X[:, hh, p, :].rearrange("q (n two j) -> q n two j", two=2, j=b)[:, :, 0, :]
                            last = mm(bank[3 + hh][:, p * 64:(p + 1) * 64], ATd[hh][:, p, :], even, start=True, stop=True)
                        last.then_inc(S["t1_ps"], 1)
                    for hh in range(2):
                        if l:
                            pe.wait_ge(S["xt"], i * 2 * NL + 2 * (l - 1) + hh + 1)
                        pe.wait_ge(S["t1"], i * 2 * NL + 2 * l + hh + 1)
                        for p in range(PC):
                            last = mm(bank[3 + hh][:, p * 64:(p + 1) * 64], XT[:, hh, p, :], T1s[:, hh, p, :], start=True, stop=True)
                        last.then_inc(S["dx_ps"], 1)
                    for hh in range(2):
                        pe.wait_ge(S["x"], i * 2 * NL + 2 * l + hh + 1)
                        for p in range(PC):
                            last = tp(bank[5 + hh][:, p * P:(p + 1) * P], X[:, hh, p, :], ident[:, :])
                        last.then_inc(S["xt_ps"], 1)
                pe.wait_ge(S["v_in"], i * 16 + 16)
                for p in range(PC):
                    if p:
                        for hh in range(2):
                            pe.wait_ge(S["yv"], i * 8 + 2 * (p - 1) + hh + 1)
                            for q in range(p):
                                last = mm(bank[3 + hh][:, 0:DH], AT[hh][:, q * PAIRS + p * P:q * PAIRS + (p + 1) * P],
                                          Y[:, hh, q, :], start=(q == 0), stop=(q == p - 1))
                            last.then_inc(S["r_ps"], 1)
                    for hh in range(2):
                        if p == 0:
                            pe.wait_ge(S["xt"], i * 2 * NL + 2 * (NL - 1) + hh + 1)
                            rhs = v_st[:, 0, hh * DH:(hh + 1) * DH]
                        else:
                            pe.wait_ge(S["r"], i * 6 + 2 * (p - 1) + hh + 1)
                            rhs = Rr[:, hh, :]
                        mm(bank[5 + hh][:, 0:DH], XT[:, hh, p, :], rhs, start=True, stop=True).then_inc(S["y_mm"], 1)
                pe.wait_ge(S["yv"], i * 8 + 8)
                for hh in range(2):
                    for p in range(PC):
                        for q in range(p + 1):
                            last = mm(bank[7][:, p * P + hh * DH:p * P + (hh + 1) * DH],
                                      MT[hh][:, q * PAIRS + p * P:q * PAIRS + (p + 1) * P], Y[:, hh, q, :],
                                      start=(q == 0), stop=(q == p))
                last.then_inc(S["o_ps"], 1)
                pe.wait_ge(S["o_st"], i + 1)

            pe.wait_ge(S["o_out"], 16 * (HEADS // 2))
            for c in range(NC):
                for p in range(PC):
                    last = mm(bank[c][:, :], permT[:, p, c * P:(c + 1) * P], oall[:, p, :], start=(p == 0), stop=(p == PC - 1))
                last.then_inc(S["core_ps"], 1)
            pe.wait_ge(S["core"], 2)
            to_fm(tm(T_a), bank[2], bank[3], "coreT_ps")
            pe.wait_ge(S["coreT"], 2)
            proj_tm(fm(F_a), U_DO, bank[4], bank[5], "fin_ps")

        @block.scalar
        def _(act):
            A = nc.scalar.activation

            def copy2(dst, b0, b1, ps, done, at=0):
                for c in range(2):
                    act.wait_ge(S[ps], at + c + 1)
                    A(dst[:, c * 512:(c + 1) * 512], (b0, b1)[c][:, :], ACT.Copy).then_inc(S[done], 1)

            def attention(l):
                for c in range(NC):
                    act.wait_ge(S["qsub"], l * 2 + c + 1)
                    A(tm(T_b)[:, c, :], tm(T_b)[:, c, :], ACT.Exp).then_inc(S["qexp"], 1)
                for k in range(FC):
                    act.wait_ge(S["kmx"], l * 2 + k // 2 + 1)
                    A(fm(F_c)[:, k, :], bank[4 + k // 2][:, (k % 2) * N:(k % 2 + 1) * N], ACT.Exp,
                      bias=kmx[:, k:k + 1], accum_out=ksum[:, k:k + 1]).then_inc(S["ek"], 1)
                copy2(T_d, bank[6], bank[7], "v_ps", "v", 2 * l)
                copy2(T_c, bank[4], bank[5], "ekt_ps", "ekt", 2 * l)
                copy2(F_b, bank[2], bank[3], "qT_ps", "qT", 2 * l)
                copy2(F_a, bank[4], bank[5], "oT_ps", "oT", 2 * l)

            act.wait_ge(S["cols_in"], 16)
            for k in range(FC):
                act.wait_ge(S["yT_ps"], k // 2 + 1)
                ins = A(fm(F_a)[:, k, :], bank[k // 2][:, (k % 2) * N:(k % 2 + 1) * N], ACT.Copy,
                        scale=cols[:, C_GAMMA + k:C_GAMMA + k + 1])
                if k % 2:
                    ins.then_inc(S["yT"], 1)
            attention(0)
            for l in range(2):
                copy2(F_b, bank[4], bank[5], "h1_ps", "h1T", 2 * l)
                for k in range(FC):
                    act.wait_ge(S["h2_ps"], 2 * l + k // 2 + 1)
                    ins = A(fm(F_c)[:, k, :], bank[6 + k // 2][:, (k % 2) * N:(k % 2 + 1) * N], ACT.Identity,
                            bias=cols[:, C_GCN + 4 * l + k:C_GCN + 4 * l + k + 1])
                    if k % 2:
                        ins.then_inc(S["h2T"], 1)
            copy2(F_a, bank[2], bank[3], "zT_ps", "zT")
            act.wait_ge(S["gsub"], 1)
            A(gl[:, 1, :, :], gl[:, 1, :, :], ACT.Exp).then_inc(S["gexp"], 1)
            for k in range(FC):
                act.wait_ge(S["hid_ps"], k // 2 + 1)
                A(fm(F_b)[:, k, :], bank[6 + k // 2][:, (k % 2) * N:(k % 2 + 1) * N], ACT.Relu,
                  bias=cols[:, C_B1 + k:C_B1 + k + 1]).then_inc(S["hid"], 1)
            act.wait_ge(S["hs_ps"], 1)
            A(hsT[:, :], bank[5][0:DH, 0:N], ACT.Relu, bias=cols[0:DH, C_BS1:C_BS1 + 1]).then_inc(S["hsT1"], 1)
            act.wait_ge(S["hsT1"], 1)
            A(hsT[:, :], hsT[:, :], ACT.Copy, scale=0.5).then_inc(S["hsT"], 1)
            act.wait_ge(S["combT_ps"], 1)
            A(combT[:, :], bank[4][0:E0 + 1, 0:N], ACT.Copy).then_inc(S["combT"], 1)
            copy2(F_a, bank[0], bank[1], "xT_ps", "xT")
            attention_first = True
            copy2(T_a, bank[0], bank[1], "agg_ps", "aggT")
            attention(1)
            copy2(F_a, bank[0], bank[1], "dT_ps", "dT")
            act.wait_ge(S["sm_ps"], 1)
            A(sm[:, :, :], bank[2][:, 0:40].rearrange("p (c e) -> p c e", c=NC), ACT.Copy).then_inc(S["sm"], 1)
            act.wait_ge(S["ssub"], 1)
            A(gl[:, 1, :, 0:E1], gl[:, 1, :, 0:E1], ACT.Exp).then_inc(S["sexp"], 1)
            act.wait_ge(S["aabs"], 1)
            A(dl[:, 1, :, :], dl[:, 1, :, :], ACT.Exp, scale=-1.0).then_inc(S["aexp"], 1)
            act.wait_ge(S["rows_in"], 16)
            A(dl[:, 2, 0, :], rows[:, R_ALOG:R_ALOG + HEADS], ACT.Exp).then_inc(S["alog"], 1)
            A(dl[:, 3, :, :], sm[:, :, 4:12], ACT.Sigmoid).then_inc(S["beta"], 1)
            for b0, b1, dst, ps, done in ((3, 4, T_a, "dq_ps", "dq"), (5, 6, T_b, "dk_ps", "dk"),
                                          (7, 0, T_c, "dv_ps", "dv"), (1, 2, T_d, "dg_ps", "dg")):
                for c in range(NC):
                    act.wait_ge(S[ps], c + 1)
                    A(tm(dst)[:, c, :], bank[(b0, b1)[c]][:, :], ACT.Silu).then_inc(S[done], 1)
            act.wait_ge(S["qss"], 1)
            A(hsum[:, :], hsum[:, :], ACT.Sqrt).then_inc(S["qrt"], 1)
            act.wait_ge(S["kss"], 1)
            A(hmx[:, :], hmx[:, :], ACT.Sqrt).then_inc(S["krt"], 1)
            for p in range(PC):
                act.wait_ge(S["vp_ps"], p + 1)
                A(vp[:, p, :], bank[4 + p][:, :], ACT.Copy).then_inc(S["vp"], 1)
            for n in range(8):
                act.wait_ge(S["kp_ps"], n + 1)
                A(kp[:, n % 4, n // 4, :], bank[(0, 1, 2, 4, 5, 6, 7, 0)[n]][:, :], ACT.Copy).then_inc(S["kp"], 1)
            for c in range(2):
                act.wait_ge(S["permT_ps"], c + 1)
                A(permT[:, 2 * c:2 * c + 2, :], bank[1 + c][:, :].rearrange("p (a n) -> p a n", a=2), ACT.Copy)\
                    .then_inc(S["permT"], 1)
            act.wait_ge(S["pv"], 1)
            for p in range(PC):
                ins = A(ba[:, :, 1, p, :], pv[:, p, 8:16].rearrange("p (a b) -> p a b", b=2), ACT.Exp)
            ins.then_inc(S["ba"], 1)

            with act.Fori(0, HEADS // 2) as i:
                for hh in range(2):
                    act.wait_ge(S["x0_ps"], i * 2 + hh + 1)
                    A(X[:, hh, :, :], bank[5 + hh][:, :].rearrange("p (a n) -> p a n", a=PC), ACT.Copy)\
                        .then_inc(S["x0"], 1)
                for l in range(NL):
                    for hh in range(2):
                        act.wait_ge(S["xt_ps"], i * 2 * NL + 2 * l + hh + 1)
                        A(XT[:, hh, :, :], bank[5 + hh][:, :].rearrange("p (a n) -> p a n", a=PC), ACT.Copy)\
                            .then_inc(S["xt"], 1)
                for p in range(PC):
                    for hh in range(2):
                        act.wait_ge(S["y_mm"], i * 8 + 2 * p + hh + 1)
                        A(Y[:, hh, p, :], bank[5 + hh][:, 0:DH], ACT.Copy).then_inc(S["yv"], 1)
                act.wait_ge(S["o_ps"], i + 1)
                for p in range(PC):
                    ins = A(o_st[:, p, :], bank[7][:, p * P:(p + 1) * P], ACT.Copy, scale=pv[:, p, 16:17])
                ins.then_inc(S["o_st"], 1)
                act.wait_ge(S["o_out"], i * 16 + 16)

            act.wait_ge(S["css"], 1)
            A(hsum[:, :], hsum[:, :], ACT.Sqrt).then_inc(S["crt"], 1)
            copy2(F_a, bank[2], bank[3], "coreT_ps", "coreT")

        @block.vector
        def _(dve):
            V = nc.vector
            count = [0]

            def link(ins):
                count[0] += 1
                ins.then_inc(S["dve_step"], 1)
                dve.wait_ge(S["dve_step"], count[0])

            def signal(ins, name, value):
                ins.then_inc(S[name], 1)
                dve.wait_ge(S[name], value)

            def norm(src, dst, n):
                for c in range(NC):
                    link(V.bn_stats(st[:, c, :], src(c)))
                for c in range(NC):
                    link(V.bn_aggr(mv[:, c, :], st[:, c, :]))
                signal(V.tensor_scalar(mv[:, :, 1], mv[:, :, 1], EPS, None, ALU.add), "var", n + 1)
                dve.wait_ge(S["rstd"], n + 1)
                for c in range(NC):
                    signal(V.tensor_scalar(dst[:, c, :], src(c), mv[:, c, 0:1], rstd[:, c, 0:1],
                                           ALU.subtract, ALU.mult), "normed", 2 * n + c + 1)

            def heads(ap):
                return ap.rearrange("p (h d) -> p h d", h=HEADS)

            def per_head(t, c):
                return t[:, c * HEADS:(c + 1) * HEADS].rearrange("p (h o) -> p h o", o=1).to_broadcast([P, HEADS, DH])

            def attention_soft(l, scale):
                for c in range(NC):
                    dve.wait_ge(S["q_ps"], l * 2 + c + 1)
                    link(V.tensor_reduce(hmx[:, c * HEADS:(c + 1) * HEADS], heads(bank[2 + c][:, :]), AX, ALU.max))
                    signal(V.tensor_tensor(heads(tm(T_b)[:, c, :]), heads(bank[2 + c][:, :]), per_head(hmx, c),
                                           ALU.subtract), "qsub", l * 2 + c + 1)
                for b in range(2):
                    dve.wait_ge(S["k_ps"], l * 2 + b + 1)
                    link(V.tensor_reduce(kmx[:, 2 * b:2 * b + 2], bank[4 + b][:, :].rearrange("p (a n) -> p a n", a=2),
                                         AX, ALU.max))
                    signal(V.tensor_scalar(kmx[:, 2 * b:2 * b + 2], kmx[:, 2 * b:2 * b + 2], -1.0, None, ALU.mult),
                           "kmx", l * 2 + b + 1)
                for c in range(NC):
                    s = hsum[:, c * HEADS:(c + 1) * HEADS]
                    dve.wait_ge(S["qexp"], l * 2 + c + 1)
                    link(V.tensor_reduce(s, heads(tm(T_b)[:, c, :]), AX, ALU.add))
                    link(V.reciprocal(s, s))
                    if scale != 1.0:
                        link(V.tensor_scalar(s, s, scale, None, ALU.mult))
                    signal(V.tensor_tensor(heads(tm(T_b)[:, c, :]), heads(tm(T_b)[:, c, :]), per_head(hsum, c),
                                           ALU.mult), "qs", l * 2 + c + 1)

            def attention_ctx(l):
                dve.wait_ge(S["ek"], l * 4 + 4)
                link(V.reciprocal(ksum[:, :], ksum[:, :]))
                dve.wait_ge(S["ctx_ps"], l * 1 + 1)
                for j in range(FC):
                    ins = V.scalar_tensor_tensor(out=ctxs[:, j, :], in0=bank[6][:, j * P:(j + 1) * P],
                                                 scalar=ksum[:, j:j + 1], in1=blockm[:, :], op0=ALU.mult, op1=ALU.mult)
                ins.then_inc(S["ctx"], 1)

            def ranks(lg, e):
                lj = lg.rearrange("p c (o j) -> p c o j", o=1).to_broadcast([P, NC, e, e])
                li = lg.rearrange("p c (i o) -> p c i o", o=1).to_broadcast([P, NC, e, e])
                gt, eq = rk[:, 0, :, 0:e, 0:e], rk[:, 1, :, 0:e, 0:e]
                link(V.tensor_tensor(gt, lj, li, ALU.is_gt))
                link(V.tensor_tensor(eq, lj, li, ALU.is_equal))
                for c in range(NC):
                    link(V.tensor_tensor(rk[:, 1, c, 0:e, 0:e], rk[:, 1, c, 0:e, 0:e], ltri[:, 0:e, 0:e], ALU.mult))
                link(V.tensor_tensor(gt, gt, eq, ALU.add))
                for c in range(NC):
                    link(V.tensor_reduce(sel[:, c, 0:e], rk[:, 0, c, 0:e, 0:e], AX, ALU.add))
                link(V.tensor_scalar(sel[:, :, 0:e], sel[:, :, 0:e], 1.5, None, ALU.is_lt))

            def over(t, e):
                return t.rearrange("p (c o) -> p c o", o=1).to_broadcast([P, NC, e])

            dve.wait_ge(S["x_in"], 16)
            norm(lambda c: xs[:, c, :], tm(T_n), 0)
            norm(lambda c: tm(T_n)[:, c, :], tm(T_a), 1)

            dve.wait_ge(S["ew_in"], 16)
            dve.wait_ge(S["edge_in"], 16)
            link(V.tensor_copy(edge_f[:, :, :], edge_i[:, :, :]))
            for part in range(3):
                link(V.tensor_copy(ewb[:, :, :], ew[:, :, :]))
                link(V.tensor_copy(ewp[:, part, :, :], ewb[:, :, :]))
                if part < 2:
                    link(V.tensor_tensor(ew[:, :, :], ew[:, :, :], ewp[:, part, :, :], ALU.subtract))

            attention_soft(0, DH ** -0.5)

            dve.wait_ge(S["iota"], 2)

            def onehots(t, half, own):
                V.tensor_scalar(src1h[:, half, :], iota_b[:, :], edge_f[:, 0, t], None, ALU.is_equal)
                for part in range(3):
                    for w in range(2):
                        ins = V.tensor_scalar(dst1h[:, half, part, w, :], iota_b[:, :], edge_f[:, 1, t],
                                              ewp[:, part, w, t], ALU.is_equal, ALU.mult)
                ins.then_inc(S["onehot"], 1)

            for half in range(2):
                onehots(slice(half, half + 1), half, None)
            with dve.Fori(1, ET // 2) as i:
                for half in range(2):
                    dve.wait_ge(S["adj_tile"], i * 2 - 1 + half)
                    onehots(bass.ds(i * 2 + half, 1), half, None)

            dve.wait_ge(S["consts"], 1)
            attention_ctx(0)
            for c in range(NC):
                dve.wait_ge(S["adj_ps"], c + 1)
                link(V.tensor_copy(A0[:, c, :], bank[c][:, 0:N]))
                signal(V.tensor_copy(A1[:, c, :], bank[c][:, N:2 * N]), "A1c", c + 1)
                link(V.tensor_reduce(deg[:, 0, c:c + 1], A0[:, c, :], AX, ALU.add))
            V.tensor_scalar(deg[:, 2, :], deg[:, 0, :], 0.0, None, ALU.is_gt).then_inc(S["A1"], 1)
            signal(V.tensor_scalar(deg[:, 1, :], deg[:, 0, :], 1e-38, None, ALU.max), "deg", 1)
            dve.wait_ge(S["A1"], 1)
            dve.wait_ge(S["degp"], 1)
            link(V.tensor_tensor(deg[:, 3, :], deg[:, 1, :], deg[:, 2, :], ALU.mult))
            for c in range(NC):
                ins = V.tensor_scalar(A0[:, c, :], A0[:, c, :], deg[:, 3, c:c + 1], None, ALU.mult)
            ins.then_inc(S["A0s"], 1)
            dve.wait_ge(S["AnT_ps"], 1)
            for c in range(NC):
                ins = V.tensor_scalar(AnT[:, c, :], bank[7][:, c * N:(c + 1) * N], deg[:, 3, c:c + 1], None, ALU.mult)
            ins.then_inc(S["AnT"], 1)

            dve.wait_ge(S["rows_in"], 16)
            dve.wait_ge(S["mix_ps"], 2)
            norm(lambda c: bank[2 + c][:, :], tm(T_a), 2)
            for c in range(NC):
                link(V.tensor_tensor(tm(T_a)[:, c, :], tm(T_a)[:, c, :], row(R_OG), ALU.mult))
                link(V.tensor_tensor(xs[:, c, :], xs[:, c, :], tm(T_a)[:, c, :], ALU.add))
            for l in range(2):
                for c in range(NC):
                    dve.wait_ge(S["h3_ps"], 2 * l + c + 1)
                    link(V.tensor_tensor(tm(T_c)[:, c, :], bank[c][:, :], row((R_MLP0, R_MLP1)[l]), ALU.add))
                    ins = V.scalar_tensor_tensor(out=tm(T_b)[:, c, :], in0=tm(T_c)[:, c, :], scalar=0.01,
                                                 in1=tm(T_c)[:, c, :], op0=ALU.mult, op1=ALU.max)
                    if l == 0:
                        ins.then_inc(S["h"], 1)
                    else:
                        link(ins)
                        link(V.tensor_tensor(xs[:, c, :], xs[:, c, :], tm(T_b)[:, c, :], ALU.add))

            norm(lambda c: xs[:, c, :], tm(T_a), 3)
            dve.wait_ge(S["gate_ps"], 1)
            g0, g1, g2 = gl[:, 0, :, :], gl[:, 1, :, :], gl[:, 2, :, :]
            bg = rows[:, R_BG:R_BG + E0].rearrange("p (o e) -> p o e", o=1).to_broadcast([P, NC, E0])
            link(V.tensor_tensor(g0, bank[4][:, 0:2 * E0].rearrange("p (c e) -> p c e", c=NC), bg, ALU.add))
            link(V.tensor_reduce(gmx[:, 0, :], g0, AX, ALU.max))
            signal(V.tensor_tensor(g1, g0, over(gmx[:, 0, :], E0), ALU.subtract), "gsub", 1)
            ranks(g0, E0)
            dve.wait_ge(S["gexp"], 1)
            link(V.tensor_tensor(g1, g1, sel[:, :, 0:E0], ALU.mult))
            link(V.tensor_reduce(gmx[:, 1, :], g1, AX, ALU.add))
            link(V.reciprocal(gmx[:, 1, :], gmx[:, 1, :]))
            signal(V.tensor_tensor(comb[:, :, 0:E0], g1, over(gmx[:, 1, :], E0), ALU.mult), "comb", 1)
            dve.wait_ge(S["hid"], 4)
            for b in range(2):
                dve.wait_ge(S["combB_ps"], b + 1)
                V.tensor_tensor(F_c[:, b * 512:(b + 1) * 512], F_b[:, b * 512:(b + 1) * 512], bank[b][:, :],
                                ALU.mult).then_inc(S["hw"], 1)
            for c in range(NC):
                dve.wait_ge(S["y_ps"], c + 1)
                link(V.tensor_tensor(xs[:, c, :], xs[:, c, :], bank[2 + c][:, :], ALU.add))

            norm(lambda c: xs[:, c, :], tm(T_n), 4)
            attention_soft(1, 1.0)
            attention_ctx(1)
            link(V.tensor_tensor(row(R_B1), row(R_B1), row(R_BOUT), ALU.add))
            for c in range(NC):
                link(V.tensor_tensor(xs[:, c, :], xs[:, c, :], row(R_B1), ALU.add))
                dve.wait_ge(S["mix_ps"], 2 + c + 1)
                link(V.tensor_tensor(xs[:, c, :], xs[:, c, :], bank[2 + c][:, :], ALU.add))
            norm(lambda c: xs[:, c, :], tm(T_n), 5)

            dve.wait_ge(S["sm"], 1)
            s0, s1, w = gl[:, 0, :, 0:E1], gl[:, 1, :, 0:E1], gl[:, 2, :, 0:E1]
            link(V.tensor_reduce(gmx[:, 0, :], sm[:, :, 0:E1], AX, ALU.max))
            signal(V.tensor_tensor(s1, sm[:, :, 0:E1], over(gmx[:, 0, :], E1), ALU.subtract), "ssub", 1)
            x_a, u_a, ea, beta = dl[:, 0, :, :], dl[:, 1, :, :], dl[:, 2, 0, :], dl[:, 3, :, :]
            s_a, s2, pl, sp_ = dl[:, 4, :, :], dl[:, 5, :, :], dl[:, 6, :, :], dl[:, 7, :, :]
            dtb = rows[:, R_DT:R_DT + HEADS].rearrange("p (o e) -> p o e", o=1).to_broadcast([P, NC, HEADS])
            link(V.tensor_tensor(x_a, sm[:, :, 12:20], dtb, ALU.add))
            signal(V.scalar_tensor_tensor(out=u_a, in0=x_a, scalar=-1.0, in1=x_a, op0=ALU.mult, op1=ALU.max), "aabs", 1)
            dve.wait_ge(S["sexp"], 1)
            link(V.tensor_reduce(gmx[:, 1, :], s1, AX, ALU.add))
            link(V.reciprocal(gmx[:, 1, :], gmx[:, 1, :]))
            link(V.tensor_tensor(s0, s1, over(gmx[:, 1, :], E1), ALU.mult))
            ranks(s0, E1)
            link(V.memset(pre[:, :, 0:1], 0.0))
            for e in range(1, E1):
                ins = V.tensor_tensor(pre[:, :, e], pre[:, :, e - 1], sel[:, :, e - 1], ALU.add)
                if e < E1 - 1:
                    link(ins)
            signal(ins, "sel", 1)
            link(V.tensor_tensor(w, s0, sel[:, :, 0:E1], ALU.mult))
            link(V.tensor_reduce(gmx[:, 1, :], w, AX, ALU.add))
            link(V.reciprocal(gmx[:, 1, :], gmx[:, 1, :]))
            link(V.tensor_tensor(w, w, over(gmx[:, 1, :], E1), ALU.mult))
            link(V.tensor_scalar(s1, w, 0.0, None, ALU.is_gt))
            dve.wait_ge(S["aexp"], 1)
            link(V.tensor_scalar(s_a, u_a, 2.0, None, ALU.add))
            link(V.reciprocal(s_a, s_a))
            link(V.tensor_tensor(s_a, s_a, u_a, ALU.mult))
            link(V.tensor_tensor(s2, s_a, s_a, ALU.mult))
            link(V.tensor_scalar(pl, s2, 1.0 / 17, None, ALU.mult))
            for k in range(15, 1, -2):
                link(V.scalar_tensor_tensor(out=pl, in0=pl, scalar=1.0 / k, in1=s2, op0=ALU.add, op1=ALU.mult))
            link(V.scalar_tensor_tensor(out=pl, in0=pl, scalar=1.0, in1=s_a, op0=ALU.add, op1=ALU.mult))
            link(V.tensor_scalar(sp_, x_a, 0.0, None, ALU.max))
            link(V.scalar_tensor_tensor(out=sp_, in0=pl, scalar=2.0, in1=sp_, op0=ALU.mult, op1=ALU.add))
            dve.wait_ge(S["alog"], 1)
            eab = ea.rearrange("p (o e) -> p o e", o=1).to_broadcast([P, NC, HEADS])
            link(V.scalar_tensor_tensor(out=sp_, in0=sp_, scalar=-1.0, in1=eab, op0=ALU.mult, op1=ALU.mult))
            link(V.tensor_scalar(sp_, sp_, -200.0, None, ALU.max))
            dve.wait_ge(S["beta"], 1)
            for c in range(NC):
                on = s1[:, c, :].rearrange("p (e o) -> p e o", o=1).to_broadcast([P, E1, HEADS])
                bb = beta[:, c, :].rearrange("p (o h) -> p o h", o=1).to_broadcast([P, E1, HEADS])
                gg = sp_[:, c, :].rearrange("p (o h) -> p o h", o=1).to_broadcast([P, E1, HEADS])
                link(V.tensor_tensor(vals[:, c, :, 0:8], bb, on, ALU.mult))
                link(V.tensor_tensor(vals[:, c, :, 8:16], gg, on, ALU.mult))
            link(V.tensor_copy(vals[:, :, :, 16], w))
            dve.wait_ge(S["pos_ps"], 1)
            p3 = bank[3][:, 0:2 * E1].rearrange("p (c e) -> p c e", c=NC)
            link(V.scalar_tensor_tensor(out=posm[:, :, :], in0=p3, scalar=1.0, in1=sel[:, :, 0:E1], op0=ALU.add, op1=ALU.mult))
            link(V.tensor_scalar(posm[:, :, :], posm[:, :, :], -1.0, None, ALU.add))
            for p in range(PC):
                link(V.tensor_scalar(ge[:, p, 0:E1], bank[3][:, 2 * E1:3 * E1], idx[:, p:p + 1], None, ALU.is_le))
            for p in range(PC):
                link(V.tensor_scalar(first[:, p, :], bank[3][:, 2 * E1:3 * E1], idx[:, p:p + 1], -200.0,
                                     ALU.is_equal, ALU.mult))
            link(V.tensor_reduce(forget[:, :], first[:, :, :], AX, ALU.min))
            link(V.tensor_tensor(oh[:, :, :], ge[:, :, 0:E1], ge[:, :, 1:E1 + 1], ALU.subtract))
            for e in range(E1):
                for c in range(NC):
                    if e == 0:
                        ins = V.tensor_scalar(perm[:, c, :], iota_f[:, :], posm[:, c, 0:1], None, ALU.is_equal)
                    else:
                        ins = V.scalar_tensor_tensor(out=perm[:, c, :], in0=iota_f[:, :], scalar=posm[:, c, e:e + 1],
                                                     in1=perm[:, c, :], op0=ALU.is_equal, op1=ALU.add)
                    if (e, c) != (E1 - 1, NC - 1):
                        link(ins)
            signal(ins, "perm", 1)
            for t, ss, got, sig, rt, out, scale in ((T_b, hmx, "dk", "kss", "krt", "kn", 1.0),
                                                    (T_a, hsum, "dq", "qss", "qrt", "qn", DH ** -0.5)):
                for c in range(NC):
                    dve.wait_ge(S[got], c + 1)
                    link(V.tensor_tensor(F_b[:, c * D:(c + 1) * D], tm(t)[:, c, :], tm(t)[:, c, :], ALU.mult))
                    link(V.tensor_reduce(ss[:, c * HEADS:(c + 1) * HEADS], heads(F_b[:, c * D:(c + 1) * D]), AX, ALU.add))
                signal(V.tensor_scalar(ss[:, :], ss[:, :], 1e-6, None, ALU.add), sig, 1)
            for t, ss, got, sig, rt, out, scale in ((T_b, hmx, "dk", "kss", "krt", "kn", 1.0),
                                                    (T_a, hsum, "dq", "qss", "qrt", "qn", DH ** -0.5)):
                dve.wait_ge(S[rt], 1)
                link(V.reciprocal(ss[:, :], ss[:, :]))
                if scale != 1.0:
                    link(V.tensor_scalar(ss[:, :], ss[:, :], scale, None, ALU.mult))
                for c in range(NC):
                    V.tensor_tensor(heads(tm(t)[:, c, :]), heads(tm(t)[:, c, :]), per_head(ss, c), ALU.mult)\
                        .then_inc(S[out], 1)
            dve.wait_ge(S["vals_ps"], 1)
            vps = bank[3][:, 0:PC * 68].rearrange("p (a e v) -> p a e v", a=PC, e=E1)
            for p in range(PC):
                link(V.tensor_tensor(vmask[:, p, :, :], vps[:, p, :, :],
                                     oh[:, p, :].rearrange("p (e o) -> p e o", o=1).to_broadcast([P, E1, 17]), ALU.mult))
            for p in range(PC):
                ins = V.tensor_reduce(pv[:, p, :], vmask[:, p, :, :].rearrange("p e v -> p v e"), AX, ALU.add)
            link(ins)
            for p in range(PC):
                ins = V.tensor_scalar(pv[:, p, 8:16], pv[:, p, 8:16], forget[:, p:p + 1], None, ALU.add)
            signal(ins, "pv", 1)
            for p in range(PC):
                link(V.tensor_copy(ba[:, :, 0, p, :], pv[:, p, 0:8].rearrange("p (a b) -> p a b", b=2)))
            dve.wait_ge(S["ba"], 1)

            STEPS = 2 * PC
            with dve.Fori(0, HEADS // 2) as i:
                step = [0]

                def chain(ins):
                    step[0] += 1
                    ins.then_inc(S["loop_step"], 1)
                    dve.wait_ge(S["loop_step"], i * STEPS + step[0])

                V.tensor_scalar(ba_st[:, :, :, :], ba[:, bass.ds(i, 1), :, :, :].rearrange("p o a b c -> p (o a) b c"),
                                1.0, None, ALU.mult).then_inc(S["ba_st"], 1)
                dve.wait_ge(S["ba_st"], i + 1)
                for hh in range(2):
                    dve.wait_ge(S["arow"], i * 2 + hh + 1)
                    for p in range(PC):
                        ins = V.tensor_tensor_scan(dec[:, p * PAIRS + p * P:(p + 1) * PAIRS], bank[0][:, p * P:PAIRS],
                                                   identz[:, 0:PAIRS - p * P], 0.0, ALU.mult, ALU.add)
                        if p < PC - 1:
                            chain(ins)
                    ins.then_inc(S["scan"], 1)
                    dve.wait_ge(S["scan"], i * 2 + hh + 1)
                    for p in range(PC):
                        for z in range(2):
                            n = hh * 8 + p * 2 + z
                            dve.wait_ge(S["kq_ps"], i * 16 + n + 1)
                            sl = slice(p * PAIRS + p * P, (p + 1) * PAIRS)
                            V.scalar_tensor_tensor(out=(AT, MT)[z][hh][:, sl], in0=dec[:, sl],
                                                   scalar=ba_st[:, 0, p, hh:hh + 1], in1=bank[1 + n % 6][:, 0:PAIRS - p * P],
                                                   op0=ALU.mult, op1=ALU.mult).then_inc(S["prod"], 1)
                    dve.wait_ge(S["prod"], i * 16 + hh * 8 + 8)
                    m0b = m0[:, :].rearrange("p (o n) -> p o n", o=1).to_broadcast([P, PC, P])
                    idb = ident[:, :].rearrange("p (o n) -> p o n", o=1).to_broadcast([P, PC, P])
                    chain(V.tensor_tensor(XT[:, hh, :, :], ATd[hh], m0b, ALU.mult))
                    V.tensor_tensor(XT[:, hh, :, :], XT[:, hh, :, :], idb, ALU.add).then_inc(S["xt0"], 1)
                for l, b in enumerate(LEVELS):
                    for hh in range(2):
                        dve.wait_ge(S["t1_ps"], i * 2 * NL + 2 * l + hh + 1)
                        if l == 0:
                            dve.wait_ge(S["x0"], i * 2 + hh + 1)
                        mb = mlev[:, l, :].rearrange("p (o n) -> p o n", o=1).to_broadcast([P, PC, P // 2])
                        V.tensor_tensor(T1s[:, hh, :, :], bank[3 + hh][:, 0:256].rearrange("p (a n) -> p a n", a=PC), mb,
                                        ALU.mult).then_inc(S["t1"], 1)
                    for hh in range(2):
                        dve.wait_ge(S["dx_ps"], i * 2 * NL + 2 * l + hh + 1)
                        if l:
                            dve.wait_ge(S["x"], i * 2 * NL + 2 * (l - 1) + hh + 1)
                        even = X[:, hh, :, :].rearrange("q a (n two j) -> q (a n) two j", two=2, j=b)[:, :, 0, :]
                        dx = bank[3 + hh][:, 0:256].rearrange("p (m j) -> p m j", j=b)
                        V.tensor_tensor(even, even, dx, ALU.add).then_inc(S["x"], 1)
                for p in range(1, PC):
                    for hh in range(2):
                        dve.wait_ge(S["r_ps"], i * 6 + 2 * (p - 1) + hh + 1)
                        V.tensor_tensor(Rr[:, hh, :], v_st[:, p, hh * DH:(hh + 1) * DH], bank[3 + hh][:, 0:DH],
                                        ALU.subtract).then_inc(S["r"], 1)
                dve.wait_ge(S["o_ps"], i + 1)
                assert step[0] == STEPS

            for c in range(NC):
                dve.wait_ge(S["core_ps"], c + 1)
                link(V.tensor_copy(tm(T_a)[:, c, :], bank[c][:, :]))
                link(V.tensor_tensor(F_b[:, c * D:(c + 1) * D], tm(T_a)[:, c, :], tm(T_a)[:, c, :], ALU.mult))
                link(V.tensor_reduce(hsum[:, c * HEADS:(c + 1) * HEADS], heads(F_b[:, c * D:(c + 1) * D]), AX, ALU.add))
            signal(V.tensor_scalar(hsum[:, :], hsum[:, :], 1.0 / DH, EPS, ALU.mult, ALU.add), "css", 1)
            for c in range(NC):
                link(V.tensor_tensor(tm(T_d)[:, c, :], tm(T_d)[:, c, :], row(R_ON), ALU.mult))
                link(V.tensor_tensor(tm(T_a)[:, c, :], tm(T_a)[:, c, :], tm(T_d)[:, c, :], ALU.mult))
            dve.wait_ge(S["crt"], 1)
            link(V.reciprocal(hsum[:, :], hsum[:, :]))
            for c in range(NC):
                V.tensor_tensor(heads(tm(T_a)[:, c, :]), heads(tm(T_a)[:, c, :]), per_head(hsum, c), ALU.mult)\
                    .then_inc(S["core"], 1)
            for c in range(NC):
                dve.wait_ge(S["fin_ps"], c + 1)
                V.tensor_tensor(xs[:, c, :], xs[:, c, :], bank[4 + c][:, :], ALU.add).then_inc(S["fin"], 1)


def kernel(**inputs):
    import numpy as np
    import concourse.bacc as bacc
    from concourse import mybir as mb
    from concourse.bass_utils import run_bass_kernel_spmd

    g = {k: np.asarray(v) for k, v in inputs.items()}

    def unit(w):
        return w.reshape(FC, P, D).transpose(1, 0, 2).reshape(P, UNIT)

    q0, k0, v0 = (g["L0_mix_w_qkv"][i * D:(i + 1) * D].T for i in range(3))
    q1, k1, v1 = (g["L1_mix_Wqkv"][i * D:(i + 1) * D].T for i in range(3))
    weights = [q0, k0, v0, g["L0_mix_w_out"].T, g["L0_gnn_W_gcn"][0], g["L0_gnn_W_mlp"][0], g["L0_gnn_W_gcn"][1],
               g["L0_gnn_W_mlp"][1], g["L0_ffn_W1"].transpose(1, 0, 2).reshape(D, D), g["L0_ffn_W2"].reshape(D, D),
               q1, k1, v1, g["L1_gnn_W"].T, g["L1_mix_Wout"].T, g["L1_ffn_Wq"], g["L1_ffn_Wk"], g["L1_ffn_Wv"],
               g["L1_ffn_Wg"], g["L1_ffn_Wo"]]
    rows = np.concatenate([g["L0_gnn_b_mlp"][0], g["L0_gnn_b_mlp"][1], g["L0_mix_out_gamma"], g["L1_gnn_b"],
                           g["L1_mix_bout"], np.tile(g["L1_ffn_o_norm_weight"], HEADS), g["L0_ffn_bg"],
                           g["L1_ffn_A_log"], g["L1_ffn_dt_bias"]])[None]
    cols = np.concatenate([g["L0_gnn_b_gcn"].reshape(8, P).T, g["L0_mix_norm_gamma"].reshape(4, P).T,
                           g["L0_ffn_b1"].reshape(4, P).T, np.tile(g["L0_ffn_bs1"], 2).reshape(P, 1)], axis=1)
    gw = np.concatenate([g["L0_ffn_Wg"], g["L0_ffn_Ws1"], g["L1_ffn_Wgate"], g["L1_ffn_Wb"], g["L1_ffn_Wa"]], axis=1)
    arrays = {
        "x": g["x"].reshape(NC, P, D).transpose(1, 0, 2),
        "edges": np.stack([g["src"], g["dst"]]).reshape(2, ET, P).transpose(2, 0, 1),
        "edge_weights": np.stack([g["edge_weight"], g["edge_weight1"][:, 0]]).reshape(2, ET, P).transpose(2, 0, 1),
        "weights": np.stack([unit(w) for w in weights]),
        "rows": rows,
        "cols": cols,
        "gw": gw.reshape(FC, P, GW).transpose(1, 0, 2),
        "b29": np.concatenate([g["L0_ffn_b2"], g["L0_ffn_bs2"][None]]),
        "ws2": g["L0_ffn_Ws2"],
    }
    nc = bacc.Bacc("TRN2", target_bir_lowering=False, num_devices=1)
    arrays = {"in_" + k: np.ascontiguousarray(v) for k, v in arrays.items()}
    args = [nc.dram_tensor(k, v.shape, mb.dt.from_np(v.dtype), kind="ExternalInput").ap() for k, v in arrays.items()]
    out = nc.dram_tensor("out", (P, NC, D), mb.dt.float32, kind="ExternalOutput").ap()
    build(nc, *args, out)
    r = run_bass_kernel_spmd(nc, [arrays], core_ids=[0])
    return np.asarray(r.results[0]["out"]).transpose(1, 0, 2).reshape(N, D)
```

```python
from contextlib import ExitStack

import concourse.bass as bass
from concourse import mybir

P = 128
N = 256
D = 512
NC = N // P
FC = D // P
HEADS = 8
DH = D // HEADS
UNIT = FC * D
SLOTS = 8
EDGES = 4352
ET = EDGES // P
E0 = 8
E1 = 4
PAIRS = 2 * N
PC = PAIRS // P
B = 32
NB = P // B
HC = PC * HEADS
PAIR_HEADS = HEADS // 2
EPS = 1e-5

F32 = mybir.dt.float32
BF16 = mybir.dt.bfloat16
I32 = mybir.dt.int32
ALU = mybir.AluOpType
ACT = mybir.ActivationFunctionType
AX = mybir.AxisListType.X

(U_Q0, U_K0, U_V0, U_O0, U_GCN0, U_MLP0, U_GCN1, U_MLP1, U_W1, U_W2,
 U_Q1, U_K1, U_V1, U_AGG, U_O1, U_DQ, U_DK, U_DV, U_DG, U_DO) = range(20)
UNITS = 20
(R_MLP0, R_MLP1, R_OG, R_B1, R_BOUT, R_ON) = range(6)
ROWS = 6 * D
R_BG, R_ALOG, R_DT = ROWS, ROWS + 8, ROWS + 16
ROWS_ALL = ROWS + 24
C_GCN, C_GAMMA, C_B1, C_BS1 = 0, 8, 12, 16
COLS = 17
G_WG, G_WS1, G_SM = 0, 8, 72
GW = 92


def build(nc, d_x, d_edge, d_ew, d_w, d_rows, d_cols, d_gw, d_b29, d_ws2, d_out):
    with ExitStack() as ctx:
        def sb(name, shape, dt=F32):
            return ctx.enter_context(nc.sbuf_tensor(name, shape, dt))

        def sem(name):
            return ctx.enter_context(nc.semaphore(name))

        class Sems:
            def __init__(self):
                self.made = {}

            def __getitem__(self, name):
                if name not in self.made:
                    self.made[name] = sem("s_" + name)
                return self.made[name]

        S = Sems()

        bank = [ctx.enter_context(nc.psum_tensor(f"bank{i}", [P, 512], F32)) for i in range(8)]

        ring = sb("ring", [P, SLOTS * UNIT])
        xs = sb("xs", [P, NC, D])
        T_n = sb("T_n", [P, NC * D])
        T_a = sb("T_a", [P, NC * D])
        T_b = sb("T_b", [P, NC * D])
        T_c = sb("T_c", [P, NC * D])
        T_d = sb("T_d", [P, NC * D])
        F_a = sb("F_a", [P, FC * N])
        F_b = sb("F_b", [P, FC * N])
        F_c = sb("F_c", [P, FC * N])
        tm = lambda t: t[:, :].rearrange("p (c f) -> p c f", c=NC)
        fm = lambda t: t[:, :].rearrange("p (k n) -> p k n", k=FC)
        rows = sb("rows", [P, ROWS_ALL])
        row = lambda r: rows[:, r * D:(r + 1) * D]
        cols = sb("cols", [P, COLS])
        gw = sb("gw", [P, FC, GW])
        b29 = sb("b29", [E0 + 1, D])
        ws2 = sb("ws2", [DH, D])
        edge_i = sb("edge_i", [P, 2, ET], I32)
        edge_f = sb("edge_f", [P, 2, ET])
        ew = sb("ew", [P, 2, ET])
        ewp = sb("ewp", [P, 3, 2, ET])
        ewb = sb("ewb", [P, 2, ET], BF16)
        iota_b = sb("iota_b", [P, N], BF16)
        iota_f = sb("iota_f", [P, PAIRS])
        ident = sb("ident", [P, P])
        identz = sb("identz", [P, PAIRS])
        ones = sb("ones", [P, P])
        tri = sb("tri", [P, P])
        zer = sb("zer", [P, 512], BF16)
        src1h = sb("src1h", [P, 2, N], BF16)
        dst1h = sb("dst1h", [P, 2, 3, 2, N], BF16)
        A0 = sb("A0", [P, NC, N])
        A1 = sb("A1", [P, NC, N])
        AnT = sb("AnT", [P, NC, N])
        ctxs = sb("ctxs", [P, FC, P])
        blockm = sb("blockm", [P, P])
        st = sb("st", [P, NC, 6])
        mv = sb("mv", [P, NC, 2])
        rstd = sb("rstd", [P, NC, 1])
        mhalf = sb("mhalf", [P, 2])
        deg = sb("deg", [P, 4, NC])
        hmx = sb("hmx", [P, NC * HEADS])
        hsum = sb("hsum", [P, NC * HEADS])
        kmx = sb("kmx", [P, FC])
        ksum = sb("ksum", [P, FC])
        ltri = sb("ltri", [P, E0, E0])
        rk = sb("rk", [P, 2, NC, E0, E0])
        gl = sb("gl", [P, 4, NC, E0])
        sel = sb("sel", [P, NC, E0])
        gmx = sb("gmx", [P, 2, NC])
        comb = sb("comb", [P, NC, E0 + 1])
        combT = sb("combT", [E0 + 1, N])
        spread = sb("spread", [E0 + 1, FC, P])
        hsT = sb("hsT", [DH, N])
        sm = sb("sm", [P, NC, 20])
        dl = sb("dl", [P, 8, NC, HEADS])
        vals = sb("vals", [P, NC, E1, 17])
        pre = sb("pre", [P, NC, E1])
        posm = sb("posm", [P, NC, E1])
        idx = sb("idx", [P, PC])
        ge = sb("ge", [P, PC, E1 + 1])
        oh = sb("oh", [P, PC, E1])
        first = sb("first", [P, PC, E1])
        forget = sb("forget", [P, PC])
        vmask = sb("vmask", [P, PC, E1, 17])
        pv = sb("pv", [P, PC, 17])
        perm = sb("perm", [P, NC, PAIRS])
        permT = sb("permT", [P, PC, N])
        kp = sb("kp", [P, FC, 2, PAIRS])
        vp = sb("vp", [P, PC, D])
        a4 = sb("a4", [P, PC, HEADS])
        a0 = sb("a0", [P, PC, HEADS])
        later = sb("later", [P, 1])
        dbeta = sb("dbeta", [P, PC, HEADS])
        cT = sb("cT", [HEADS, PAIRS])
        cend = sb("cend", [P, PC, PAIR_HEADS])
        kd = sb("kd", [P, PC, D])
        Xf = sb("Xf", [P, HC, 2 * B])

        def wslot(u):
            s = u % SLOTS
            return ring[:, s * UNIT:(s + 1) * UNIT].rearrange("p (k o) -> p k o", k=FC)

        XT = ring[:, 0:2 * UNIT].rearrange("p (n t) -> p n t", n=HC)
        oall = ring[:, 2 * UNIT:3 * UNIT].rearrange("p (a f) -> p a f", a=PC)
        AT = ring[:, 4 * UNIT:6 * UNIT].rearrange("p (n t) -> p n t", n=HC)
        MT = ring[:, 6 * UNIT:8 * UNIT].rearrange("p (n t) -> p n t", n=HC)
        zb = T_n[:, :].rearrange("p (two c t) -> p two c t", two=2, c=PC)
        dec = F_b[:, :].rearrange("p (two c t) -> p two c t", two=2, c=PC)
        Ab = F_a[:, :].rearrange("p (t s) -> p t s", t=B)
        Xb = T_n[:, :].rearrange("p (t s) -> p t s", t=B)
        prodb = F_b[:, 0:B * B // 4]
        T32 = F_b[:, :].rearrange("p (n s) -> p n s", n=HC)
        U = F_c[:, :].rearrange("p (two f) -> p two f", two=2)
        St = T_a[:, :].rearrange("p (two j v) -> p two j v", two=2, j=PAIR_HEADS)
        crow = lambda j: (T_b, T_c)[j // 2][:, (j % 2) * PAIRS:(j % 2 + 1) * PAIRS]

        used = {U_Q0: ("q_ps", 2), U_K0: ("k_ps", 2), U_V0: ("v_ps", 2), U_O0: ("mix_ps", 2),
                U_GCN0: ("h2_ps", 2), U_MLP0: ("h3_ps", 2), U_GCN1: ("h2_ps", 4), U_MLP1: ("h3_ps", 4),
                U_W1: ("hid_ps", 2), U_W2: ("y_ps", 2), U_Q1: ("q_ps", 4), U_K1: ("k_ps", 4)}

        block = ctx.enter_context(nc.Block())

        @block.sync
        def _(sp):
            sp.dma_start(xs[:, :, :], d_x).then_inc(S["x_in"], 16)
            sp.dma_start(cols[:, :], d_cols).then_inc(S["cols_in"], 16)
            for u in range(3):
                sp.dma_start(ring[:, u * UNIT:(u + 1) * UNIT], d_w[u]).then_inc(S["w%d" % (u % SLOTS)], 16)
            sp.dma_start(rows[:, :], d_rows[0, :].partition_broadcast(P)).then_inc(S["rows_in"], 16)
            sp.dma_start(gw[:, :, :], d_gw).then_inc(S["gw_in"], 16)
            sp.dma_start(b29[:, :], d_b29).then_inc(S["ffn_in"], 16)
            sp.dma_start(ws2[:, :], d_ws2).then_inc(S["ffn_in"], 16)
            for u in range(3, UNITS):
                if u >= SLOTS:
                    sp.wait_ge(S[used[u - SLOTS][0]], used[u - SLOTS][1])
                s = u % SLOTS
                sp.dma_start(ring[:, s * UNIT:(s + 1) * UNIT], d_w[u]).then_inc(S["w%d" % (u % SLOTS)], 16)
            for c in range(NC):
                sp.wait_ge(S["fin"], c + 1)
                sp.dma_start(d_out[:, c, :], xs[:, c, :]).then_inc(S["out"], 16)
            sp.wait_ge(S["out"], 16 * NC)

        def diagonal_block(q, half):
            r = slice(q * B, (q + 1) * B)
            return (XT[r, :, q * B + 16 * half:q * B + 16 * half + 16],
                    bank[4 + half][r, :].rearrange("p (t n) -> p n t", n=HC))

        def inverse_block(q, half):
            r, at = slice(q * B, (q + 1) * B), (q % 2) * B + 16 * half
            return Xf[r, :, at:at + 16], bank[6 + half][r, :].rearrange("p (s n) -> p n s", n=HC)

        def t32_block(qe, g_):
            ro = slice((qe + 1) * B, (qe + 2) * B)
            return (T32[ro, g_ * HC // 2:(g_ + 1) * HC // 2, :], bank[g_][ro, :].rearrange("p (n s) -> p n s", s=B))

        @block.gpsimd
        def _(g):
            count = [0]

            def link(ins):
                count[0] += 1
                ins.then_inc(S["pool_step"], 1)
                g.wait_ge(S["pool_step"], count[0])

            g.dma_start(edge_i[:, :, :], d_edge).then_inc(S["edges_in"], 16)
            g.dma_start(ew[:, :, :], d_ew).then_inc(S["edges_in"], 16)
            g.memset(mhalf[:, :], -0.5).then_inc(S["mhalf"], 1)
            g.memset(zer[:, :], 0.0).then_inc(S["zer"], 1)
            link(g.memset(identz[:, :], 0.0))
            link(g.affine_select(out=identz[:, 0:P], in_=identz[:, 0:P], compare_op=ALU.not_equal, fill=1.0,
                                 base=0, pattern=[[-1, P]], channel_multiplier=1))
            g.tensor_copy(ident[:, :], identz[:, 0:P]).then_inc(S["ident"], 1)
            g.iota(iota_f[:, :], [[1, PAIRS]], base=0, channel_multiplier=0,
                   allow_small_or_imprecise_dtypes=True).then_inc(S["iota"], 1)
            g.wait_ge(S["iota"], 1)
            g.tensor_copy(iota_b[:, :], iota_f[:, 0:N]).then_inc(S["iota"], 1)

            def power(n):
                g.wait_ge(S["mhalf"], 1)
                g.wait_ge(S["var"], n + 1)
                g.tensor_tensor(rstd[:, :, 0], mv[:, :, 1], mhalf[:, :], ALU.pow).then_inc(S["rstd"], 1)

            power(0)
            link(g.memset(ones[:, :], 1.0))
            link(g.memset(blockm[:, :], 0.0))
            link(g.memset(blockm[0:DH, 0:DH], 1.0))
            link(g.memset(blockm[DH:P, DH:P], 1.0))
            power(1)
            link(g.affine_select(out=tri[:, :], in_=ones[:, :], compare_op=ALU.is_ge, fill=0.0,
                                 base=-1, pattern=[[1, P]], channel_multiplier=-1))
            link(g.memset(ltri[:, :, :], 1.0))
            link(g.affine_select(out=ltri[:, :, :], in_=ltri[:, :, :], compare_op=ALU.is_ge, fill=0.0,
                                 base=-1, pattern=[[1, E0], [-1, E0]], channel_multiplier=0))
            link(g.memset(spread[:, :, :], 1.0))
            link(g.affine_select(out=spread[:, :, :], in_=spread[:, :, :], compare_op=ALU.is_ge, fill=0.0,
                                 base=0, pattern=[[P, FC], [1, P]], channel_multiplier=-DH))
            link(g.affine_select(out=spread[:, :, :], in_=spread[:, :, :], compare_op=ALU.is_ge, fill=0.0,
                                 base=DH - 1, pattern=[[-P, FC], [-1, P]], channel_multiplier=DH))
            link(g.memset(later[:, :], 1.0))
            link(g.affine_select(out=later[:, :], in_=later[:, :], compare_op=ALU.is_ge, fill=0.0,
                                 base=-1, pattern=[[0, 1]], channel_multiplier=1))
            link(g.memset(Xf[:, :, :], 0.0))
            link(g.iota(idx[:, :], [[P, PC]], base=0, channel_multiplier=1, allow_small_or_imprecise_dtypes=True))
            link(g.memset(ge[:, :, :], 0.0))
            g.memset(comb[:, :, E0:E0 + 1], 0.5).then_inc(S["consts"], 1)
            g.wait_ge(S["deg"], 1)
            g.tensor_tensor(deg[:, 1, :], deg[:, 1, :], mhalf[:, :], ALU.pow).then_inc(S["degp"], 1)
            for n in range(2, 6):
                power(n)

            g.wait_ge(S["dk_ps"], 2)
            g.wait_ge(S["dv_ps"], 2)
            g.memset(XT[:, :, :], 0.0).then_inc(S["xt_zero"], 1)
            g.wait_ge(S["pv"], 1)
            for h in range(HEADS):
                if h >= 2:
                    g.wait_ge(S["scan"], h - 1)
                g.tensor_tensor(zb[:, h % 2, :, :], ident[:, :].rearrange("p (o t) -> p o t", o=1).to_broadcast([P, PC, P]),
                                pv[:, :, h:h + 1].to_broadcast([P, PC, P]), ALU.mult).then_inc(S["zb"], 1)
            g.wait_ge(S["scan"], HEADS)
            link(g.memset(T_n[:, :], 0.0))
            g.memset(T_n[:, 0:B * B].rearrange("p (r) -> p r")[:, 0:B * B:B + 1], 1.0).then_inc(S["xb0"], 1)
            g.wait_ge(S["kp_ps"], 2 * FC)
            g.memset(T_a[:, :], 0.0).then_inc(S["st_zero"], 1)
            g.wait_ge(S["ktm_ps"], PC)
            g.wait_ge(S["mt"], HEADS)
            for j in range(PAIR_HEADS):
                g.wait_ge(S["crow"], j + 1)
                if j % 2:
                    v = (T_b, T_c)[j // 2][:, :].rearrange("p (a c t) -> p c a t", a=2, c=PC)
                    g.tensor_copy(cend[:, :, j - 1:j + 1], v[:, :, :, P - 1]).then_inc(S["cend"], 1)
                for z in range(2):
                    g.tensor_tensor(kp[:, j, z, :], kp[:, j, z, :], crow(j), ALU.mult).then_inc(S["kqc"], 1)

        @block.tensor
        def _(pe):
            mm, tp = nc.tensor.matmul, nc.tensor.transpose

            def weight(u):
                pe.wait_ge(S["w%d" % (u % SLOTS)], 16 * (u // SLOTS + 1))

            def to_fm(src, b0, b1, name):
                for k in range(FC):
                    for c in range(NC):
                        last = tp((b0, b1)[k // 2][:, (k % 2) * N + c * P:(k % 2) * N + (c + 1) * P],
                                  src[:, c, k * P:(k + 1) * P], ident[:, :])
                    if k % 2:
                        last.then_inc(S[name], 1)

            def to_tm(src, b0, b1, name):
                for c in range(NC):
                    for k in range(FC):
                        last = tp((b0, b1)[c][:, k * P:(k + 1) * P], src[:, k, c * P:(c + 1) * P], ident[:, :])
                    last.then_inc(S[name], 1)

            def proj_tm(act, u, b0, b1, name):
                weight(u)
                for c in range(NC):
                    for k in range(FC):
                        last = mm((b0, b1)[c][:, :], act[:, k, c * P:(c + 1) * P], wslot(u)[:, k, :],
                                  start=(k == 0), stop=(k == FC - 1))
                    last.then_inc(S[name], 1)

            def proj_fm(act, u, b0, b1, name):
                weight(u)
                for o in range(FC):
                    for k in range(FC):
                        last = mm((b0, b1)[o // 2][:, (o % 2) * N:(o % 2 + 1) * N], wslot(u)[:, k, o * P:(o + 1) * P],
                                  act[:, k, :], start=(k == 0), stop=(k == FC - 1))
                    if o % 2:
                        last.then_inc(S[name], 1)

            def attention_in(l, uq, uk, uv):
                proj_tm(fm(F_a), uq, bank[2], bank[3], "q_ps")
                proj_fm(fm(F_a), uk, bank[4], bank[5], "k_ps")
                proj_tm(fm(F_a), uv, bank[6], bank[7], "v_ps")

            def attention_core(l):
                pe.wait_ge(S["ek"], l * 4 + 4)
                to_tm(fm(F_c), bank[4], bank[5], "ekt_ps")
                pe.wait_ge(S["qs"], l * 2 + 2)
                to_fm(tm(T_b), bank[2], bank[3], "qT_ps")
                pe.wait_ge(S["v"], l * 2 + 2)
                pe.wait_ge(S["ekt"], l * 2 + 2)
                for j in range(FC):
                    for c in range(NC):
                        last = mm(bank[6][:, j * P:(j + 1) * P], tm(T_c)[:, c, j * P:(j + 1) * P],
                                  tm(T_d)[:, c, j * P:(j + 1) * P], start=(c == 0), stop=(c == NC - 1))
                last.then_inc(S["ctx_ps"], 1)
                pe.wait_ge(S["ctx"], l * 1 + 1)
                pe.wait_ge(S["qT"], l * 2 + 2)
                for j in range(FC):
                    last = mm(bank[4 + j // 2][:, (j % 2) * N:(j % 2 + 1) * N], ctxs[:, j, :], fm(F_b)[:, j, :],
                              start=True, stop=True)
                    if j % 2:
                        last.then_inc(S["oT_ps"], 1)

            def x64(c):
                lo, hi = slice(0, 2 * B), slice(2 * B, P)
                pe.wait_ge(S["t64"], c + 1)
                pe.wait_ge(S["xt32"], 4)
                if c >= 2:
                    pe.wait_ge(S["xt64"], c - 1)
                for h in range(HEADS):
                    last = mm(bank[4 + c % 2][lo, h * DH:(h + 1) * DH], Xf[hi, c * HEADS + h, :],
                              XT[hi, c * HEADS + h, hi], start=True, stop=True)
                last.then_inc(S["x64_ps"], 1)

            pe.wait_ge(S["ident"], 1)
            pe.wait_ge(S["normed"], 4)
            to_fm(tm(T_a), bank[0], bank[1], "turned_ps")
            pe.wait_ge(S["turned"], 2)
            attention_in(0, U_Q0, U_K0, U_V0)

            pe.wait_ge(S["zer"], 1)
            for c in range(NC):
                mm(bank[c][:, :], zer[:, 0:P], zer[:, :], start=True, stop=False, skip_group_check=True)
            with pe.Fori(0, ET // 2) as i:
                for half in range(2):
                    pe.wait_ge(S["onehot"], i * 2 + half + 1)
                    for c in range(NC):
                        for part in range(3):
                            last = mm(bank[c][:, :], src1h[:, half, c * P:(c + 1) * P],
                                      dst1h[:, half, part, :, :], start=False, stop=False, skip_group_check=True)
                    last.then_inc(S["adj_tile"], 1)
            for c in range(NC):
                mm(bank[c][:, :], zer[:, 0:P], zer[:, :], start=False, stop=True,
                   skip_group_check=True).then_inc(S["adj_ps"], 1)

            attention_core(0)
            pe.wait_ge(S["oT"], 2)
            proj_tm(fm(F_a), U_O0, bank[2], bank[3], "mix_ps")

            pe.wait_ge(S["A0s"], 1)
            for dc in range(NC):
                for sc in range(NC):
                    last = tp(bank[7][:, dc * N + sc * P:dc * N + (sc + 1) * P], A0[:, sc, dc * P:(dc + 1) * P], ident[:, :])
            last.then_inc(S["AnT_ps"], 1)
            pe.wait_ge(S["AnT"], 1)
            for l in range(2):
                h = tm(T_n) if l == 0 else tm(T_b)
                if l == 1:
                    pe.wait_ge(S["h"], 2)
                for k in range(FC):
                    for dc in range(NC):
                        last = mm(bank[4 + k // 2][:, (k % 2) * N:(k % 2 + 1) * N], h[:, dc, k * P:(k + 1) * P],
                                  AnT[:, dc, :], start=(dc == 0), stop=(dc == NC - 1))
                    if k % 2:
                        last.then_inc(S["h1_ps"], 1)
                pe.wait_ge(S["h1T"], 2 * l + 2)
                proj_fm(fm(F_b), (U_GCN0, U_GCN1)[l], bank[6], bank[7], "h2_ps")
                pe.wait_ge(S["h2T"], 2 * l + 2)
                proj_tm(fm(F_c), (U_MLP0, U_MLP1)[l], bank[0], bank[1], "h3_ps")

            pe.wait_ge(S["normed"], 8)
            to_fm(tm(T_a), bank[2], bank[3], "turned_ps")
            pe.wait_ge(S["turned"], 4)
            pe.wait_ge(S["gw_in"], 16)
            for c in range(NC):
                for k in range(FC):
                    last = mm(bank[4][:, c * E0:(c + 1) * E0], fm(F_a)[:, k, c * P:(c + 1) * P],
                              gw[:, k, G_WG:G_WG + E0], start=(k == 0), stop=(k == FC - 1))
            last.then_inc(S["gate_ps"], 1)
            proj_fm(fm(F_a), U_W1, bank[6], bank[7], "hid_ps")
            for k in range(FC):
                last = mm(bank[5][0:DH, 0:N], gw[:, k, G_WS1:G_WS1 + DH], fm(F_a)[:, k, :],
                          start=(k == 0), stop=(k == FC - 1))
            last.then_inc(S["hs_ps"], 1)
            pe.wait_ge(S["comb"], 1)
            for c in range(NC):
                last = tp(bank[4][0:E0 + 1, c * P:(c + 1) * P], comb[:, c, :], ident[:, :])
            last.then_inc(S["combT_ps"], 1)
            pe.wait_ge(S["combT"], 1)
            for o in range(FC):
                last = mm(bank[o // 2][:, (o % 2) * N:(o % 2 + 1) * N], spread[:, o, :], combT[:, :],
                          start=True, stop=True)
                if o % 2:
                    last.then_inc(S["combB_ps"], 1)
            pe.wait_ge(S["hw"], 2)
            pe.wait_ge(S["hsT"], 1)
            pe.wait_ge(S["ffn_in"], 32)
            weight(U_W2)
            for c in range(NC):
                for k in range(FC):
                    mm(bank[2 + c][:, :], fm(F_c)[:, k, c * P:(c + 1) * P], wslot(U_W2)[:, k, :], start=(k == 0), stop=False)
                mm(bank[2 + c][:, :], hsT[:, c * P:(c + 1) * P], ws2[:, :], start=False, stop=False)
                mm(bank[2 + c][:, :], combT[:, c * P:(c + 1) * P], b29[:, :], start=False, stop=True).then_inc(S["y_ps"], 1)

            pe.wait_ge(S["normed"], 10)
            to_fm(tm(T_n), bank[0], bank[1], "turned_ps")
            pe.wait_ge(S["turned"], 6)
            attention_in(1, U_Q1, U_K1, U_V1)
            pe.wait_ge(S["A1"], 1)
            for k in range(FC):
                for c in range(NC):
                    last = mm(bank[k // 2][:, (k % 2) * N:(k % 2 + 1) * N], tm(T_n)[:, c, k * P:(k + 1) * P],
                              A1[:, c, :], start=(c == 0), stop=(c == NC - 1))
                if k % 2:
                    last.then_inc(S["agg_ps"], 1)
            attention_core(1)
            pe.wait_ge(S["oT"], 4)
            pe.wait_ge(S["aggT"], 2)
            weight(U_AGG)
            weight(U_O1)
            for c in range(NC):
                for k in range(FC):
                    mm(bank[2 + c][:, :], fm(T_a)[:, k, c * P:(c + 1) * P], wslot(U_AGG)[:, k, :], start=(k == 0), stop=False)
                for k in range(FC):
                    last = mm(bank[2 + c][:, :], fm(F_a)[:, k, c * P:(c + 1) * P], wslot(U_O1)[:, k, :],
                              start=False, stop=(k == FC - 1))
                last.then_inc(S["mix_ps"], 1)

            pe.wait_ge(S["normed"], 12)
            to_fm(tm(T_n), bank[0], bank[1], "turned_ps")
            pe.wait_ge(S["turned"], 8)
            for c in range(NC):
                for k in range(FC):
                    last = mm(bank[2][:, c * 20:(c + 1) * 20], fm(F_a)[:, k, c * P:(c + 1) * P],
                              gw[:, k, G_SM:G_SM + 20], start=(k == 0), stop=(k == FC - 1))
            last.then_inc(S["sm_ps"], 1)
            proj_tm(fm(F_a), U_DQ, bank[3], bank[4], "dq_ps")
            proj_tm(fm(F_a), U_DK, bank[5], bank[6], "dk_ps")
            proj_tm(fm(F_a), U_DV, bank[7], bank[0], "dv_ps")
            pe.wait_ge(S["sm"], 1)
            proj_tm(fm(F_a), U_DG, bank[1], bank[2], "dg_ps")
            pe.wait_ge(S["dq"], 2)
            pe.wait_ge(S["sel"], 1)
            for c in range(NC):
                for kc in range(NC):
                    mm(bank[3][:, c * E1:(c + 1) * E1], ones[:, :], pre[:, kc, :], start=(kc == 0), stop=False)
                for kc in range(c + 1):
                    mm(bank[3][:, c * E1:(c + 1) * E1], (tri if kc == c else ones)[:, :], sel[:, kc, 0:E1],
                       start=False, stop=(kc == c))
            for kc in range(NC):
                last = mm(bank[3][:, 2 * E1:3 * E1], ones[:, :], pre[:, kc, :], start=(kc == 0), stop=(kc == NC - 1))
            last.then_inc(S["pos_ps"], 1)
            pe.wait_ge(S["perm"], 1)
            pe.wait_ge(S["dv"], 2)
            for p in range(PC):
                for c in range(NC):
                    last = mm(bank[3][:, p * 68:(p + 1) * 68], perm[:, c, p * P:(p + 1) * P],
                              vals[:, c, :, :], start=(c == 0), stop=(c == NC - 1))
            last.then_inc(S["vals_ps"], 1)
            for p in range(PC):
                b = (4, 5, 6, 7)[p]
                if p == 1:
                    pe.wait_ge(S["dk"], 2)
                for c in range(NC):
                    last = mm(bank[b][:, :], perm[:, c, p * P:(p + 1) * P], tm(T_c)[:, c, :],
                              start=(c == 0), stop=(c == NC - 1))
                last.then_inc(S["vp_ps"], 1)
            pe.wait_ge(S["kn"], 2)
            pe.wait_ge(S["dg"], 2)
            for k in range(FC):
                b = (0, 1, 2, 4)[k]
                if k == 3:
                    pe.wait_ge(S["vp"], 1)
                for c in range(NC):
                    last = mm(bank[b][:, :], tm(T_b)[:, c, k * P:(k + 1) * P], perm[:, c, :],
                              start=(c == 0), stop=(c == NC - 1))
                last.then_inc(S["kp_ps"], 1)
            pe.wait_ge(S["qn"], 2)
            for k in range(FC):
                b = (5, 6, 7, 0)[k]
                if k < 3:
                    pe.wait_ge(S["vp"], k + 2)
                else:
                    pe.wait_ge(S["kp"], 1)
                for c in range(NC):
                    last = mm(bank[b][:, :], tm(T_a)[:, c, k * P:(k + 1) * P], perm[:, c, :],
                              start=(c == 0), stop=(c == NC - 1))
                last.then_inc(S["kp_ps"], 1)
            for p in range(PC):
                if p % 2 == 0:
                    pe.wait_ge(S["kp"], 2 + p // 2)
                for c in range(NC):
                    last = tp(bank[1 + p // 2][:, (p % 2) * N + c * P:(p % 2) * N + (c + 1) * P],
                              perm[:, c, p * P:(p + 1) * P], ident[:, :])
                if p % 2:
                    last.then_inc(S["permT_ps"], 1)
            pe.wait_ge(S["kp"], 8)
            pe.wait_ge(S["permT"], 2)
            pe.wait_ge(S["pv"], 1)

            pe.wait_ge(S["a0"], 1)
            for c in range(PC):
                last = tp(bank[6][0:HEADS, c * P:(c + 1) * P], a4[:, c, :], ident[:, :])
            last.then_inc(S["aT_ps"], 1)
            for h in range(HEADS):
                j, r = h // 2, slice((h % 2) * DH, (h % 2 + 1) * DH)
                if h >= 2:
                    pe.wait_ge(S["scan"], h - 1)
                for c in range(PC):
                    last = tp(bank[h % 2][:, c * P:(c + 1) * P], a0[:, c, h:h + 1].to_broadcast([P, P]), ident[:, :])
                last.then_inc(S["arow"], 1)
                for z, ps, used_by in ((0, "kk_ps", "at"), (1, "qk_ps", "mt")):
                    if h >= 2:
                        pe.wait_ge(S[used_by], h - 1)
                    for c in range(PC):
                        last = mm(bank[2 + 2 * z + h % 2][:, c * P:(c + 1) * P], kp[r, j, 0, c * P:(c + 1) * P],
                                  kp[r, j, z, c * P:(c + 1) * P], start=True, stop=True)
                    last.then_inc(S[ps], 1)
            pe.wait_ge(S["at"], HEADS)
            pe.wait_ge(S["scan"], HEADS)
            for c in range(PC):
                for j in range(FC):
                    last = tp(bank[(2, 3, 0, 1)[c]][:, j * P:(j + 1) * P], kp[:, j, 0, c * P:(c + 1) * P], ident[:, :])
                last.then_inc(S["ktm_ps"], 1)
            pe.wait_ge(S["cT"], 1)
            for t in range(B):
                for q in range(NB):
                    r = slice(q * B, (q + 1) * B)
                    last = mm(bank[6 + t // 16][r, (t % 16) * B:(t % 16 + 1) * B], AT[r, :, q * B + t], ident[r, r],
                              start=True, stop=True)
                if t % 16 == 15:
                    last.then_inc(S["ab_ps"], 1)
            for j in range(PAIR_HEADS):
                pe.wait_ge(S["kd"], j + 1)
                mm(bank[(2, 3, 0, 1)[j]][:, :], spread[0:HEADS, j, :], cT[:, :], start=True, stop=True)\
                    .then_inc(S["crow_ps"], 1)
            pe.wait_ge(S["mt"], HEADS)
            pe.wait_ge(S["xb0"], 1)
            for t in range(B):
                if t:
                    pe.wait_ge(S["xrow"], t)
                for q in range(NB):
                    r = slice(q * B, (q + 1) * B)
                    last = mm(bank[4 + t // 16][r, (t % 16) * HC:(t % 16 + 1) * HC], Xb[r, t, :], ident[r, r],
                              start=True, stop=True)
                if t % 16 == 15:
                    last.then_inc(S["xd_ps"], 1)
            pe.wait_ge(S["ab"], 2)
            for s_ in range(B):
                for q in range(NB - 1):
                    r = slice(q * B, (q + 1) * B)
                    last = mm(bank[6 + s_ // 16][r, (s_ % 16) * HC:(s_ % 16 + 1) * HC], Xb[r, :, s_], ident[r, r],
                              start=True, stop=True)
                if s_ % 16 == 15:
                    last.then_inc(S["xf_ps"], 1)
            pe.wait_ge(S["crow"], PAIR_HEADS)
            pe.wait_ge(S["xf_act"], 3)
            pe.wait_ge(S["xf_dve"], 3)
            G = HC // 2
            for g_ in range(2):
                for n in range(G):
                    for qe in (0, 2):
                        re, ro = slice(qe * B, (qe + 1) * B), slice((qe + 1) * B, (qe + 2) * B)
                        last = mm(bank[g_][ro, n * B:(n + 1) * B], AT[re, g_ * G + n, ro], Xf[re, g_ * G + n, 0:B],
                                  start=True, stop=True)
                last.then_inc(S["t32_ps"], 1)
            pe.wait_ge(S["xd_act"], 4)
            pe.wait_ge(S["xd_dve"], 4)
            for g_ in range(2):
                pe.wait_ge(S["t32_act"], g_ + 1)
                pe.wait_ge(S["t32_dve"], g_ + 1)
                for n in range(G):
                    m = g_ * G + n
                    for qe in (0, 2):
                        re, ro = slice(qe * B, (qe + 1) * B), slice((qe + 1) * B, (qe + 2) * B)
                        mm(bank[2 + g_][re, n * B:(n + 1) * B], T32[ro, m, :], XT[ro, m, ro], start=True, stop=True)
                    last = mm(bank[4 + g_][B:2 * B, n * B:(n + 1) * B], XT[B:2 * B, m, B:2 * B], T32[B:2 * B, m, :],
                              start=True, stop=True)
                last.then_inc(S["x32_ps"], 1)
            lo, hi = slice(0, 2 * B), slice(2 * B, P)
            for c in range(PC):
                pe.wait_ge(S["x21"], c // 2 + 1)
                if c >= 2:
                    pe.wait_ge(S["xt32"], 4)
                for h in range(HEADS):
                    last = mm(bank[(6, 7, 2, 3)[c]][hi, h * DH:(h + 1) * DH], AT[lo, c * HEADS + h, hi],
                              Xf[lo, c * HEADS + h, :], start=True, stop=True)
                last.then_inc(S["t64_ps"], 1)
                if c:
                    x64(c - 1)
            x64(PC - 1)
            for c in range(PC):
                cs = slice(c * P, (c + 1) * P)
                if c:
                    pe.wait_ge(S["kqc"], 2 * PAIR_HEADS)
                    pe.wait_ge(S["st"], c)
                    for j in range(PAIR_HEADS):
                        last = mm(bank[0][:, j * P:(j + 1) * P], kp[:, j, 0, cs], St[:, c % 2, j, :], start=True, stop=True)
                    last.then_inc(S["ks_ps"], 1)
                    pe.wait_ge(S["rhs"], c)
                pe.wait_ge(S["xt64"], c + 1)
                if c:
                    pe.wait_ge(S["u"], c)
                for h in range(HEADS):
                    last = mm(bank[1][:, h * DH:(h + 1) * DH], XT[:, c * HEADS + h, :], vp[:, c, h * DH:(h + 1) * DH],
                              start=True, stop=True)
                last.then_inc(S["u_ps"], 1)
                pe.wait_ge(S["u"], c + 1)
                if c < PC - 1:
                    for j in range(PAIR_HEADS):
                        last = mm(bank[6][:, j * P:(j + 1) * P], kd[:, c, j * P:(j + 1) * P], U[:, c % 2, j * P:(j + 1) * P],
                                  start=True, stop=True)
                    last.then_inc(S["ku_ps"], 1)
                if c:
                    pe.wait_ge(S["o"], c)
                for j in range(PAIR_HEADS):
                    if c:
                        mm(bank[7][:, j * P:(j + 1) * P], kp[:, j, 1, cs], St[:, c % 2, j, :], start=True, stop=False,
                           skip_group_check=True)
                    for h in (2 * j, 2 * j + 1):
                        last = mm(bank[7][:, h * DH:(h + 1) * DH], MT[:, c * HEADS + h, :], U[:, c % 2, h * DH:(h + 1) * DH],
                                  start=(c == 0), stop=True, skip_group_check=True)
                last.then_inc(S["o_ps"], 1)

            pe.wait_ge(S["o"], PC)
            for c in range(NC):
                for p in range(PC):
                    last = mm(bank[c][:, :], permT[:, p, c * P:(c + 1) * P], oall[:, p, :], start=(p == 0), stop=(p == PC - 1))
                last.then_inc(S["core_ps"], 1)
            pe.wait_ge(S["core"], 2)
            to_fm(tm(T_a), bank[2], bank[3], "turned_ps")
            pe.wait_ge(S["turned"], 10)
            proj_tm(fm(F_a), U_DO, bank[4], bank[5], "fin_ps")

        @block.scalar
        def _(act):
            A = nc.scalar.activation

            def block_of(A, q, half):
                return A(*diagonal_block(q, half), ACT.Copy)

            def copy2(dst, b0, b1, ps, done, at=0):
                for c in range(2):
                    act.wait_ge(S[ps], at + c + 1)
                    A(dst[:, c * 512:(c + 1) * 512], (b0, b1)[c][:, :], ACT.Copy).then_inc(S[done], 1)

            def attention(l):
                for c in range(NC):
                    act.wait_ge(S["qsub"], l * 2 + c + 1)
                    A(tm(T_b)[:, c, :], tm(T_b)[:, c, :], ACT.Exp).then_inc(S["qexp"], 1)
                for k in range(FC):
                    act.wait_ge(S["kmx"], l * 2 + k // 2 + 1)
                    A(fm(F_c)[:, k, :], bank[4 + k // 2][:, (k % 2) * N:(k % 2 + 1) * N], ACT.Exp,
                      bias=kmx[:, k:k + 1], accum_out=ksum[:, k:k + 1]).then_inc(S["ek"], 1)
                copy2(T_d, bank[6], bank[7], "v_ps", "v", 2 * l)
                copy2(T_c, bank[4], bank[5], "ekt_ps", "ekt", 2 * l)
                copy2(F_b, bank[2], bank[3], "qT_ps", "qT", 2 * l)
                copy2(F_a, bank[4], bank[5], "oT_ps", "oT", 2 * l)

            act.wait_ge(S["cols_in"], 16)
            for k in range(FC):
                act.wait_ge(S["turned_ps"], k // 2 + 1)
                ins = A(fm(F_a)[:, k, :], bank[k // 2][:, (k % 2) * N:(k % 2 + 1) * N], ACT.Copy,
                        scale=cols[:, C_GAMMA + k:C_GAMMA + k + 1])
                if k % 2:
                    ins.then_inc(S["turned"], 1)
            attention(0)
            for l in range(2):
                copy2(F_b, bank[4], bank[5], "h1_ps", "h1T", 2 * l)
                for k in range(FC):
                    act.wait_ge(S["h2_ps"], 2 * l + k // 2 + 1)
                    ins = A(fm(F_c)[:, k, :], bank[6 + k // 2][:, (k % 2) * N:(k % 2 + 1) * N], ACT.Identity,
                            bias=cols[:, C_GCN + 4 * l + k:C_GCN + 4 * l + k + 1])
                    if k % 2:
                        ins.then_inc(S["h2T"], 1)
            copy2(F_a, bank[2], bank[3], "turned_ps", "turned", 2)
            act.wait_ge(S["logits"], 1)
            A(gl[:, 1, :, :], gl[:, 1, :, :], ACT.Exp).then_inc(S["lexp"], 1)
            for k in range(FC):
                act.wait_ge(S["hid_ps"], k // 2 + 1)
                A(fm(F_b)[:, k, :], bank[6 + k // 2][:, (k % 2) * N:(k % 2 + 1) * N], ACT.Relu,
                  bias=cols[:, C_B1 + k:C_B1 + k + 1]).then_inc(S["hid"], 1)
            act.wait_ge(S["hs_ps"], 1)
            A(hsT[:, :], bank[5][0:DH, 0:N], ACT.Relu, bias=cols[0:DH, C_BS1:C_BS1 + 1]).then_inc(S["act_step"], 1)
            act.wait_ge(S["act_step"], 1)
            A(hsT[:, :], hsT[:, :], ACT.Copy, scale=0.5).then_inc(S["hsT"], 1)
            act.wait_ge(S["combT_ps"], 1)
            A(combT[:, :], bank[4][0:E0 + 1, 0:N], ACT.Copy).then_inc(S["combT"], 1)
            copy2(F_a, bank[0], bank[1], "turned_ps", "turned", 4)
            attention_first = True
            copy2(T_a, bank[0], bank[1], "agg_ps", "aggT")
            attention(1)
            copy2(F_a, bank[0], bank[1], "turned_ps", "turned", 6)
            act.wait_ge(S["sm_ps"], 1)
            A(sm[:, :, :], bank[2][:, 0:40].rearrange("p (c e) -> p c e", c=NC), ACT.Copy).then_inc(S["sm"], 1)
            act.wait_ge(S["logits"], 2)
            A(gl[:, 1, :, 0:E1], gl[:, 1, :, 0:E1], ACT.Exp).then_inc(S["lexp"], 1)
            act.wait_ge(S["aabs"], 1)
            A(dl[:, 1, :, :], dl[:, 1, :, :], ACT.Exp, scale=-1.0).then_inc(S["aexp"], 1)
            act.wait_ge(S["rows_in"], 16)
            A(dl[:, 2, 0, :], rows[:, R_ALOG:R_ALOG + HEADS], ACT.Exp).then_inc(S["alog"], 1)
            A(dl[:, 3, :, :], sm[:, :, 4:12], ACT.Sigmoid).then_inc(S["beta"], 1)
            for b0, b1, dst, ps, done in ((3, 4, T_a, "dq_ps", "dq"), (5, 6, T_b, "dk_ps", "dk"),
                                          (7, 0, T_c, "dv_ps", "dv"), (1, 2, T_d, "dg_ps", "dg")):
                for c in range(NC):
                    act.wait_ge(S[ps], c + 1)
                    A(tm(dst)[:, c, :], bank[(b0, b1)[c]][:, :], ACT.Silu).then_inc(S[done], 1)
            act.wait_ge(S["squares"], 1)
            A(hmx[:, :], hmx[:, :], ACT.Sqrt).then_inc(S["roots"], 1)
            act.wait_ge(S["squares"], 2)
            A(hsum[:, :], hsum[:, :], ACT.Sqrt).then_inc(S["roots"], 1)
            for p in range(PC):
                act.wait_ge(S["vp_ps"], p + 1)
                A(vp[:, p, :], bank[4 + p][:, :], ACT.Copy).then_inc(S["vp"], 1)
            for n in range(8):
                act.wait_ge(S["kp_ps"], n + 1)
                A(kp[:, n % 4, n // 4, :], bank[(0, 1, 2, 4, 5, 6, 7, 0)[n]][:, :], ACT.Copy).then_inc(S["kp"], 1)
            for c in range(2):
                act.wait_ge(S["permT_ps"], c + 1)
                A(permT[:, 2 * c:2 * c + 2, :], bank[1 + c][:, :].rearrange("p (a n) -> p a n", a=2), ACT.Copy)\
                    .then_inc(S["permT"], 1)
            act.wait_ge(S["pv"], 1)
            A(a4[:, :, :], pv[:, :, 8:16], ACT.Exp).then_inc(S["act_step"], 1)
            act.wait_ge(S["act_step"], 2)
            A(a0[:, :, :], a4[:, :, :], ACT.Copy, scale=later[:, 0:1]).then_inc(S["a0"], 1)
            for b in range(2):
                act.wait_ge(S["ab_ps"], b + 1)
                A(F_a[:, b * 512:(b + 1) * 512], bank[6 + b][:, :], ACT.Copy).then_inc(S["ab"], 1)
            for j in range(PAIR_HEADS):
                act.wait_ge(S["crow_ps"], j + 1)
                A(crow(j), bank[(2, 3, 0, 1)[j]][:, :], ACT.Copy).then_inc(S["crow"], 1)
            act.wait_ge(S["xt_zero"], 1)
            act.wait_ge(S["xd_ps"], 1)
            for q in range(NB):
                block_of(A, q, 0).then_inc(S["xd_act"], 1)
            act.wait_ge(S["xf_ps"], 2)
            for q in range(NB - 1):
                A(*inverse_block(q, 1), ACT.Copy).then_inc(S["xf_act"], 1)
            for g_ in range(2):
                act.wait_ge(S["t32_ps"], g_ + 1)
                A(*t32_block(0, g_), ACT.Copy, scale=-1.0).then_inc(S["t32_act"], 1)
            for g_ in range(2):
                act.wait_ge(S["x32_ps"], g_ + 1)
                A(Xf[B:2 * B, g_ * HC // 2:(g_ + 1) * HC // 2, 0:B], bank[4 + g_][B:2 * B, :].rearrange("p (n s) -> p n s", s=B),
                  ACT.Copy).then_inc(S["x21"], 1)
            for c in range(PC):
                act.wait_ge(S["t64_ps"], c + 1)
                A(Xf[2 * B:P, c * HEADS:(c + 1) * HEADS, :],
                  bank[(6, 7, 2, 3)[c]][2 * B:P, :].rearrange("p (n s) -> p n s", n=HEADS), ACT.Copy, scale=-1.0)\
                    .then_inc(S["t64"], 1)
            for c in range(PC):
                act.wait_ge(S["u_ps"], c + 1)
                if c >= 2:
                    act.wait_ge(S["o_ps"], c - 1)
                A(U[:, c % 2, :], bank[1][:, :], ACT.Copy).then_inc(S["u"], 1)
                act.wait_ge(S["o_ps"], c + 1)
                A(oall[:, c, :], bank[7][:, :], ACT.Copy, scale=pv[:, c, 16:17]).then_inc(S["o"], 1)

            act.wait_ge(S["squares"], 3)
            A(hsum[:, :], hsum[:, :], ACT.Sqrt).then_inc(S["roots"], 1)
            copy2(F_a, bank[2], bank[3], "turned_ps", "turned", 8)

        @block.vector
        def _(dve):
            V = nc.vector
            count = [0]

            def link(ins):
                count[0] += 1
                ins.then_inc(S["dve_step"], 1)
                dve.wait_ge(S["dve_step"], count[0])

            def signal(ins, name, value):
                ins.then_inc(S[name], 1)
                dve.wait_ge(S[name], value)

            def norm(src, dst, n):
                for c in range(NC):
                    link(V.bn_stats(st[:, c, :], src(c)))
                for c in range(NC):
                    link(V.bn_aggr(mv[:, c, :], st[:, c, :]))
                signal(V.tensor_scalar(mv[:, :, 1], mv[:, :, 1], EPS, None, ALU.add), "var", n + 1)
                dve.wait_ge(S["rstd"], n + 1)
                for c in range(NC):
                    signal(V.tensor_scalar(dst[:, c, :], src(c), mv[:, c, 0:1], rstd[:, c, 0:1],
                                           ALU.subtract, ALU.mult), "normed", 2 * n + c + 1)

            def heads(ap):
                return ap.rearrange("p (h d) -> p h d", h=HEADS)

            def per_head(t, c):
                return t[:, c * HEADS:(c + 1) * HEADS].rearrange("p (h o) -> p h o", o=1).to_broadcast([P, HEADS, DH])

            def attention_soft(l, scale):
                for c in range(NC):
                    dve.wait_ge(S["q_ps"], l * 2 + c + 1)
                    link(V.tensor_reduce(hmx[:, c * HEADS:(c + 1) * HEADS], heads(bank[2 + c][:, :]), AX, ALU.max))
                    signal(V.tensor_tensor(heads(tm(T_b)[:, c, :]), heads(bank[2 + c][:, :]), per_head(hmx, c),
                                           ALU.subtract), "qsub", l * 2 + c + 1)
                for b in range(2):
                    dve.wait_ge(S["k_ps"], l * 2 + b + 1)
                    link(V.tensor_reduce(kmx[:, 2 * b:2 * b + 2], bank[4 + b][:, :].rearrange("p (a n) -> p a n", a=2),
                                         AX, ALU.max))
                    signal(V.tensor_scalar(kmx[:, 2 * b:2 * b + 2], kmx[:, 2 * b:2 * b + 2], -1.0, None, ALU.mult),
                           "kmx", l * 2 + b + 1)
                for c in range(NC):
                    s = hsum[:, c * HEADS:(c + 1) * HEADS]
                    dve.wait_ge(S["qexp"], l * 2 + c + 1)
                    link(V.tensor_reduce(s, heads(tm(T_b)[:, c, :]), AX, ALU.add))
                    link(V.reciprocal(s, s))
                    if scale != 1.0:
                        link(V.tensor_scalar(s, s, scale, None, ALU.mult))
                    signal(V.tensor_tensor(heads(tm(T_b)[:, c, :]), heads(tm(T_b)[:, c, :]), per_head(hsum, c),
                                           ALU.mult), "qs", l * 2 + c + 1)

            def attention_ctx(l):
                dve.wait_ge(S["ek"], l * 4 + 4)
                link(V.reciprocal(ksum[:, :], ksum[:, :]))
                dve.wait_ge(S["ctx_ps"], l * 1 + 1)
                for j in range(FC):
                    ins = V.scalar_tensor_tensor(out=ctxs[:, j, :], in0=bank[6][:, j * P:(j + 1) * P],
                                                 scalar=ksum[:, j:j + 1], in1=blockm[:, :], op0=ALU.mult, op1=ALU.mult)
                ins.then_inc(S["ctx"], 1)

            def ranks(lg, e):
                lj = lg.rearrange("p c (o j) -> p c o j", o=1).to_broadcast([P, NC, e, e])
                li = lg.rearrange("p c (i o) -> p c i o", o=1).to_broadcast([P, NC, e, e])
                gt, eq = rk[:, 0, :, 0:e, 0:e], rk[:, 1, :, 0:e, 0:e]
                link(V.tensor_tensor(gt, lj, li, ALU.is_gt))
                link(V.tensor_tensor(eq, lj, li, ALU.is_equal))
                for c in range(NC):
                    link(V.tensor_tensor(rk[:, 1, c, 0:e, 0:e], rk[:, 1, c, 0:e, 0:e], ltri[:, 0:e, 0:e], ALU.mult))
                link(V.tensor_tensor(gt, gt, eq, ALU.add))
                for c in range(NC):
                    link(V.tensor_reduce(sel[:, c, 0:e], rk[:, 0, c, 0:e, 0:e], AX, ALU.add))
                link(V.tensor_scalar(sel[:, :, 0:e], sel[:, :, 0:e], 1.5, None, ALU.is_lt))

            def over(t, e):
                return t.rearrange("p (c o) -> p c o", o=1).to_broadcast([P, NC, e])

            dve.wait_ge(S["x_in"], 16)
            norm(lambda c: xs[:, c, :], tm(T_n), 0)
            norm(lambda c: tm(T_n)[:, c, :], tm(T_a), 1)

            dve.wait_ge(S["edges_in"], 32)
            link(V.tensor_copy(edge_f[:, :, :], edge_i[:, :, :]))
            for part in range(3):
                link(V.tensor_copy(ewb[:, :, :], ew[:, :, :]))
                link(V.tensor_copy(ewp[:, part, :, :], ewb[:, :, :]))
                if part < 2:
                    link(V.tensor_tensor(ew[:, :, :], ew[:, :, :], ewp[:, part, :, :], ALU.subtract))

            attention_soft(0, DH ** -0.5)

            dve.wait_ge(S["iota"], 2)

            def onehots(t, half, own):
                V.tensor_scalar(src1h[:, half, :], iota_b[:, :], edge_f[:, 0, t], None, ALU.is_equal)
                for part in range(3):
                    for w in range(2):
                        ins = V.tensor_scalar(dst1h[:, half, part, w, :], iota_b[:, :], edge_f[:, 1, t],
                                              ewp[:, part, w, t], ALU.is_equal, ALU.mult)
                ins.then_inc(S["onehot"], 1)

            for half in range(2):
                onehots(slice(half, half + 1), half, None)
            with dve.Fori(1, ET // 2) as i:
                for half in range(2):
                    dve.wait_ge(S["adj_tile"], i * 2 - 1 + half)
                    onehots(bass.ds(i * 2 + half, 1), half, None)

            dve.wait_ge(S["consts"], 1)
            attention_ctx(0)
            for c in range(NC):
                dve.wait_ge(S["adj_ps"], c + 1)
                link(V.tensor_copy(A0[:, c, :], bank[c][:, 0:N]))
                signal(V.tensor_copy(A1[:, c, :], bank[c][:, N:2 * N]), "A1c", c + 1)
                link(V.tensor_reduce(deg[:, 0, c:c + 1], A0[:, c, :], AX, ALU.add))
            V.tensor_scalar(deg[:, 2, :], deg[:, 0, :], 0.0, None, ALU.is_gt).then_inc(S["A1"], 1)
            signal(V.tensor_scalar(deg[:, 1, :], deg[:, 0, :], 1e-38, None, ALU.max), "deg", 1)
            dve.wait_ge(S["A1"], 1)
            dve.wait_ge(S["degp"], 1)
            link(V.tensor_tensor(deg[:, 3, :], deg[:, 1, :], deg[:, 2, :], ALU.mult))
            for c in range(NC):
                ins = V.tensor_scalar(A0[:, c, :], A0[:, c, :], deg[:, 3, c:c + 1], None, ALU.mult)
            ins.then_inc(S["A0s"], 1)
            dve.wait_ge(S["AnT_ps"], 1)
            for c in range(NC):
                ins = V.tensor_scalar(AnT[:, c, :], bank[7][:, c * N:(c + 1) * N], deg[:, 3, c:c + 1], None, ALU.mult)
            ins.then_inc(S["AnT"], 1)

            dve.wait_ge(S["rows_in"], 16)
            dve.wait_ge(S["mix_ps"], 2)
            norm(lambda c: bank[2 + c][:, :], tm(T_a), 2)
            for c in range(NC):
                link(V.tensor_tensor(tm(T_a)[:, c, :], tm(T_a)[:, c, :], row(R_OG), ALU.mult))
                link(V.tensor_tensor(xs[:, c, :], xs[:, c, :], tm(T_a)[:, c, :], ALU.add))
            for l in range(2):
                for c in range(NC):
                    dve.wait_ge(S["h3_ps"], 2 * l + c + 1)
                    link(V.tensor_tensor(tm(T_c)[:, c, :], bank[c][:, :], row((R_MLP0, R_MLP1)[l]), ALU.add))
                    ins = V.scalar_tensor_tensor(out=tm(T_b)[:, c, :], in0=tm(T_c)[:, c, :], scalar=0.01,
                                                 in1=tm(T_c)[:, c, :], op0=ALU.mult, op1=ALU.max)
                    if l == 0:
                        ins.then_inc(S["h"], 1)
                    else:
                        link(ins)
                        link(V.tensor_tensor(xs[:, c, :], xs[:, c, :], tm(T_b)[:, c, :], ALU.add))

            norm(lambda c: xs[:, c, :], tm(T_a), 3)
            dve.wait_ge(S["gate_ps"], 1)
            g0, g1, g2 = gl[:, 0, :, :], gl[:, 1, :, :], gl[:, 2, :, :]
            bg = rows[:, R_BG:R_BG + E0].rearrange("p (o e) -> p o e", o=1).to_broadcast([P, NC, E0])
            link(V.tensor_tensor(g0, bank[4][:, 0:2 * E0].rearrange("p (c e) -> p c e", c=NC), bg, ALU.add))
            link(V.tensor_reduce(gmx[:, 0, :], g0, AX, ALU.max))
            signal(V.tensor_tensor(g1, g0, over(gmx[:, 0, :], E0), ALU.subtract), "logits", 1)
            ranks(g0, E0)
            dve.wait_ge(S["lexp"], 1)
            link(V.tensor_tensor(g1, g1, sel[:, :, 0:E0], ALU.mult))
            link(V.tensor_reduce(gmx[:, 1, :], g1, AX, ALU.add))
            link(V.reciprocal(gmx[:, 1, :], gmx[:, 1, :]))
            signal(V.tensor_tensor(comb[:, :, 0:E0], g1, over(gmx[:, 1, :], E0), ALU.mult), "comb", 1)
            dve.wait_ge(S["hid"], 4)
            for b in range(2):
                dve.wait_ge(S["combB_ps"], b + 1)
                V.tensor_tensor(F_c[:, b * 512:(b + 1) * 512], F_b[:, b * 512:(b + 1) * 512], bank[b][:, :],
                                ALU.mult).then_inc(S["hw"], 1)
            for c in range(NC):
                dve.wait_ge(S["y_ps"], c + 1)
                link(V.tensor_tensor(xs[:, c, :], xs[:, c, :], bank[2 + c][:, :], ALU.add))

            norm(lambda c: xs[:, c, :], tm(T_n), 4)
            attention_soft(1, 1.0)
            attention_ctx(1)
            link(V.tensor_tensor(row(R_B1), row(R_B1), row(R_BOUT), ALU.add))
            for c in range(NC):
                link(V.tensor_tensor(xs[:, c, :], xs[:, c, :], row(R_B1), ALU.add))
                dve.wait_ge(S["mix_ps"], 2 + c + 1)
                link(V.tensor_tensor(xs[:, c, :], xs[:, c, :], bank[2 + c][:, :], ALU.add))
            norm(lambda c: xs[:, c, :], tm(T_n), 5)

            dve.wait_ge(S["sm"], 1)
            s0, s1, w = gl[:, 0, :, 0:E1], gl[:, 1, :, 0:E1], gl[:, 2, :, 0:E1]
            link(V.tensor_reduce(gmx[:, 0, :], sm[:, :, 0:E1], AX, ALU.max))
            signal(V.tensor_tensor(s1, sm[:, :, 0:E1], over(gmx[:, 0, :], E1), ALU.subtract), "logits", 2)
            x_a, u_a, ea, beta = dl[:, 0, :, :], dl[:, 1, :, :], dl[:, 2, 0, :], dl[:, 3, :, :]
            s_a, s2, pl, sp_ = dl[:, 4, :, :], dl[:, 5, :, :], dl[:, 6, :, :], dl[:, 7, :, :]
            dtb = rows[:, R_DT:R_DT + HEADS].rearrange("p (o e) -> p o e", o=1).to_broadcast([P, NC, HEADS])
            link(V.tensor_tensor(x_a, sm[:, :, 12:20], dtb, ALU.add))
            signal(V.scalar_tensor_tensor(out=u_a, in0=x_a, scalar=-1.0, in1=x_a, op0=ALU.mult, op1=ALU.max), "aabs", 1)
            dve.wait_ge(S["lexp"], 2)
            link(V.tensor_reduce(gmx[:, 1, :], s1, AX, ALU.add))
            link(V.reciprocal(gmx[:, 1, :], gmx[:, 1, :]))
            link(V.tensor_tensor(s0, s1, over(gmx[:, 1, :], E1), ALU.mult))
            ranks(s0, E1)
            link(V.memset(pre[:, :, 0:1], 0.0))
            for e in range(1, E1):
                ins = V.tensor_tensor(pre[:, :, e], pre[:, :, e - 1], sel[:, :, e - 1], ALU.add)
                if e < E1 - 1:
                    link(ins)
            signal(ins, "sel", 1)
            link(V.tensor_tensor(w, s0, sel[:, :, 0:E1], ALU.mult))
            link(V.tensor_reduce(gmx[:, 1, :], w, AX, ALU.add))
            link(V.reciprocal(gmx[:, 1, :], gmx[:, 1, :]))
            link(V.tensor_tensor(w, w, over(gmx[:, 1, :], E1), ALU.mult))
            link(V.tensor_scalar(s1, w, 0.0, None, ALU.is_gt))
            dve.wait_ge(S["aexp"], 1)
            link(V.tensor_scalar(s_a, u_a, 2.0, None, ALU.add))
            link(V.reciprocal(s_a, s_a))
            link(V.tensor_tensor(s_a, s_a, u_a, ALU.mult))
            link(V.tensor_tensor(s2, s_a, s_a, ALU.mult))
            link(V.tensor_scalar(pl, s2, 1.0 / 17, None, ALU.mult))
            for k in range(15, 1, -2):
                link(V.scalar_tensor_tensor(out=pl, in0=pl, scalar=1.0 / k, in1=s2, op0=ALU.add, op1=ALU.mult))
            link(V.scalar_tensor_tensor(out=pl, in0=pl, scalar=1.0, in1=s_a, op0=ALU.add, op1=ALU.mult))
            link(V.tensor_scalar(sp_, x_a, 0.0, None, ALU.max))
            link(V.scalar_tensor_tensor(out=sp_, in0=pl, scalar=2.0, in1=sp_, op0=ALU.mult, op1=ALU.add))
            dve.wait_ge(S["alog"], 1)
            eab = ea.rearrange("p (o e) -> p o e", o=1).to_broadcast([P, NC, HEADS])
            link(V.scalar_tensor_tensor(out=sp_, in0=sp_, scalar=-1.0, in1=eab, op0=ALU.mult, op1=ALU.mult))
            link(V.tensor_scalar(sp_, sp_, -200.0, None, ALU.max))
            dve.wait_ge(S["beta"], 1)
            for c in range(NC):
                on = s1[:, c, :].rearrange("p (e o) -> p e o", o=1).to_broadcast([P, E1, HEADS])
                bb = beta[:, c, :].rearrange("p (o h) -> p o h", o=1).to_broadcast([P, E1, HEADS])
                gg = sp_[:, c, :].rearrange("p (o h) -> p o h", o=1).to_broadcast([P, E1, HEADS])
                link(V.tensor_tensor(vals[:, c, :, 0:8], bb, on, ALU.mult))
                link(V.tensor_tensor(vals[:, c, :, 8:16], gg, on, ALU.mult))
            link(V.tensor_copy(vals[:, :, :, 16], w))
            dve.wait_ge(S["pos_ps"], 1)
            p3 = bank[3][:, 0:2 * E1].rearrange("p (c e) -> p c e", c=NC)
            link(V.scalar_tensor_tensor(out=posm[:, :, :], in0=p3, scalar=1.0, in1=sel[:, :, 0:E1], op0=ALU.add, op1=ALU.mult))
            link(V.tensor_scalar(posm[:, :, :], posm[:, :, :], -1.0, None, ALU.add))
            for p in range(PC):
                link(V.tensor_scalar(ge[:, p, 0:E1], bank[3][:, 2 * E1:3 * E1], idx[:, p:p + 1], None, ALU.is_le))
            for p in range(PC):
                link(V.tensor_scalar(first[:, p, :], bank[3][:, 2 * E1:3 * E1], idx[:, p:p + 1], -200.0,
                                     ALU.is_equal, ALU.mult))
            link(V.tensor_reduce(forget[:, :], first[:, :, :], AX, ALU.min))
            link(V.tensor_tensor(oh[:, :, :], ge[:, :, 0:E1], ge[:, :, 1:E1 + 1], ALU.subtract))
            for e in range(E1):
                for c in range(NC):
                    if e == 0:
                        ins = V.tensor_scalar(perm[:, c, :], iota_f[:, :], posm[:, c, 0:1], None, ALU.is_equal)
                    else:
                        ins = V.scalar_tensor_tensor(out=perm[:, c, :], in0=iota_f[:, :], scalar=posm[:, c, e:e + 1],
                                                     in1=perm[:, c, :], op0=ALU.is_equal, op1=ALU.add)
                    if (e, c) != (E1 - 1, NC - 1):
                        link(ins)
            signal(ins, "perm", 1)
            for t, ss, got, turn, out, scale in ((T_b, hmx, "dk", 1, "kn", 1.0),
                                                    (T_a, hsum, "dq", 2, "qn", DH ** -0.5)):
                for c in range(NC):
                    dve.wait_ge(S[got], c + 1)
                    link(V.tensor_tensor(F_b[:, c * D:(c + 1) * D], tm(t)[:, c, :], tm(t)[:, c, :], ALU.mult))
                    link(V.tensor_reduce(ss[:, c * HEADS:(c + 1) * HEADS], heads(F_b[:, c * D:(c + 1) * D]), AX, ALU.add))
                signal(V.tensor_scalar(ss[:, :], ss[:, :], 1e-6, None, ALU.add), "squares", turn)
            for t, ss, got, turn, out, scale in ((T_b, hmx, "dk", 1, "kn", 1.0),
                                                    (T_a, hsum, "dq", 2, "qn", DH ** -0.5)):
                dve.wait_ge(S["roots"], turn)
                link(V.reciprocal(ss[:, :], ss[:, :]))
                if scale != 1.0:
                    link(V.tensor_scalar(ss[:, :], ss[:, :], scale, None, ALU.mult))
                for c in range(NC):
                    V.tensor_tensor(heads(tm(t)[:, c, :]), heads(tm(t)[:, c, :]), per_head(ss, c), ALU.mult)\
                        .then_inc(S[out], 1)
            dve.wait_ge(S["vals_ps"], 1)
            vps = bank[3][:, 0:PC * 68].rearrange("p (a e v) -> p a e v", a=PC, e=E1)
            for p in range(PC):
                link(V.tensor_tensor(vmask[:, p, :, :], vps[:, p, :, :],
                                     oh[:, p, :].rearrange("p (e o) -> p e o", o=1).to_broadcast([P, E1, 17]), ALU.mult))
            for p in range(PC):
                ins = V.tensor_reduce(pv[:, p, :], vmask[:, p, :, :].rearrange("p e v -> p v e"), AX, ALU.add)
            link(ins)
            for p in range(PC):
                ins = V.tensor_scalar(pv[:, p, 8:16], pv[:, p, 8:16], forget[:, p:p + 1], None, ALU.add)
            signal(ins, "pv", 1)

            dve.wait_ge(S["aT_ps"], 1)
            for c in range(PC):
                ins = V.tensor_tensor_scan(cT[:, c * P:(c + 1) * P], bank[6][0:HEADS, c * P:(c + 1) * P],
                                           identz[0:HEADS, P:2 * P], 1.0, ALU.mult, ALU.add)
            ins.then_inc(S["cT"], 1)
            for h in range(HEADS):
                dve.wait_ge(S["arow"], h + 1)
                dve.wait_ge(S["zb"], h + 1)
                d4 = dec[:, h % 2, :, :]
                signal(V.tensor_tensor_scan(F_b[:, (h % 2) * PAIRS:(h % 2 + 1) * PAIRS], bank[h % 2][:, :],
                                            T_n[:, (h % 2) * PAIRS:(h % 2 + 1) * PAIRS], 0.0, ALU.mult, ALU.add), "scan", h + 1)
                for z, ps, out, done in ((0, "kk_ps", AT, "at"), (1, "qk_ps", MT, "mt")):
                    dve.wait_ge(S[ps], h + 1)
                    V.tensor_tensor(out.rearrange("p (c h) t -> p c h t", c=PC)[:, :, h, :], d4,
                                    bank[2 + 2 * z + h % 2][:, :].rearrange("p (c t) -> p c t", c=PC), ALU.mult)\
                        .then_inc(S[done], 1)
                ins = V.tensor_copy(dbeta[:, :, h], d4[:, :, P - 1])
            link(ins)
            for c in range(PC):
                dve.wait_ge(S["ktm_ps"], c + 1)
                V.tensor_tensor(heads(kd[:, c, :]), heads(bank[(2, 3, 0, 1)[c]][:, :]),
                                dbeta[:, c, :].rearrange("p (h o) -> p h o", o=1).to_broadcast([P, HEADS, DH]), ALU.mult)\
                    .then_inc(S["kd"], 1)
            dve.wait_ge(S["ab"], 2)
            dve.wait_ge(S["xb0"], 1)
            for s_ in range(B - 1):
                rest, w_ = B - 1 - s_, s_ + 1
                part = prodb[:, 0:rest * w_].rearrange("p (t c) -> p t c", t=rest)
                link(V.tensor_tensor(part, Ab[:, s_ + 1:B, s_:s_ + 1].to_broadcast([P, rest, w_]),
                                     Xb[:, s_:s_ + 1, 0:w_].to_broadcast([P, rest, w_]), ALU.mult))
                signal(V.tensor_tensor(Xb[:, s_ + 1:B, 0:w_], Xb[:, s_ + 1:B, 0:w_], part, ALU.subtract), "xrow", s_ + 1)
            dve.wait_ge(S["xt_zero"], 1)
            dve.wait_ge(S["xd_ps"], 2)
            for q in range(NB):
                V.tensor_copy(*diagonal_block(q, 1)).then_inc(S["xd_dve"], 1)
            dve.wait_ge(S["xf_ps"], 1)
            for q in range(NB - 1):
                V.tensor_copy(*inverse_block(q, 0)).then_inc(S["xf_dve"], 1)
            for g_ in range(2):
                dve.wait_ge(S["t32_ps"], g_ + 1)
                V.tensor_scalar(*t32_block(2, g_), -1.0, None, ALU.mult).then_inc(S["t32_dve"], 1)
            for g_ in range(2):
                dve.wait_ge(S["x32_ps"], g_ + 1)
                for qe in (0, 2):
                    re, ro = slice(qe * B, (qe + 1) * B), slice((qe + 1) * B, (qe + 2) * B)
                    V.tensor_copy(XT[re, g_ * HC // 2:(g_ + 1) * HC // 2, ro],
                                  bank[2 + g_][re, :].rearrange("p (n s) -> p n s", s=B)).then_inc(S["xt32"], 1)
            for c in range(PC):
                dve.wait_ge(S["x64_ps"], c + 1)
                V.tensor_copy(XT[0:2 * B, c * HEADS:(c + 1) * HEADS, 2 * B:P],
                              bank[4 + c % 2][0:2 * B, :].rearrange("p (n s) -> p n s", n=HEADS)).then_inc(S["xt64"], 1)
            dve.wait_ge(S["st_zero"], 1)
            dve.wait_ge(S["cend"], 2)
            for c in range(PC):
                if c:
                    dve.wait_ge(S["ks_ps"], c)
                    V.tensor_tensor(vp[:, c, :], vp[:, c, :], bank[0][:, :], ALU.subtract).then_inc(S["rhs"], 1)
                if c == PC - 1:
                    break
                new = St[:, (c + 1) % 2, :, :]
                if c:
                    dve.wait_ge(S["o_ps"], c)
                    link(V.tensor_tensor(new, St[:, c % 2, :, :],
                                         cend[:, c, :].rearrange("p (j o) -> p j o", o=1).to_broadcast([P, PAIR_HEADS, P]),
                                         ALU.mult))
                dve.wait_ge(S["ku_ps"], c + 1)
                for hh in range(2):
                    r = slice(hh * DH, (hh + 1) * DH)
                    add = bank[6][r, :].rearrange("p (j v) -> p j v", j=PAIR_HEADS)[:, :, r]
                    ins = V.tensor_tensor(new[r, :, r], new[r, :, r], add, ALU.add)
                signal(ins, "st", c + 1)

            for c in range(NC):
                dve.wait_ge(S["core_ps"], c + 1)
                link(V.tensor_copy(tm(T_a)[:, c, :], bank[c][:, :]))
                link(V.tensor_tensor(F_b[:, c * D:(c + 1) * D], tm(T_a)[:, c, :], tm(T_a)[:, c, :], ALU.mult))
                link(V.tensor_reduce(hsum[:, c * HEADS:(c + 1) * HEADS], heads(F_b[:, c * D:(c + 1) * D]), AX, ALU.add))
            signal(V.tensor_scalar(hsum[:, :], hsum[:, :], 1.0 / DH, EPS, ALU.mult, ALU.add), "squares", 3)
            for c in range(NC):
                link(V.tensor_tensor(tm(T_d)[:, c, :], tm(T_d)[:, c, :], row(R_ON), ALU.mult))
                link(V.tensor_tensor(tm(T_a)[:, c, :], tm(T_a)[:, c, :], tm(T_d)[:, c, :], ALU.mult))
            dve.wait_ge(S["roots"], 3)
            link(V.reciprocal(hsum[:, :], hsum[:, :]))
            for c in range(NC):
                V.tensor_tensor(heads(tm(T_a)[:, c, :]), heads(tm(T_a)[:, c, :]), per_head(hsum, c), ALU.mult)\
                    .then_inc(S["core"], 1)
            for c in range(NC):
                dve.wait_ge(S["fin_ps"], c + 1)
                V.tensor_tensor(xs[:, c, :], xs[:, c, :], bank[4 + c][:, :], ALU.add).then_inc(S["fin"], 1)


def kernel(**inputs):
    import numpy as np
    import concourse.bacc as bacc
    from concourse import mybir as mb
    from concourse.bass_utils import run_bass_kernel_spmd

    g = {k: np.asarray(v) for k, v in inputs.items()}

    def unit(w):
        return w.reshape(FC, P, D).transpose(1, 0, 2).reshape(P, UNIT)

    q0, k0, v0 = (g["L0_mix_w_qkv"][i * D:(i + 1) * D].T for i in range(3))
    q1, k1, v1 = (g["L1_mix_Wqkv"][i * D:(i + 1) * D].T for i in range(3))
    weights = [q0, k0, v0, g["L0_mix_w_out"].T, g["L0_gnn_W_gcn"][0], g["L0_gnn_W_mlp"][0], g["L0_gnn_W_gcn"][1],
               g["L0_gnn_W_mlp"][1], g["L0_ffn_W1"].transpose(1, 0, 2).reshape(D, D), g["L0_ffn_W2"].reshape(D, D),
               q1, k1, v1, g["L1_gnn_W"].T, g["L1_mix_Wout"].T, g["L1_ffn_Wq"], g["L1_ffn_Wk"], g["L1_ffn_Wv"],
               g["L1_ffn_Wg"], g["L1_ffn_Wo"]]
    rows = np.concatenate([g["L0_gnn_b_mlp"][0], g["L0_gnn_b_mlp"][1], g["L0_mix_out_gamma"], g["L1_gnn_b"],
                           g["L1_mix_bout"], np.tile(g["L1_ffn_o_norm_weight"], HEADS), g["L0_ffn_bg"],
                           g["L1_ffn_A_log"], g["L1_ffn_dt_bias"]])[None]
    cols = np.concatenate([g["L0_gnn_b_gcn"].reshape(8, P).T, g["L0_mix_norm_gamma"].reshape(4, P).T,
                           g["L0_ffn_b1"].reshape(4, P).T, np.tile(g["L0_ffn_bs1"], 2).reshape(P, 1)], axis=1)
    gw = np.concatenate([g["L0_ffn_Wg"], g["L0_ffn_Ws1"], g["L1_ffn_Wgate"], g["L1_ffn_Wb"], g["L1_ffn_Wa"]], axis=1)
    arrays = {
        "x": g["x"].reshape(NC, P, D).transpose(1, 0, 2),
        "edges": np.stack([g["src"], g["dst"]]).reshape(2, ET, P).transpose(2, 0, 1),
        "edge_weights": np.stack([g["edge_weight"], g["edge_weight1"][:, 0]]).reshape(2, ET, P).transpose(2, 0, 1),
        "weights": np.stack([unit(w) for w in weights]),
        "rows": rows,
        "cols": cols,
        "gw": gw.reshape(FC, P, GW).transpose(1, 0, 2),
        "b29": np.concatenate([g["L0_ffn_b2"], g["L0_ffn_bs2"][None]]),
        "ws2": g["L0_ffn_Ws2"],
    }
    nc = bacc.Bacc("TRN2", target_bir_lowering=False, num_devices=1)
    arrays = {"in_" + k: np.ascontiguousarray(v) for k, v in arrays.items()}
    args = [nc.dram_tensor(k, v.shape, mb.dt.from_np(v.dtype), kind="ExternalInput").ap() for k, v in arrays.items()]
    out = nc.dram_tensor("out", (P, NC, D), mb.dt.float32, kind="ExternalOutput").ap()
    build(nc, *args, out)
    r = run_bass_kernel_spmd(nc, [arrays], core_ids=[0])
    return np.asarray(r.results[0]["out"]).transpose(1, 0, 2).reshape(N, D)
```

```python
from contextlib import ExitStack

import concourse.bass as bass
from concourse import mybir

P = 128
N = 256
D = 512
NC = N // P
FC = D // P
HEADS = 8
DH = D // HEADS
UNIT = FC * D
SLOTS = 8
EDGES = 4352
ET = EDGES // P
BUFS = 3
LAST = ET - ET // BUFS * BUFS
E0 = 8
E1 = 4
PAIRS = 2 * N
PC = PAIRS // P
B = 32
NB = P // B
HC = PC * HEADS
PAIR_HEADS = HEADS // 2
EPS = 1e-5

F32 = mybir.dt.float32
BF16 = mybir.dt.bfloat16
F32R = mybir.dt.float32r
I32 = mybir.dt.int32
ALU = mybir.AluOpType
ACT = mybir.ActivationFunctionType
AX = mybir.AxisListType.X

(U_Q0, U_K0, U_V0, U_O0, U_GCN0, U_MLP0, U_GCN1, U_MLP1, U_W1, U_W2,
 U_Q1, U_K1, U_V1, U_AGG, U_O1, U_DQ, U_DK, U_DV, U_DG, U_DO) = range(20)
UNITS = 20
(R_MLP0, R_MLP1, R_OG, R_B1, R_BOUT, R_ON) = range(6)
ROWS = 6 * D
R_BG, R_ALOG, R_DT = ROWS, ROWS + 8, ROWS + 16
ROWS_ALL = ROWS + 24
C_GCN, C_GAMMA, C_B1, C_BS1 = 0, 8, 12, 16
COLS = 17
G_WG, G_WS1, G_SM = 0, 8, 72
GW = 92


def build(nc, d_x, d_edge, d_ew, d_w, d_rows, d_cols, d_gw, d_b29, d_ws2, d_out):
    with ExitStack() as ctx:
        def sb(name, shape, dt=F32):
            return ctx.enter_context(nc.sbuf_tensor(name, shape, dt))

        def sem(name):
            return ctx.enter_context(nc.semaphore(name))

        class Sems:
            def __init__(self):
                self.made = {}

            def __getitem__(self, name):
                if name not in self.made:
                    self.made[name] = sem("s_" + name)
                return self.made[name]

        S = Sems()

        bank = [ctx.enter_context(nc.psum_tensor(f"bank{i}", [P, 512], F32)) for i in range(8)]

        ring = sb("ring", [P, SLOTS * UNIT])
        xs = sb("xs", [P, NC, D])
        T_n = sb("T_n", [P, NC * D])
        T_a = sb("T_a", [P, NC * D])
        T_b = sb("T_b", [P, NC * D])
        T_c = sb("T_c", [P, NC * D])
        T_d = sb("T_d", [P, NC * D])
        F_a = sb("F_a", [P, FC * N])
        F_b = sb("F_b", [P, FC * N])
        F_c = sb("F_c", [P, FC * N])
        tm = lambda t: t[:, :].rearrange("p (c f) -> p c f", c=NC)
        fm = lambda t: t[:, :].rearrange("p (k n) -> p k n", k=FC)
        tm2 = lambda ap: ap.rearrange("p (c f) -> p c f", c=NC)
        rows = sb("rows", [P, ROWS_ALL])
        row = lambda r: rows[:, r * D:(r + 1) * D]
        cols = sb("cols", [P, COLS])
        gw = sb("gw", [P, FC, GW])
        b29 = sb("b29", [E0 + 1, D])
        ws2 = sb("ws2", [DH, D])
        edge_i = sb("edge_i", [P, 2, ET], I32)
        edge_f = sb("edge_f", [P, 2, ET])
        ew = sb("ew", [P, 2, ET])
        ewh = sb("ewh", [P, 2, ET], F32R)
        ewl = sb("ewl", [P, 2, ET])
        iota_b = sb("iota_b", [P, N], BF16)
        iota_f = sb("iota_f", [P, PAIRS])
        ident = sb("ident", [P, P])
        identz = sb("identz", [P, PAIRS])
        ones = sb("ones", [P, P])
        tri = sb("tri", [P, P])
        zer = sb("zer", [P, 512], BF16)
        dst1 = sb("dst1", [P, BUFS, N], BF16)
        split = sb("split", [P, 4, NC * D], F32R)
        src1h = split[:, 0, 0:BUFS * N].rearrange("p (b n) -> p b n", b=BUFS)
        dst1h = split[:, 1:1 + BUFS, :].rearrange("p b (s w n) -> p b s w n", s=2, w=2)
        A0 = sb("A0", [P, NC, N])
        A1 = sb("A1", [P, NC, N])
        AnT = sb("AnT", [P, NC, N])
        ctxs = sb("ctxs", [P, FC, P])
        blockm = sb("blockm", [P, P])
        st = sb("st", [P, NC, 6])
        mv = sb("mv", [P, NC, 2])
        rstd = sb("rstd", [P, NC, 1])
        rstd2 = sb("rstd2", [P, NC, 1])
        junk = sb("junk", [P, 5])
        mhalf = sb("mhalf", [P, 2])
        deg = sb("deg", [P, 4, NC])
        hmx = sb("hmx", [P, NC * HEADS])
        hsum = sb("hsum", [P, NC * HEADS])
        kmx = sb("kmx", [P, FC])
        ksum = sb("ksum", [P, FC])
        ltri = sb("ltri", [P, E0, E0])
        rk = sb("rk", [P, 2, NC, E0, E0])
        gl = sb("gl", [P, 4, NC, E0])
        sel = sb("sel", [P, NC, E0])
        gmx = sb("gmx", [P, 2, NC])
        comb = sb("comb", [P, NC, E0 + 1])
        combT = sb("combT", [E0 + 1, N])
        spread = sb("spread", [E0 + 1, FC, P])
        hsT = sb("hsT", [DH, N])
        sm = sb("sm", [P, NC, 20])
        dl = sb("dl", [P, 8, NC, HEADS])
        vals = sb("vals", [P, NC, E1, 17])
        pre = sb("pre", [P, NC, E1])
        posm = sb("posm", [P, NC, E1])
        idx = sb("idx", [P, PC])
        ge = sb("ge", [P, PC, E1 + 1])
        oh = sb("oh", [P, PC, E1])
        first = sb("first", [P, PC, E1])
        forget = sb("forget", [P, PC])
        vmask = sb("vmask", [P, PC, E1, 17])
        pv = sb("pv", [P, PC, 17])
        perm = sb("perm", [P, NC, PAIRS], F32R)
        permf = perm[:, :, :].bitcast(F32)
        kp = sb("kp", [P, FC, 2, PAIRS])
        vp = sb("vp", [P, PC, D])
        a4 = sb("a4", [P, PC, HEADS])
        a0 = sb("a0", [P, PC, HEADS])
        later = sb("later", [P, 1])
        dbeta = sb("dbeta", [P, PC, HEADS])
        cT = sb("cT", [HEADS, PAIRS])
        cend = sb("cend", [P, PC, PAIR_HEADS])
        kd = sb("kd", [P, PC, D])
        Xf = sb("Xf", [P, HC, 2 * B])

        def wslot(u):
            s = u % SLOTS
            return ring[:, s * UNIT:(s + 1) * UNIT].rearrange("p (k o) -> p k o", k=FC)

        XT = ring[:, 0:2 * UNIT].rearrange("p (n t) -> p n t", n=HC)
        kz = ring[:, 0:2 * UNIT].rearrange("p (h t) -> p h t", h=HEADS)
        AT = ring[:, 4 * UNIT:6 * UNIT].rearrange("p (n t) -> p n t", n=HC)
        MT = ring[:, 6 * UNIT:8 * UNIT].rearrange("p (h t) -> p h t", h=HEADS)
        zb = T_n[:, :].rearrange("p (two c t) -> p two c t", two=2, c=PC)
        Ab = F_c[:, :].rearrange("p (t s) -> p t s", t=B)
        Xb = T_n[:, :].rearrange("p (t s) -> p t s", t=B)
        prodb = F_b[:, 0:B * B // 4]
        T32 = F_b[:, :].rearrange("p (n s) -> p n s", n=HC)
        U = F_c[:, :].rearrange("p (two f) -> p two f", two=2)
        St = T_a[:, :].rearrange("p (two j v) -> p two j v", two=2, j=PAIR_HEADS)
        qkb = (F_b[:, PAIRS:2 * PAIRS], ctxs[:, :, :].rearrange("p k t -> p (k t)"))
        oparts = split[:, 0:2, :].rearrange("p s (two f) -> p s two f", two=2)
        crow = lambda j: (T_b, T_c)[j // 2][:, (j % 2) * PAIRS:(j % 2 + 1) * PAIRS]

        used = {U_Q0: ("q_ps", 2), U_K0: ("k_ps", 2), U_V0: ("v_ps", 2), U_O0: ("mix_ps", 2),
                U_GCN0: ("h2_ps", 2), U_MLP0: ("h3_ps", 2), U_GCN1: ("h2_ps", 4), U_MLP1: ("h3_ps", 4),
                U_W1: ("hid_ps", 2), U_W2: ("y_ps", 2), U_Q1: ("q_ps", 4), U_K1: ("k_ps", 4)}

        block = ctx.enter_context(nc.Block())

        @block.sync
        def _(sp):
            sp.dma_start(edge_i[:, :, :], d_edge).then_inc(S["edges_in"], 16)
            sp.dma_start(ew[:, :, :], d_ew).then_inc(S["edges_in"], 16)
            sp.dma_start(xs[:, :, :], d_x).then_inc(S["x_in"], 16)
            sp.dma_start(cols[:, :], d_cols).then_inc(S["cols_in"], 16)
            for u in range(3):
                sp.dma_start(ring[:, u * UNIT:(u + 1) * UNIT], d_w[u]).then_inc(S["w%d" % (u % SLOTS)], 16)
            sp.dma_start(rows[:, :], d_rows[0, :].partition_broadcast(P)).then_inc(S["rows_in"], 16)
            sp.dma_start(gw[:, :, :], d_gw).then_inc(S["gw_in"], 16)
            sp.dma_start(b29[:, :], d_b29).then_inc(S["ffn_in"], 16)
            sp.dma_start(ws2[:, :], d_ws2).then_inc(S["ffn_in"], 16)
            for u in range(3, UNITS):
                if u >= SLOTS:
                    sp.wait_ge(S[used[u - SLOTS][0]], used[u - SLOTS][1])
                s = u % SLOTS
                sp.dma_start(ring[:, s * UNIT:(s + 1) * UNIT], d_w[u]).then_inc(S["w%d" % (u % SLOTS)], 16)
            for c in range(NC):
                sp.wait_ge(S["fin"], c + 1)
                sp.dma_start(d_out[:, c, :], xs[:, c, :]).then_inc(S["out"], 16)
            sp.wait_ge(S["out"], 16 * NC)

        KP_BANKS = (1, 4, 5, 6, 2, 7, 0, 1)
        VP_BANKS = (4, 5, 6, 2)

        def permT(p):
            return split[:, 2, p * N:(p + 1) * N]

        def diagonal_block(q, half):
            r = slice(q * B, (q + 1) * B)
            return (XT[r, :, q * B + 16 * half:q * B + 16 * half + 16],
                    bank[4 + half][r, :].rearrange("p (t n) -> p n t", n=HC))

        def inverse_block(q, half):
            r, at = slice(q * B, (q + 1) * B), (q % 2) * B + 16 * half
            return Xf[r, :, at:at + 16], bank[(6, 2)[q % 2] + half][r, :].rearrange("p (s n) -> p n s", n=HC)

        def t32_block(qe, g_):
            ro = slice((qe + 1) * B, (qe + 2) * B)
            return (T32[ro, g_ * HC // 2:(g_ + 1) * HC // 2, :], bank[g_][ro, :].rearrange("p (n s) -> p n s", s=B))

        @block.gpsimd
        def _(g):
            count = [0]

            def link(ins):
                count[0] += 1
                ins.then_inc(S["pool_step"], 1)
                g.wait_ge(S["pool_step"], count[0])

            g.memset(mhalf[:, :], -0.5).then_inc(S["made"], 1)
            g.memset(zer[:, :], 0.0).then_inc(S["made"], 1)
            g.iota(iota_f[:, :], [[1, PAIRS]], base=0, channel_multiplier=0,
                   allow_small_or_imprecise_dtypes=True).then_inc(S["made"], 1)
            g.wait_ge(S["made"], 3)
            g.tensor_copy(iota_b[:, :], iota_f[:, 0:N]).then_inc(S["made"], 1)
            link(g.memset(identz[:, :], 0.0))
            link(g.affine_select(out=identz[:, 0:P], in_=identz[:, 0:P], compare_op=ALU.not_equal, fill=1.0,
                                 base=0, pattern=[[-1, P]], channel_multiplier=1))
            g.tensor_copy(ident[:, :], identz[:, 0:P]).then_inc(S["made"], 1)

            def power(n):
                g.wait_ge(S["made"], 1)
                for c in range(NC):
                    g.wait_ge(S["var"], NC * n + c + 1)
                    g.tensor_tensor((rstd2 if n == 1 else rstd)[:, c, :], mv[:, c, 1:2], mhalf[:, 0:1], ALU.pow)\
                        .then_inc(S["rstd"], 1)

            g.wait_ge(S["parts"], 1)

            def targets_low(t, half, tile):
                g.wait_ge(S["dst1"], tile + 1)
                g.tensor_tensor(dst1h[:, half, 1, 1, :], dst1[:, half, :], ewl[:, 1, t].to_broadcast([P, N]), ALU.mult)\
                    .then_inc(S["dst_pool"], 1)

            for b in range(BUFS):
                targets_low(slice(b, b + 1), b, b)
            power(0)
            power(1)
            link(g.memset(ones[:, :], 1.0))
            link(g.memset(blockm[:, :], 0.0))
            link(g.memset(blockm[0:DH, 0:DH], 1.0))
            link(g.memset(blockm[DH:P, DH:P], 1.0))
            link(g.affine_select(out=tri[:, :], in_=ones[:, :], compare_op=ALU.is_ge, fill=0.0,
                                 base=-1, pattern=[[1, P]], channel_multiplier=-1))
            link(g.memset(ltri[:, :, :], 1.0))
            link(g.affine_select(out=ltri[:, :, :], in_=ltri[:, :, :], compare_op=ALU.is_ge, fill=0.0,
                                 base=-1, pattern=[[1, E0], [-1, E0]], channel_multiplier=0))
            link(g.memset(spread[:, :, :], 1.0))
            link(g.affine_select(out=spread[:, :, :], in_=spread[:, :, :], compare_op=ALU.is_ge, fill=0.0,
                                 base=0, pattern=[[P, FC], [1, P]], channel_multiplier=-DH))
            link(g.affine_select(out=spread[:, :, :], in_=spread[:, :, :], compare_op=ALU.is_ge, fill=0.0,
                                 base=DH - 1, pattern=[[-P, FC], [-1, P]], channel_multiplier=DH))
            link(g.memset(later[:, :], 1.0))
            link(g.affine_select(out=later[:, :], in_=later[:, :], compare_op=ALU.is_ge, fill=0.0,
                                 base=-1, pattern=[[0, 1]], channel_multiplier=1))
            link(g.memset(Xf[:, :, :], 0.0))
            link(g.iota(idx[:, :], [[P, PC]], base=0, channel_multiplier=1, allow_small_or_imprecise_dtypes=True))
            link(g.memset(ge[:, :, :], 0.0))
            g.memset(comb[:, :, E0:E0 + 1], 0.5).then_inc(S["made"], 1)
            with g.Fori(1, ET // BUFS) as i:
                for b in range(BUFS):
                    targets_low(bass.ds(i * BUFS + b, 1), b, i * BUFS + b)
            for b in range(LAST):
                targets_low(slice(ET - LAST + b, ET - LAST + b + 1), b, ET - LAST + b)
            g.wait_ge(S["deg"], 1)
            g.tensor_tensor(deg[:, 1, :], deg[:, 1, :], mhalf[:, :], ALU.pow).then_inc(S["degp"], 1)
            for n in range(2, 6):
                power(n)

            g.wait_ge(S["dk_ps"], 2)
            g.wait_ge(S["dv_ps"], 2)
            g.memset(kz[:, :, :], 0.0).then_inc(S["zeroed"], 1)
            g.wait_ge(S["pv"], 1)
            for h in range(HEADS):
                if h >= 2:
                    g.wait_ge(S["scan"], h - 1)
                g.tensor_tensor(zb[:, h % 2, :, :], ident[:, :].rearrange("p (o t) -> p o t", o=1).to_broadcast([P, PC, P]),
                                pv[:, :, h:h + 1].to_broadcast([P, PC, P]), ALU.mult).then_inc(S["zb"], 1)
            g.wait_ge(S["scan"], HEADS)
            link(g.memset(T_n[:, :], 0.0))
            g.memset(T_n[:, 0:B * B].rearrange("p (r) -> p r")[:, 0:B * B:B + 1], 1.0).then_inc(S["zeroed"], 1)
            g.wait_ge(S["kp_ps"], 2 * FC)
            g.memset(T_a[:, :], 0.0).then_inc(S["zeroed"], 1)
            g.wait_ge(S["dbeta"], 1)
            for h in range(HEADS):
                g.wait_ge(S["qk"], h + 1)
                g.tensor_tensor(MT[:, h, :], MT[:, h, :], qkb[h % 2], ALU.mult).then_inc(S["mt"], 1)
            g.memset(XT[:, :, :], 0.0).then_inc(S["zeroed"], 1)
            g.wait_ge(S["ktm_ps"], PC)
            g.wait_ge(S["mt"], HEADS)
            for j in range(PAIR_HEADS):
                g.wait_ge(S["crow"], j + 1)
                if j % 2:
                    v = (T_b, T_c)[j // 2][:, :].rearrange("p (a c t) -> p c a t", a=2, c=PC)
                    g.tensor_copy(cend[:, :, j - 1:j + 1], v[:, :, :, P - 1]).then_inc(S["cend"], 1)
                for z in range(2):
                    g.tensor_tensor(kp[:, j, z, :], kp[:, j, z, :], crow(j), ALU.mult).then_inc(S["kqc"], 1)

        @block.tensor
        def _(pe):
            mm, tp = nc.tensor.matmul, nc.tensor.transpose

            def weight(u):
                pe.wait_ge(S["w%d" % (u % SLOTS)], 16 * (u // SLOTS + 1))

            def to_fm(src, b0, b1, name):
                for k in range(FC):
                    for c in range(NC):
                        last = tp((b0, b1)[k // 2][:, (k % 2) * N + c * P:(k % 2) * N + (c + 1) * P],
                                  src[:, c, k * P:(k + 1) * P], ident[:, :])
                    if k % 2:
                        last.then_inc(S[name], 1)

            def turn(src, b, ready, m, c):
                pe.wait_ge(S[ready[0]], ready[1] + c + 1)
                for k in range(FC):
                    last = tp(bank[b][:, k * P:(k + 1) * P], src[:, c, k * P:(k + 1) * P], ident[:, :])
                last.then_inc(S["turned_ps"], 1)
                pe.wait_ge(S["turned"], NC * m + c + 1)

            def to_tm(src, b0, b1, name):
                for c in range(NC):
                    for k in range(FC):
                        last = tp((b0, b1)[c][:, k * P:(k + 1) * P], src[:, k, c * P:(c + 1) * P], ident[:, :])
                    last.then_inc(S[name], 1)

            def half_ready(ready, k):
                if ready is not None and k % 2 == 0:
                    pe.wait_ge(S[ready[0]], ready[1] + k // 2 + 1)

            def proj_chunk(act, u, b, name, c, ready=None):
                if c == 0:
                    weight(u)
                for k in range(FC):
                    half_ready(ready, k)
                    last = mm(b[:, :], act[:, k, c * P:(c + 1) * P], wslot(u)[:, k, :], start=(k == 0), stop=(k == FC - 1))
                last.then_inc(S[name], 1)

            def proj_tm(act, u, b0, b1, name, ready=None):
                for c in range(NC):
                    proj_chunk(act, u, (b0, b1)[c], name, c, ready if c == 0 else None)

            def proj_fm(act, u, b0, b1, name, ready=None):
                weight(u)
                for o in range(FC):
                    for k in range(FC):
                        half_ready(ready if o == 0 else None, k)
                        last = mm((b0, b1)[o // 2][:, (o % 2) * N:(o % 2 + 1) * N], wslot(u)[:, k, o * P:(o + 1) * P],
                                  act[:, k, :], start=(k == 0), stop=(k == FC - 1))
                    if o % 2:
                        last.then_inc(S[name], 1)

            def attention_in(src, banks, normed, m, uq, uk, uv):
                for c in range(NC):
                    turn(src, banks[c], ("normed", NC * normed), m, c)
                    proj_chunk(fm(F_a), uq, bank[2 + c], "q_ps", c)
                attention_kv(uk, uv)

            def attention_kv(uk, uv):
                proj_fm(fm(F_a), uk, bank[4], bank[5], "k_ps")
                proj_tm(fm(F_a), uv, bank[6], bank[7], "v_ps")

            def attention_core(l):
                pe.wait_ge(S["ek"], l * 4 + 4)
                to_tm(fm(F_c), bank[4], bank[5], "ekt_ps")
                pe.wait_ge(S["qs"], l * 2 + 2)
                to_fm(tm(T_b), bank[2], bank[3], "qT_ps")
                pe.wait_ge(S["v"], l * 2 + 2)
                pe.wait_ge(S["ekt"], l * 2 + 2)
                for j in range(FC):
                    for c in range(NC):
                        last = mm(bank[6][:, j * P:(j + 1) * P], tm(T_c)[:, c, j * P:(j + 1) * P],
                                  tm(T_d)[:, c, j * P:(j + 1) * P], start=(c == 0), stop=(c == NC - 1))
                last.then_inc(S["ctx_ps"], 1)
                pe.wait_ge(S["ctx"], l + 1)
                pe.wait_ge(S["qT"], l * 2 + 2)
                for j in range(FC):
                    last = mm(bank[4 + j // 2][:, (j % 2) * N:(j % 2 + 1) * N], ctxs[:, j, :], fm(F_b)[:, j, :],
                              start=True, stop=True)
                    if j % 2:
                        last.then_inc(S["oT_ps"], 1)

            def keep_clock(b, n):
                for _ in range(n):
                    mm(bank[b][:, :], zer[:, 0:P], zer[:, :], start=True, stop=True)

            def x64(c):
                lo, hi = slice(0, 2 * B), slice(2 * B, P)
                pe.wait_ge(S["t64"], c + 1)
                pe.wait_ge(S["xt32"], 4)
                if c >= 2:
                    pe.wait_ge(S["xt64"], c - 1)
                for h in range(HEADS):
                    last = mm(bank[4 + c % 2][lo, h * DH:(h + 1) * DH], Xf[hi, c * HEADS + h, :],
                              XT[hi, c * HEADS + h, hi], start=True, stop=True)
                last.then_inc(S["x64_ps"], 1)

            pe.wait_ge(S["made"], 2)
            for c in range(NC):
                mm(bank[c][:, :], zer[:, 0:P], zer[:, :], start=True, stop=False, skip_group_check=True)

            def edge_tile(b, tile):
                pe.wait_ge(S["dst_dve"], tile + 1)
                pe.wait_ge(S["dst_act"], tile + 1)
                pe.wait_ge(S["dst_pool"], tile + 1)
                for c in range(NC):
                    for part in range(2):
                        last = mm(bank[c][:, :], src1h[:, b, c * P:(c + 1) * P],
                                  dst1h[:, b, part, :, :], start=False, stop=False, skip_group_check=True)
                last.then_inc(S["adj_tile"], 1)

            for b in range(BUFS):
                edge_tile(b, b)

            keep_clock(7, 8)
            pe.wait_ge(S["made"], 5)
            pe.wait_ge(S["normed"], 4)
            to_fm(tm(T_a), bank[2], bank[3], "turned_ps")
            proj_tm(fm(F_a), U_Q0, bank[2], bank[3], "q_ps", ("turned", 0))
            attention_kv(U_K0, U_V0)

            with pe.Fori(1, ET // BUFS) as i:
                for b in range(BUFS):
                    edge_tile(b, i * BUFS + b)
            for b in range(LAST):
                edge_tile(b, ET - LAST + b)
            for c in range(NC):
                mm(bank[c][:, :], zer[:, 0:P], zer[:, :], start=False, stop=True,
                   skip_group_check=True).then_inc(S["adj_ps"], 1)

            attention_core(0)
            proj_tm(fm(F_a), U_O0, bank[2], bank[3], "mix_ps", ("oT", 0))

            pe.wait_ge(S["A0s"], 1)
            for dc in range(NC):
                for sc in range(NC):
                    last = tp(bank[7][:, dc * N + sc * P:dc * N + (sc + 1) * P], A0[:, sc, dc * P:(dc + 1) * P], ident[:, :])
            last.then_inc(S["AnT_ps"], 1)
            pe.wait_ge(S["AnT"], 1)
            for l in range(2):
                h = tm(T_n) if l == 0 else tm(T_b)
                if l == 1:
                    pe.wait_ge(S["h"], 2)
                for k in range(FC):
                    for dc in range(NC):
                        last = mm(bank[4 + k // 2][:, (k % 2) * N:(k % 2 + 1) * N], h[:, dc, k * P:(k + 1) * P],
                                  AnT[:, dc, :], start=(dc == 0), stop=(dc == NC - 1))
                    if k % 2:
                        last.then_inc(S["h1_ps"], 1)
                proj_fm(fm(F_b), (U_GCN0, U_GCN1)[l], bank[6], bank[7], "h2_ps", ("h1T", 2 * l))
                proj_tm(fm(F_c), (U_MLP0, U_MLP1)[l], bank[0], bank[1], "h3_ps", ("h2T", 2 * l))

            pe.wait_ge(S["gw_in"], 16)
            keep_clock(4, 8)
            for c in range(NC):
                turn(tm(T_a), 2 + c, ("normed", 3 * NC), 1, c)
                for k in range(FC):
                    last = mm(bank[4][:, c * E0:(c + 1) * E0], fm(F_a)[:, k, c * P:(c + 1) * P],
                              gw[:, k, G_WG:G_WG + E0], start=(k == 0), stop=(k == FC - 1))
                if c == 0:
                    keep_clock(0, 8)
            last.then_inc(S["gate_ps"], 1)
            proj_fm(fm(F_a), U_W1, bank[6], bank[7], "hid_ps")
            for k in range(FC):
                last = mm(bank[5][0:DH, 0:N], gw[:, k, G_WS1:G_WS1 + DH], fm(F_a)[:, k, :],
                          start=(k == 0), stop=(k == FC - 1))
            last.then_inc(S["hs_ps"], 1)
            pe.wait_ge(S["comb"], 1)
            for c in range(NC):
                last = tp(bank[4][0:E0 + 1, c * P:(c + 1) * P], comb[:, c, :], ident[:, :])
            last.then_inc(S["combT_ps"], 1)
            pe.wait_ge(S["combT"], 1)
            for o in range(FC):
                last = mm(bank[o // 2][:, (o % 2) * N:(o % 2 + 1) * N], spread[:, o, :], combT[:, :],
                          start=True, stop=True)
                if o % 2:
                    last.then_inc(S["combB_ps"], 1)
            pe.wait_ge(S["hw"], 2)
            pe.wait_ge(S["hsT"], 1)
            pe.wait_ge(S["ffn_in"], 32)
            weight(U_W2)
            for c in range(NC):
                for k in range(FC):
                    mm(bank[2 + c][:, :], fm(F_c)[:, k, c * P:(c + 1) * P], wslot(U_W2)[:, k, :], start=(k == 0), stop=False)
                mm(bank[2 + c][:, :], hsT[:, c * P:(c + 1) * P], ws2[:, :], start=False, stop=False)
                mm(bank[2 + c][:, :], combT[:, c * P:(c + 1) * P], b29[:, :], start=False, stop=True).then_inc(S["y_ps"], 1)

            attention_in(tm(T_n), (0, 1), 4, 2, U_Q1, U_K1, U_V1)
            pe.wait_ge(S["A1"], 1)
            for k in range(FC):
                for c in range(NC):
                    last = mm(bank[k // 2][:, (k % 2) * N:(k % 2 + 1) * N], tm(T_n)[:, c, k * P:(k + 1) * P],
                              A1[:, c, :], start=(c == 0), stop=(c == NC - 1))
                if k % 2:
                    last.then_inc(S["agg_ps"], 1)
            pe.wait_ge(S["aggT"], 2)
            keep_clock(0, 14)
            attention_core(1)
            pe.wait_ge(S["aggT"], 2)
            weight(U_AGG)
            weight(U_O1)
            for c in range(NC):
                for k in range(FC):
                    mm(bank[2 + c][:, :], fm(T_a)[:, k, c * P:(c + 1) * P], wslot(U_AGG)[:, k, :], start=(k == 0), stop=False)
                pe.wait_ge(S["oT"], 4)
                for k in range(FC):
                    last = mm(bank[2 + c][:, :], fm(F_a)[:, k, c * P:(c + 1) * P], wslot(U_O1)[:, k, :],
                              start=False, stop=(k == FC - 1))
                last.then_inc(S["mix_ps"], 1)

            for c in range(NC):
                turn(tm(T_n), c, ("normed", 5 * NC), 3, c)
                for k in range(FC):
                    last = mm(bank[2][:, c * 20:(c + 1) * 20], fm(F_a)[:, k, c * P:(c + 1) * P],
                              gw[:, k, G_SM:G_SM + 20], start=(k == 0), stop=(k == FC - 1))
                if c == NC - 1:
                    last.then_inc(S["sm_ps"], 1)
                proj_chunk(fm(F_a), U_DQ, bank[4 - c], "dq_ps", c)
            pe.wait_ge(S["sm"], 1)
            pe.wait_ge(S["sel"], 1)
            for c in range(NC):
                for kc in range(NC):
                    mm(bank[2][:, c * E1:(c + 1) * E1], ones[:, :], pre[:, kc, :], start=(kc == 0), stop=False)
                for kc in range(c + 1):
                    mm(bank[2][:, c * E1:(c + 1) * E1], (tri if kc == c else ones)[:, :], sel[:, kc, 0:E1],
                       start=False, stop=(kc == c))
            for kc in range(NC):
                last = mm(bank[2][:, 2 * E1:3 * E1], ones[:, :], pre[:, kc, :], start=(kc == 0), stop=(kc == NC - 1))
            last.then_inc(S["pos_ps"], 1)
            proj_tm(fm(F_a), U_DK, bank[5], bank[6], "dk_ps")
            proj_tm(fm(F_a), U_DV, bank[7], bank[0], "dv_ps")
            pe.wait_ge(S["perm"], 1)
            pe.wait_ge(S["silu"], 2)
            for p in range(PC):
                for c in range(NC):
                    last = mm(bank[3][:, p * 68:(p + 1) * 68], permf[:, c, p * P:(p + 1) * P],
                              vals[:, c, :, :], start=(c == 0), stop=(c == NC - 1))
            last.then_inc(S["vals_ps"], 1)
            keep_clock(1, 16)
            for n in range(2 * FC):
                k, at = n % FC, (2, 0)[n // FC]
                if k == 0:
                    pe.wait_ge(S["hi"], n // FC + 1)
                    pe.wait_ge(S["lo"], n // FC + 1)
                if n == 2:
                    pe.wait_ge(S["silu"], 4)
                if n == 5:
                    pe.wait_ge(S["silu"], 6)
                if n == 7:
                    pe.wait_ge(S["kp"], 1)
                for c in range(NC):
                    for part in range(2):
                        last = mm(bank[KP_BANKS[n]][:, :], tm2(split[:, at + part, :])[:, c, k * P:(k + 1) * P],
                                  perm[:, c, :], start=(c == 0 and part == 0), stop=(c == NC - 1 and part == 1))
                last.then_inc(S["kp_ps"], 1)
            pe.wait_ge(S["hi"], 3)
            pe.wait_ge(S["lo"], 3)
            for p in range(PC):
                pe.wait_ge(S["kp"], p + 2)
                for c in range(NC):
                    for part in range(2):
                        last = mm(bank[VP_BANKS[p]][:, :], perm[:, c, p * P:(p + 1) * P],
                                  tm2(split[:, 2 + part, :])[:, c, :],
                                  start=(c == 0 and part == 0), stop=(c == NC - 1 and part == 1))
                last.then_inc(S["vp_ps"], 1)
            for p in range(PC):
                if p % 2 == 0:
                    pe.wait_ge(S["kp"], 6 + p // 2)
                for c in range(NC):
                    last = tp(bank[(7, 0)[p // 2]][:, (p % 2) * N + c * P:(p % 2) * N + (c + 1) * P],
                              permf[:, c, p * P:(p + 1) * P], ident[:, :])
                if p % 2:
                    last.then_inc(S["vp_ps"], 1)
            pe.wait_ge(S["vp"], PC)
            pe.wait_ge(S["kp"], 8)
            pe.wait_ge(S["vp"], PC + 2)
            keep_clock(1, 10)
            pe.wait_ge(S["pv"], 1)

            pe.wait_ge(S["a0"], 1)
            pe.wait_ge(S["kz"], HEADS)
            for c in range(PC):
                last = tp(bank[6][0:HEADS, c * P:(c + 1) * P], a4[:, c, :], ident[:, :])
            last.then_inc(S["aT_ps"], 1)
            for h in range(HEADS):
                j = h // 2
                if h >= 2:
                    pe.wait_ge(S["scan"], h - 1)
                for c in range(PC):
                    last = tp(bank[h % 2][:, c * P:(c + 1) * P], a0[:, c, h:h + 1].to_broadcast([P, P]), ident[:, :])
                last.then_inc(S["arow"], 1)
                if h >= 2:
                    pe.wait_ge(S["at"], h - 1)
                for c in range(PC):
                    last = mm(bank[2 + h % 2][:, c * P:(c + 1) * P], kz[:, h, c * P:(c + 1) * P],
                              kp[:, j, 0, c * P:(c + 1) * P], start=True, stop=True)
                last.then_inc(S["kk_ps"], 1)
                if h % 2:
                    pe.wait_ge(S["cT"], 1)
                    if j >= 2:
                        pe.wait_ge(S["crow"], j - 1)
                    mm(bank[4 + j % 2][:, :], spread[0:HEADS, j, :], cT[:, :], start=True, stop=True)\
                        .then_inc(S["crow_ps"], 1)
            pe.wait_ge(S["at"], HEADS)
            pe.wait_ge(S["scan"], HEADS)
            for c in range(PC):
                for j in range(FC):
                    last = tp(bank[(2, 3, 0, 1)[c]][:, j * P:(j + 1) * P], kp[:, j, 0, c * P:(c + 1) * P], ident[:, :])
                last.then_inc(S["ktm_ps"], 1)
            pe.wait_ge(S["cT"], 1)
            for t in range(B):
                for q in range(NB):
                    r = slice(q * B, (q + 1) * B)
                    last = mm(bank[6 + t // 16][r, (t % 16) * B:(t % 16 + 1) * B], AT[r, :, q * B + t], ident[r, r],
                              start=True, stop=True)
                if t % 16 == 15:
                    last.then_inc(S["ab_ps"], 1)
            for h in range(HEADS):
                if h == 0:
                    pe.wait_ge(S["kd"], PC)
                elif h >= 2:
                    pe.wait_ge(S["qk"], h - 1)
                for c in range(PC):
                    last = mm(bank[h % 2][:, c * P:(c + 1) * P], kz[:, h, c * P:(c + 1) * P],
                              kp[:, h // 2, 1, c * P:(c + 1) * P], start=True, stop=True)
                last.then_inc(S["qk_ps"], 1)
            pe.wait_ge(S["ab"], 2)
            proj_tm(fm(F_a), U_DG, bank[6], bank[7], "dg_ps")
            pe.wait_ge(S["zeroed"], 2)
            for t in range(B):
                if t:
                    pe.wait_ge(S["xrow"], t)
                for q in range(NB):
                    r = slice(q * B, (q + 1) * B)
                    last = mm(bank[4 + t // 16][r, (t % 16) * HC:(t % 16 + 1) * HC], Xb[r, t, :], ident[r, r],
                              start=True, stop=True)
                if t % 16 == 15:
                    last.then_inc(S["xd_ps"], 1)
            pe.wait_ge(S["silu"], 8)
            pe.wait_ge(S["crow"], PAIR_HEADS)
            for blocks, at in (((0, 2), 6), ((1,), 2)):
                for s_ in range(B):
                    for q in blocks:
                        r = slice(q * B, (q + 1) * B)
                        last = mm(bank[at + s_ // 16][r, (s_ % 16) * HC:(s_ % 16 + 1) * HC], Xb[r, :, s_], ident[r, r],
                                  start=True, stop=True)
                    if s_ % 16 == 15:
                        last.then_inc(S["xf_ps"], 1)
            pe.wait_ge(S["xf"], 4)
            G = HC // 2
            for g_ in range(2):
                for n in range(G):
                    for qe in (0, 2):
                        re, ro = slice(qe * B, (qe + 1) * B), slice((qe + 1) * B, (qe + 2) * B)
                        last = mm(bank[g_][ro, n * B:(n + 1) * B], AT[re, g_ * G + n, ro], Xf[re, g_ * G + n, 0:B],
                                  start=True, stop=True)
                last.then_inc(S["t32_ps"], 1)
            pe.wait_ge(S["xd"], 8)
            pe.wait_ge(S["xf1"], 2)
            for g_ in range(2):
                pe.wait_ge(S["t32_act"], g_ + 1)
                pe.wait_ge(S["t32_dve"], g_ + 1)
                for n in range(G):
                    m = g_ * G + n
                    for qe in (0, 2):
                        re, ro = slice(qe * B, (qe + 1) * B), slice((qe + 1) * B, (qe + 2) * B)
                        mm(bank[2 + g_][re, n * B:(n + 1) * B], T32[ro, m, :], XT[ro, m, ro], start=True, stop=True)
                    last = mm(bank[4 + g_][B:2 * B, n * B:(n + 1) * B], XT[B:2 * B, m, B:2 * B], T32[B:2 * B, m, :],
                              start=True, stop=True)
                last.then_inc(S["x32_ps"], 1)
            lo, hi = slice(0, 2 * B), slice(2 * B, P)
            for c in range(PC):
                pe.wait_ge(S["x21"], c // 2 + 1)
                if c >= 2:
                    pe.wait_ge(S["xt32"], 4)
                for h in range(HEADS):
                    last = mm(bank[(6, 7, 2, 3)[c]][hi, h * DH:(h + 1) * DH], AT[lo, c * HEADS + h, hi],
                              Xf[lo, c * HEADS + h, :], start=True, stop=True)
                last.then_inc(S["t64_ps"], 1)
                if c:
                    x64(c - 1)
            x64(PC - 1)
            keep_clock(2, 3)
            def own_outputs(c, hs):
                for h in hs:
                    last = mm(bank[6 + c % 2][:, h * DH:(h + 1) * DH], MT[:, h, c * P:(c + 1) * P],
                              U[:, c % 2, h * DH:(h + 1) * DH], start=(c == 0), stop=True, skip_group_check=True)
                return last

            def to_tokens(c):
                pe.wait_ge(S["o_hi"], c + 1)
                pe.wait_ge(S["o_lo"], c + 1)
                for n in range(NC):
                    for part in range(2):
                        last = mm(bank[2 + n][:, :], permT(c)[:, n * P:(n + 1) * P], oparts[:, part, c % 2, :],
                                  start=(c == 0 and part == 0), stop=(c == PC - 1 and part == 1), skip_group_check=True)
                    if c == PC - 1:
                        last.then_inc(S["core_ps"], 1)
                if c < PC - 1:
                    last.then_inc(S["to_tokens"], 1)

            first, rest_ = range(0, HEADS // 2), range(HEADS // 2, HEADS)
            pe.wait_ge(S["mt"], HEADS)
            for c in range(PC):
                cs = slice(c * P, (c + 1) * P)
                if c:
                    pe.wait_ge(S["kqc"], 2 * PAIR_HEADS)
                    pe.wait_ge(S["st"], c)
                    for j in range(PAIR_HEADS):
                        last = mm(bank[0][:, j * P:(j + 1) * P], kp[:, j, 0, cs], St[:, c % 2, j, :], start=True, stop=True)
                    last.then_inc(S["ks_ps"], 1)
                    own_outputs(c - 1, rest_).then_inc(S["o_ps"], 1)
                    pe.wait_ge(S["rhs"], c)
                pe.wait_ge(S["xt64"], c + 1)
                if c:
                    pe.wait_ge(S["u"], c)
                for h in range(HEADS):
                    last = mm(bank[1][:, h * DH:(h + 1) * DH], XT[:, c * HEADS + h, :], vp[:, c, h * DH:(h + 1) * DH],
                              start=True, stop=True)
                last.then_inc(S["u_ps"], 1)
                if c:
                    if c >= 2:
                        pe.wait_ge(S["o_hi"], c - 1)
                        pe.wait_ge(S["o_lo"], c - 1)
                    for j in range(PAIR_HEADS):
                        last = mm(bank[6 + c % 2][:, j * P:(j + 1) * P], kp[:, j, 1, cs], St[:, c % 2, j, :], start=(j == 0),
                                  stop=False, skip_group_check=True)
                    last.then_inc(S["qs_ps"], 1)
                if c >= 2:
                    to_tokens(c - 2)
                pe.wait_ge(S["u"], c + 1)
                if c < PC - 1:
                    pe.wait_ge(S["xt64"], PC)
                    for j in range(PAIR_HEADS):
                        last = mm(bank[4][:, j * P:(j + 1) * P], kd[:, c, j * P:(j + 1) * P], U[:, c % 2, j * P:(j + 1) * P],
                                  start=True, stop=True)
                    last.then_inc(S["ku_ps"], 1)
                own_outputs(c, first)
            own_outputs(PC - 1, rest_).then_inc(S["o_ps"], 1)
            to_tokens(PC - 2)
            to_tokens(PC - 1)

            keep_clock(5, 20)
            for c in range(NC):
                turn(tm(T_a), c, ("core", 0), 4, c)
                proj_chunk(fm(F_a), U_DO, bank[4 + c], "fin_ps", c)

        @block.scalar
        def _(act):
            A = nc.scalar.activation

            def output_high(c):
                act.wait_ge(S["o_ps"], c + 1)
                if c >= 2:
                    act.wait_ge(S["to_tokens"], c - 1)
                A(oparts[:, 0, c % 2, :], bank[6 + c % 2][:, :], ACT.Copy, scale=pv[:, c, 16:17]).then_inc(S["o_hi"], 1)

            def high(part, tile):
                A(split[:, part, :], tile[:, :], ACT.Copy).then_inc(S["hi"], 1)

            def block_of(A, q, half):
                return A(*diagonal_block(q, half), ACT.Copy)

            def copy2(dst, b0, b1, ps, done, at=0):
                for c in range(2):
                    act.wait_ge(S[ps], at + c + 1)
                    A(dst[:, c * 512:(c + 1) * 512], (b0, b1)[c][:, :], ACT.Copy).then_inc(S[done], 1)

            def turned(b, m):
                for c in range(NC):
                    act.wait_ge(S["turned_ps"], NC * m + c + 1)
                    A(fm(F_a)[:, :, c * P:(c + 1) * P], bank[b + c][:, :].rearrange("p (k n) -> p k n", k=FC),
                      ACT.Copy).then_inc(S["turned"], 1)

            def adjacency_parts(t, b, tile):
                act.wait_ge(S["dst1"], tile + 1)
                A(dst1h[:, b, 0, 1, :], dst1[:, b, :], ACT.Copy, scale=ewh[:, 1, t].bitcast(F32))
                A(dst1h[:, b, 1, 0, :], dst1[:, b, :], ACT.Copy, scale=ewl[:, 0, t]).then_inc(S["dst_act"], 1)

            def attention(l):
                for c in range(NC):
                    act.wait_ge(S["qsub"], l * 2 + c + 1)
                    A(tm(T_b)[:, c, :], tm(T_b)[:, c, :], ACT.Exp).then_inc(S["qexp"], 1)
                for k in range(FC):
                    act.wait_ge(S["kmx"], l * 2 + k // 2 + 1)
                    A(fm(F_c)[:, k, :], bank[4 + k // 2][:, (k % 2) * N:(k % 2 + 1) * N], ACT.Exp,
                      bias=kmx[:, k:k + 1], accum_out=ksum[:, k:k + 1]).then_inc(S["ek"], 1)
                copy2(T_d, bank[6], bank[7], "v_ps", "v", 2 * l)
                if l == 0:
                    with act.Fori(1, ET // BUFS) as i:
                        for b in range(BUFS):
                            adjacency_parts(bass.ds(i * BUFS + b, 1), b, i * BUFS + b)
                    for b in range(LAST):
                        adjacency_parts(slice(ET - LAST + b, ET - LAST + b + 1), b, ET - LAST + b)
                copy2(T_c, bank[4], bank[5], "ekt_ps", "ekt", 2 * l)
                copy2(F_b, bank[2], bank[3], "qT_ps", "qT", 2 * l)
                copy2(F_a, bank[4], bank[5], "oT_ps", "oT", 2 * l)

            def table(fn, n):
                A(junk[:, n:n + 1], zer[:, 0:1], fn)

            act.wait_ge(S["made"], 2)
            table(ACT.Exp, 4)
            act.wait_ge(S["parts"], 1)
            for b in range(BUFS):
                adjacency_parts(slice(b, b + 1), b, b)
            act.wait_ge(S["cols_in"], 16)
            for k in range(FC):
                act.wait_ge(S["turned_ps"], k // 2 + 1)
                ins = A(fm(F_a)[:, k, :], bank[2 + k // 2][:, (k % 2) * N:(k % 2 + 1) * N], ACT.Copy,
                        scale=cols[:, C_GAMMA + k:C_GAMMA + k + 1])
                if k % 2:
                    ins.then_inc(S["turned"], 1)
            attention(0)
            for l in range(2):
                copy2(F_b, bank[4], bank[5], "h1_ps", "h1T", 2 * l)
                for k in range(FC):
                    act.wait_ge(S["h2_ps"], 2 * l + k // 2 + 1)
                    ins = A(fm(F_c)[:, k, :], bank[6 + k // 2][:, (k % 2) * N:(k % 2 + 1) * N], ACT.Identity,
                            bias=cols[:, C_GCN + 4 * l + k:C_GCN + 4 * l + k + 1])
                    if k % 2:
                        ins.then_inc(S["h2T"], 1)
            turned(2, 1)
            act.wait_ge(S["logits"], 1)
            A(gl[:, 1, :, :], gl[:, 1, :, :], ACT.Exp).then_inc(S["lexp"], 1)
            for k in range(FC):
                act.wait_ge(S["hid_ps"], k // 2 + 1)
                A(fm(F_b)[:, k, :], bank[6 + k // 2][:, (k % 2) * N:(k % 2 + 1) * N], ACT.Relu,
                  bias=cols[:, C_B1 + k:C_B1 + k + 1]).then_inc(S["hid"], 1)
            act.wait_ge(S["hs_ps"], 1)
            A(hsT[:, :], bank[5][0:DH, 0:N], ACT.Relu, bias=cols[0:DH, C_BS1:C_BS1 + 1]).then_inc(S["act_step"], 1)
            act.wait_ge(S["act_step"], 1)
            A(hsT[:, :], hsT[:, :], ACT.Copy, scale=0.5).then_inc(S["hsT"], 1)
            act.wait_ge(S["combT_ps"], 1)
            A(combT[:, :], bank[4][0:E0 + 1, 0:N], ACT.Copy).then_inc(S["combT"], 1)
            turned(0, 2)
            copy2(T_a, bank[0], bank[1], "agg_ps", "aggT")
            attention(1)
            turned(0, 3)
            act.wait_ge(S["sm_ps"], 1)
            A(sm[:, :, :], bank[2][:, 0:40].rearrange("p (c e) -> p c e", c=NC), ACT.Copy).then_inc(S["sm"], 1)
            act.wait_ge(S["logits"], 2)
            A(gl[:, 1, :, 0:E1], gl[:, 1, :, 0:E1], ACT.Exp).then_inc(S["lexp"], 1)
            act.wait_ge(S["aabs"], 1)
            A(dl[:, 1, :, :], dl[:, 1, :, :], ACT.Exp, scale=-1.0).then_inc(S["aexp"], 1)
            act.wait_ge(S["rows_in"], 16)
            A(dl[:, 2, 0, :], rows[:, R_ALOG:R_ALOG + HEADS], ACT.Exp).then_inc(S["alog"], 1)
            A(dl[:, 3, :, :], sm[:, :, 4:12], ACT.Sigmoid).then_inc(S["beta"], 1)
            def silu(b0, b1, tile, ps, squares=None, step=0):
                for c in range(NC):
                    act.wait_ge(S[ps], c + 1)
                    ins = A(tm(tile)[:, c, :], bank[(b0, b1)[c]][:, :], ACT.Silu)
                    if squares is not None:
                        ins.then_inc(S["act_step"], 1)
                        act.wait_ge(S["act_step"], step + c + 1)
                        ins = A(tm(squares)[:, c, :], tm(tile)[:, c, :], ACT.Square)
                    ins.then_inc(S["silu"], 1)

            silu(4, 3, T_a, "dq_ps", F_b, 1)
            silu(5, 6, T_b, "dk_ps", F_c, 3)
            table(ACT.Sqrt, 0)
            act.wait_ge(S["squares"], 1)
            A(hsum[:, :], hsum[:, :], ACT.Sqrt).then_inc(S["roots"], 1)
            act.wait_ge(S["squares"], 2)
            A(hmx[:, :], hmx[:, :], ACT.Sqrt).then_inc(S["roots"], 1)
            table(ACT.Silu, 1)
            act.wait_ge(S["normal"], 2)
            high(2, T_b)
            act.wait_ge(S["normal"], 4)
            high(0, T_a)
            silu(7, 0, T_c, "dv_ps")
            act.wait_ge(S["kp_ps"], FC)
            act.wait_ge(S["silu"], 6)
            high(2, T_c)
            table(ACT.Exp, 2)
            for n in range(8):
                act.wait_ge(S["kp_ps"], n + 1)
                A(kp[:, n % 4, n // 4, :], bank[KP_BANKS[n]][:, :], ACT.Copy).then_inc(S["kp"], 1)
            for p in range(PC):
                act.wait_ge(S["vp_ps"], p + 1)
                A(vp[:, p, :], bank[VP_BANKS[p]][:, :], ACT.Copy).then_inc(S["vp"], 1)
            for c in range(2):
                act.wait_ge(S["vp_ps"], PC + c + 1)
                A(split[:, 2, c * 512:(c + 1) * 512], bank[(7, 0)[c]][:, :], ACT.Copy)\
                    .then_inc(S["vp"], 1)
            act.wait_ge(S["pv"], 1)
            A(a4[:, :, :], pv[:, :, 8:16], ACT.Exp).then_inc(S["act_step"], 1)
            act.wait_ge(S["act_step"], 6)
            A(a0[:, :, :], a4[:, :, :], ACT.Copy, scale=later[:, 0:1]).then_inc(S["a0"], 1)
            for j in range(PAIR_HEADS):
                act.wait_ge(S["crow_ps"], j + 1)
                A(crow(j), bank[4 + j % 2][:, :], ACT.Copy).then_inc(S["crow"], 1)
            for b in range(2):
                act.wait_ge(S["ab_ps"], b + 1)
                A(F_c[:, b * 512:(b + 1) * 512], bank[6 + b][:, :], ACT.Copy).then_inc(S["ab"], 1)
            for h in range(HEADS):
                act.wait_ge(S["qk_ps"], h + 1)
                if h >= 2:
                    act.wait_ge(S["mt"], h - 1)
                A(qkb[h % 2], bank[h % 2][:, :], ACT.Copy).then_inc(S["qk"], 1)
            silu(6, 7, T_d, "dg_ps")
            table(ACT.Sqrt, 3)
            act.wait_ge(S["zeroed"], 4)
            act.wait_ge(S["xd_ps"], 1)
            for q in range(NB):
                block_of(A, q, 0).then_inc(S["xd"], 1)
            act.wait_ge(S["xf_ps"], 2)
            for q in (0, 2):
                A(*inverse_block(q, 1), ACT.Copy).then_inc(S["xf"], 1)
            for half in range(2):
                act.wait_ge(S["xf_ps"], 3 + half)
                A(*inverse_block(1, half), ACT.Copy).then_inc(S["xf1"], 1)
            for g_ in range(2):
                act.wait_ge(S["t32_ps"], g_ + 1)
                A(*t32_block(0, g_), ACT.Copy, scale=-1.0).then_inc(S["t32_act"], 1)
            for g_ in range(2):
                act.wait_ge(S["x32_ps"], g_ + 1)
                A(Xf[B:2 * B, g_ * HC // 2:(g_ + 1) * HC // 2, 0:B], bank[4 + g_][B:2 * B, :].rearrange("p (n s) -> p n s", s=B),
                  ACT.Copy).then_inc(S["x21"], 1)
            for c in range(PC):
                act.wait_ge(S["t64_ps"], c + 1)
                A(Xf[2 * B:P, c * HEADS:(c + 1) * HEADS, :],
                  bank[(6, 7, 2, 3)[c]][2 * B:P, :].rearrange("p (n s) -> p n s", n=HEADS), ACT.Copy, scale=-1.0)\
                    .then_inc(S["t64"], 1)
            for c in range(PC):
                act.wait_ge(S["u_ps"], c + 1)
                if c >= 2:
                    act.wait_ge(S["o_ps"], c - 1)
                A(U[:, c % 2, :], bank[1][:, :], ACT.Copy).then_inc(S["u"], 1)
                if c:
                    output_high(c - 1)
            output_high(PC - 1)
            for c in range(NC):
                act.wait_ge(S["core_ps"], c + 1)
                A(F_b[:, c * 512:(c + 1) * 512], bank[2 + c][:, :], ACT.Square).then_inc(S["core_sq"], 1)
            act.wait_ge(S["squares"], 3)
            A(hsum[:, :], hsum[:, :], ACT.Sqrt).then_inc(S["roots"], 1)
            turned(0, 4)

        @block.vector
        def _(dve):
            V = nc.vector
            count = [0]

            def link(ins):
                count[0] += 1
                ins.then_inc(S["dve_step"], 1)
                dve.wait_ge(S["dve_step"], count[0])

            def signal(ins, name, value):
                ins.then_inc(S[name], 1)
                dve.wait_ge(S[name], value)

            def variance(src, n, c):
                link(V.bn_stats(st[:, c, :], src))
                link(V.bn_aggr(mv[:, c, :], st[:, c, :]))
                signal(V.tensor_scalar(mv[:, c, 1:2], mv[:, c, 1:2], EPS, None, ALU.add), "var", NC * n + c + 1)

            def scaled(src, dst, n, c):
                dve.wait_ge(S["rstd"], NC * n + c + 1)
                signal(V.tensor_scalar(dst[:, c, :], src, mv[:, c, 0:1], rstd[:, c, 0:1],
                                       ALU.subtract, ALU.mult), "normed", NC * n + c + 1)

            def norm(src, dst, n, c):
                variance(src, n, c)
                scaled(src, dst, n, c)

            def heads(ap):
                return ap.rearrange("p (h d) -> p h d", h=HEADS)

            def per_head(t, c):
                return t[:, c * HEADS:(c + 1) * HEADS].rearrange("p (h o) -> p h o", o=1).to_broadcast([P, HEADS, DH])

            def attention_soft(l, scale):
                for c in range(NC):
                    dve.wait_ge(S["q_ps"], l * 2 + c + 1)
                    link(V.tensor_reduce(hmx[:, c * HEADS:(c + 1) * HEADS], heads(bank[2 + c][:, :]), AX, ALU.max))
                    signal(V.tensor_tensor(heads(tm(T_b)[:, c, :]), heads(bank[2 + c][:, :]), per_head(hmx, c),
                                           ALU.subtract), "qsub", l * 2 + c + 1)
                for b in range(2):
                    dve.wait_ge(S["k_ps"], l * 2 + b + 1)
                    link(V.tensor_reduce(kmx[:, 2 * b:2 * b + 2], bank[4 + b][:, :].rearrange("p (a n) -> p a n", a=2),
                                         AX, ALU.max))
                    signal(V.tensor_scalar(kmx[:, 2 * b:2 * b + 2], kmx[:, 2 * b:2 * b + 2], -1.0, None, ALU.mult),
                           "kmx", l * 2 + b + 1)
                for c in range(NC):
                    s = hsum[:, c * HEADS:(c + 1) * HEADS]
                    dve.wait_ge(S["qexp"], l * 2 + c + 1)
                    link(V.tensor_reduce(s, heads(tm(T_b)[:, c, :]), AX, ALU.add))
                    link(V.reciprocal(s, s))
                    if scale != 1.0:
                        link(V.tensor_scalar(s, s, scale, None, ALU.mult))
                    signal(V.tensor_tensor(heads(tm(T_b)[:, c, :]), heads(tm(T_b)[:, c, :]), per_head(hsum, c),
                                           ALU.mult), "qs", l * 2 + c + 1)

            def attention_ctx(l):
                dve.wait_ge(S["ek"], l * 4 + 4)
                link(V.reciprocal(ksum[:, :], ksum[:, :]))
                dve.wait_ge(S["ctx_ps"], l + 1)
                for j in range(FC):
                    ins = V.scalar_tensor_tensor(out=ctxs[:, j, :], in0=bank[6][:, j * P:(j + 1) * P],
                                                 scalar=ksum[:, j:j + 1], in1=blockm[:, :], op0=ALU.mult, op1=ALU.mult)
                ins.then_inc(S["ctx"], 1)

            def ranks(lg, e):
                lj = lg.rearrange("p c (o j) -> p c o j", o=1).to_broadcast([P, NC, e, e])
                li = lg.rearrange("p c (i o) -> p c i o", o=1).to_broadcast([P, NC, e, e])
                gt, eq = rk[:, 0, :, 0:e, 0:e], rk[:, 1, :, 0:e, 0:e]
                link(V.tensor_tensor(gt, lj, li, ALU.is_gt))
                link(V.tensor_tensor(eq, lj, li, ALU.is_equal))
                for c in range(NC):
                    link(V.tensor_tensor(rk[:, 1, c, 0:e, 0:e], rk[:, 1, c, 0:e, 0:e], ltri[:, 0:e, 0:e], ALU.mult))
                link(V.tensor_tensor(gt, gt, eq, ALU.add))
                for c in range(NC):
                    link(V.tensor_reduce(sel[:, c, 0:e], rk[:, 0, c, 0:e, 0:e], AX, ALU.add))
                link(V.tensor_scalar(sel[:, :, 0:e], sel[:, :, 0:e], 1.5, None, ALU.is_lt))

            def over(t, e):
                return t.rearrange("p (c o) -> p c o", o=1).to_broadcast([P, NC, e])

            dve.wait_ge(S["edges_in"], 32)
            link(V.tensor_copy(edge_f[:, :, :], edge_i[:, :, :]))
            link(V.tensor_copy(ewh[:, :, :], ew[:, :, :]))
            signal(V.tensor_tensor(ewl[:, :, :], ew[:, :, :], ewh[:, :, :].bitcast(F32), ALU.subtract), "parts", 1)
            dve.wait_ge(S["made"], 4)

            def targets(t, half, tile):
                V.tensor_scalar(dst1[:, half, :], iota_b[:, :], edge_f[:, 1, t], None, ALU.is_equal).then_inc(S["dst1"], 1)
                V.tensor_scalar(src1h[:, half, :], iota_b[:, :], edge_f[:, 0, t], None, ALU.is_equal)
                dve.wait_ge(S["dst1"], tile + 1)
                V.tensor_scalar(dst1h[:, half, 0, 0, :], dst1[:, half, :], ewh[:, 0, t].bitcast(F32), None, ALU.mult)\
                    .then_inc(S["dst_dve"], 1)

            for b in range(BUFS):
                targets(slice(b, b + 1), b, b)

            dve.wait_ge(S["x_in"], 16)
            for c in range(NC):
                variance(xs[:, c, :], 0, c)
            for c in range(NC):
                dve.wait_ge(S["rstd"], c + 1)
                link(V.tensor_tensor(mv[:, c, 1:2], rstd[:, c, :], rstd[:, c, :], ALU.mult))
                signal(V.tensor_scalar(mv[:, c, 1:2], mv[:, c, 1:2], -EPS, 1.0 + EPS, ALU.mult, ALU.add), "var", NC + c + 1)
            for c in range(NC):
                scaled(xs[:, c, :], tm(T_n), 0, c)
            for c in range(NC):
                dve.wait_ge(S["rstd"], NC + c + 1)
                link(V.tensor_tensor(rstd[:, c, :], rstd[:, c, :], rstd2[:, c, :], ALU.mult))
                scaled(xs[:, c, :], tm(T_a), 1, c)

            attention_soft(0, DH ** -0.5)

            with dve.Fori(1, ET // BUFS) as i:
                for b in range(BUFS):
                    dve.wait_ge(S["adj_tile"], i * BUFS - (BUFS - 1) + b)
                    targets(bass.ds(i * BUFS + b, 1), b, i * BUFS + b)
            for b in range(LAST):
                dve.wait_ge(S["adj_tile"], ET - LAST + b - (BUFS - 1))
                targets(slice(ET - LAST + b, ET - LAST + b + 1), b, ET - LAST + b)

            dve.wait_ge(S["made"], 6)
            attention_ctx(0)
            for c in range(NC):
                dve.wait_ge(S["adj_ps"], c + 1)
                link(V.tensor_copy(A0[:, c, :], bank[c][:, 0:N]))
                signal(V.tensor_copy(A1[:, c, :], bank[c][:, N:2 * N]), "A1c", c + 1)
                link(V.tensor_reduce(deg[:, 0, c:c + 1], A0[:, c, :], AX, ALU.add))
            V.tensor_scalar(deg[:, 2, :], deg[:, 0, :], 0.0, None, ALU.is_gt).then_inc(S["A1"], 1)
            signal(V.tensor_scalar(deg[:, 1, :], deg[:, 0, :], 1e-38, None, ALU.max), "deg", 1)
            dve.wait_ge(S["A1"], 1)
            dve.wait_ge(S["degp"], 1)
            link(V.tensor_tensor(deg[:, 3, :], deg[:, 1, :], deg[:, 2, :], ALU.mult))
            for c in range(NC):
                ins = V.tensor_scalar(A0[:, c, :], A0[:, c, :], deg[:, 3, c:c + 1], None, ALU.mult)
            ins.then_inc(S["A0s"], 1)
            dve.wait_ge(S["AnT_ps"], 1)
            for c in range(NC):
                ins = V.tensor_scalar(AnT[:, c, :], bank[7][:, c * N:(c + 1) * N], deg[:, 3, c:c + 1], None, ALU.mult)
            ins.then_inc(S["AnT"], 1)

            dve.wait_ge(S["rows_in"], 16)
            dve.wait_ge(S["mix_ps"], 2)
            for c in range(NC):
                norm(bank[2 + c][:, :], tm(T_a), 2, c)
                link(V.tensor_tensor(tm(T_a)[:, c, :], tm(T_a)[:, c, :], row(R_OG), ALU.mult))
                link(V.tensor_tensor(xs[:, c, :], xs[:, c, :], tm(T_a)[:, c, :], ALU.add))
            for l in range(2):
                for c in range(NC):
                    dve.wait_ge(S["h3_ps"], 2 * l + c + 1)
                    link(V.tensor_tensor(tm(T_c)[:, c, :], bank[c][:, :], row((R_MLP0, R_MLP1)[l]), ALU.add))
                    ins = V.scalar_tensor_tensor(out=tm(T_b)[:, c, :], in0=tm(T_c)[:, c, :], scalar=0.01,
                                                 in1=tm(T_c)[:, c, :], op0=ALU.mult, op1=ALU.max)
                    if l == 0:
                        ins.then_inc(S["h"], 1)
                    else:
                        link(ins)
                        link(V.tensor_tensor(xs[:, c, :], xs[:, c, :], tm(T_b)[:, c, :], ALU.add))
                        norm(xs[:, c, :], tm(T_a), 3, c)

            dve.wait_ge(S["gate_ps"], 1)
            g0, g1, g2 = gl[:, 0, :, :], gl[:, 1, :, :], gl[:, 2, :, :]
            bg = rows[:, R_BG:R_BG + E0].rearrange("p (o e) -> p o e", o=1).to_broadcast([P, NC, E0])
            link(V.tensor_tensor(g0, bank[4][:, 0:2 * E0].rearrange("p (c e) -> p c e", c=NC), bg, ALU.add))
            link(V.tensor_reduce(gmx[:, 0, :], g0, AX, ALU.max))
            signal(V.tensor_tensor(g1, g0, over(gmx[:, 0, :], E0), ALU.subtract), "logits", 1)
            ranks(g0, E0)
            dve.wait_ge(S["lexp"], 1)
            link(V.tensor_tensor(g1, g1, sel[:, :, 0:E0], ALU.mult))
            link(V.tensor_reduce(gmx[:, 1, :], g1, AX, ALU.add))
            link(V.reciprocal(gmx[:, 1, :], gmx[:, 1, :]))
            signal(V.tensor_tensor(comb[:, :, 0:E0], g1, over(gmx[:, 1, :], E0), ALU.mult), "comb", 1)
            dve.wait_ge(S["hid"], 4)
            for b in range(2):
                dve.wait_ge(S["combB_ps"], b + 1)
                V.tensor_tensor(F_c[:, b * 512:(b + 1) * 512], F_b[:, b * 512:(b + 1) * 512], bank[b][:, :],
                                ALU.mult).then_inc(S["hw"], 1)
            for c in range(NC):
                dve.wait_ge(S["y_ps"], c + 1)
                link(V.tensor_tensor(xs[:, c, :], xs[:, c, :], bank[2 + c][:, :], ALU.add))
                norm(xs[:, c, :], tm(T_n), 4, c)

            attention_soft(1, 1.0)
            attention_ctx(1)
            link(V.tensor_tensor(row(R_B1), row(R_B1), row(R_BOUT), ALU.add))
            for c in range(NC):
                link(V.tensor_tensor(xs[:, c, :], xs[:, c, :], row(R_B1), ALU.add))
            for c in range(NC):
                dve.wait_ge(S["mix_ps"], 2 + c + 1)
                link(V.tensor_tensor(xs[:, c, :], xs[:, c, :], bank[2 + c][:, :], ALU.add))
                norm(xs[:, c, :], tm(T_n), 5, c)

            dve.wait_ge(S["sm"], 1)
            s0, s1, w = gl[:, 0, :, 0:E1], gl[:, 1, :, 0:E1], gl[:, 2, :, 0:E1]
            link(V.tensor_reduce(gmx[:, 0, :], sm[:, :, 0:E1], AX, ALU.max))
            signal(V.tensor_tensor(s1, sm[:, :, 0:E1], over(gmx[:, 0, :], E1), ALU.subtract), "logits", 2)
            x_a, u_a, ea, beta = dl[:, 0, :, :], dl[:, 1, :, :], dl[:, 2, 0, :], dl[:, 3, :, :]
            s_a, s2, pl, sp_ = dl[:, 4, :, :], dl[:, 5, :, :], dl[:, 6, :, :], dl[:, 7, :, :]
            dtb = rows[:, R_DT:R_DT + HEADS].rearrange("p (o e) -> p o e", o=1).to_broadcast([P, NC, HEADS])
            link(V.tensor_tensor(x_a, sm[:, :, 12:20], dtb, ALU.add))
            signal(V.scalar_tensor_tensor(out=u_a, in0=x_a, scalar=-1.0, in1=x_a, op0=ALU.mult, op1=ALU.max), "aabs", 1)
            dve.wait_ge(S["lexp"], 2)
            link(V.tensor_reduce(gmx[:, 1, :], s1, AX, ALU.add))
            link(V.reciprocal(gmx[:, 1, :], gmx[:, 1, :]))
            link(V.tensor_tensor(s0, s1, over(gmx[:, 1, :], E1), ALU.mult))
            ranks(s0, E1)
            link(V.memset(pre[:, :, 0:1], 0.0))
            for e in range(1, E1):
                ins = V.tensor_tensor(pre[:, :, e], pre[:, :, e - 1], sel[:, :, e - 1], ALU.add)
                if e < E1 - 1:
                    link(ins)
            signal(ins, "sel", 1)
            link(V.tensor_tensor(w, s0, sel[:, :, 0:E1], ALU.mult))
            link(V.tensor_reduce(gmx[:, 1, :], w, AX, ALU.add))
            link(V.reciprocal(gmx[:, 1, :], gmx[:, 1, :]))
            link(V.tensor_tensor(w, w, over(gmx[:, 1, :], E1), ALU.mult))
            link(V.tensor_scalar(s1, w, 0.0, None, ALU.is_gt))
            dve.wait_ge(S["aexp"], 1)
            link(V.tensor_scalar(s_a, u_a, 2.0, None, ALU.add))
            link(V.reciprocal(s_a, s_a))
            link(V.tensor_tensor(s_a, s_a, u_a, ALU.mult))
            link(V.tensor_tensor(s2, s_a, s_a, ALU.mult))
            link(V.tensor_scalar(pl, s2, 1.0 / 17, None, ALU.mult))
            for k in range(15, 1, -2):
                link(V.scalar_tensor_tensor(out=pl, in0=pl, scalar=1.0 / k, in1=s2, op0=ALU.add, op1=ALU.mult))
            link(V.scalar_tensor_tensor(out=pl, in0=pl, scalar=1.0, in1=s_a, op0=ALU.add, op1=ALU.mult))
            link(V.tensor_scalar(sp_, x_a, 0.0, None, ALU.max))
            link(V.scalar_tensor_tensor(out=sp_, in0=pl, scalar=2.0, in1=sp_, op0=ALU.mult, op1=ALU.add))
            dve.wait_ge(S["alog"], 1)
            eab = ea.rearrange("p (o e) -> p o e", o=1).to_broadcast([P, NC, HEADS])
            link(V.scalar_tensor_tensor(out=sp_, in0=sp_, scalar=-1.0, in1=eab, op0=ALU.mult, op1=ALU.mult))
            link(V.tensor_scalar(sp_, sp_, -200.0, None, ALU.max))
            dve.wait_ge(S["beta"], 1)
            for c in range(NC):
                on = s1[:, c, :].rearrange("p (e o) -> p e o", o=1).to_broadcast([P, E1, HEADS])
                bb = beta[:, c, :].rearrange("p (o h) -> p o h", o=1).to_broadcast([P, E1, HEADS])
                gg = sp_[:, c, :].rearrange("p (o h) -> p o h", o=1).to_broadcast([P, E1, HEADS])
                link(V.tensor_tensor(vals[:, c, :, 0:8], bb, on, ALU.mult))
                link(V.tensor_tensor(vals[:, c, :, 8:16], gg, on, ALU.mult))
            link(V.tensor_copy(vals[:, :, :, 16], w))
            def squares(tile, ss, got, turn):
                for c in range(NC):
                    dve.wait_ge(S["silu"], got + c + 1)
                    link(V.tensor_reduce(ss[:, c * HEADS:(c + 1) * HEADS], heads(tm(tile)[:, c, :]), AX, ALU.add))
                signal(V.tensor_scalar(ss[:, :], ss[:, :], 1e-6, None, ALU.add), "squares", turn)

            squares(F_b, hsum, 0, 1)
            dve.wait_ge(S["pos_ps"], 1)
            p3 = bank[2][:, 0:2 * E1].rearrange("p (c e) -> p c e", c=NC)
            link(V.scalar_tensor_tensor(out=posm[:, :, :], in0=p3, scalar=1.0, in1=sel[:, :, 0:E1], op0=ALU.add, op1=ALU.mult))
            link(V.tensor_scalar(posm[:, :, :], posm[:, :, :], -1.0, None, ALU.add))
            for p in range(PC):
                link(V.tensor_scalar(ge[:, p, 0:E1], bank[2][:, 2 * E1:3 * E1], idx[:, p:p + 1], None, ALU.is_le))
            for p in range(PC):
                link(V.tensor_scalar(first[:, p, :], bank[2][:, 2 * E1:3 * E1], idx[:, p:p + 1], -200.0,
                                     ALU.is_equal, ALU.mult))
            link(V.tensor_reduce(forget[:, :], first[:, :, :], AX, ALU.min))
            link(V.tensor_tensor(oh[:, :, :], ge[:, :, 0:E1], ge[:, :, 1:E1 + 1], ALU.subtract))
            for e in range(E1):
                for c in range(NC):
                    if e == 0:
                        ins = V.tensor_scalar(perm[:, c, :], iota_f[:, :], posm[:, c, 0:1], None, ALU.is_equal)
                    else:
                        ins = V.scalar_tensor_tensor(out=perm[:, c, :], in0=iota_f[:, :], scalar=posm[:, c, e:e + 1],
                                                     in1=permf[:, c, :], op0=ALU.is_equal, op1=ALU.add)
                    if (e, c) != (E1 - 1, NC - 1):
                        link(ins)
            signal(ins, "perm", 1)
            squares(F_c, hmx, 2, 2)

            def low(part, tile, n):
                dve.wait_ge(S["hi"], n)
                V.tensor_tensor(split[:, part, :], tile[:, :], split[:, part - 1, :].bitcast(F32), ALU.subtract)\
                    .then_inc(S["lo"], 1)

            dve.wait_ge(S["roots"], 2)
            for t, ss, out, scale in ((T_b, hmx, 0, 1.0), (T_a, hsum, 2, DH ** -0.5)):
                link(V.reciprocal(ss[:, :], ss[:, :]))
                if scale != 1.0:
                    link(V.tensor_scalar(ss[:, :], ss[:, :], scale, None, ALU.mult))
                for c in range(NC):
                    signal(V.tensor_tensor(heads(tm(t)[:, c, :]), heads(tm(t)[:, c, :]), per_head(ss, c), ALU.mult), "normal", out + c + 1)
            low(3, T_b, 1)
            low(1, T_a, 2)
            dve.wait_ge(S["vals_ps"], 1)
            vps = bank[3][:, 0:PC * 68].rearrange("p (a e v) -> p a e v", a=PC, e=E1)
            for p in range(PC):
                link(V.tensor_tensor(vmask[:, p, :, :], vps[:, p, :, :],
                                     oh[:, p, :].rearrange("p (e o) -> p e o", o=1).to_broadcast([P, E1, 17]), ALU.mult))
            for p in range(PC):
                ins = V.tensor_reduce(pv[:, p, :], vmask[:, p, :, :].rearrange("p e v -> p v e"), AX, ALU.add)
            link(ins)
            for p in range(PC):
                ins = V.tensor_scalar(pv[:, p, 8:16], pv[:, p, 8:16], forget[:, p:p + 1], None, ALU.add)
            signal(ins, "pv", 1)
            low(3, T_c, 3)
            dve.wait_ge(S["zeroed"], 1)
            for h in range(HEADS):
                r = slice((h % 2) * DH, (h % 2 + 1) * DH)
                dve.wait_ge(S["kp"], h // 2 + 1)
                V.tensor_copy(kz[r, h, :], kp[r, h // 2, 0, :]).then_inc(S["kz"], 1)
            dve.wait_ge(S["aT_ps"], 1)
            for c in range(PC):
                ins = V.tensor_tensor_scan(cT[:, c * P:(c + 1) * P], bank[6][0:HEADS, c * P:(c + 1) * P],
                                           identz[0:HEADS, P:2 * P], 1.0, ALU.mult, ALU.add)
            ins.then_inc(S["cT"], 1)
            for h in range(HEADS):
                dve.wait_ge(S["arow"], h + 1)
                dve.wait_ge(S["zb"], h + 1)
                d4 = MT[:, h, :].rearrange("p (c t) -> p c t", c=PC)
                signal(V.tensor_tensor_scan(MT[:, h, :], bank[h % 2][:, :],
                                            T_n[:, (h % 2) * PAIRS:(h % 2 + 1) * PAIRS], 0.0, ALU.mult, ALU.add), "scan", h + 1)
                dve.wait_ge(S["kk_ps"], h + 1)
                V.tensor_tensor(AT.rearrange("p (c h) t -> p c h t", c=PC)[:, :, h, :], d4,
                                bank[2 + h % 2][:, :].rearrange("p (c t) -> p c t", c=PC), ALU.mult).then_inc(S["at"], 1)
                ins = V.tensor_copy(dbeta[:, :, h], d4[:, :, P - 1])
            signal(ins, "dbeta", 1)
            for c in range(PC):
                dve.wait_ge(S["ktm_ps"], c + 1)
                V.tensor_tensor(heads(kd[:, c, :]), heads(bank[(2, 3, 0, 1)[c]][:, :]),
                                dbeta[:, c, :].rearrange("p (h o) -> p h o", o=1).to_broadcast([P, HEADS, DH]), ALU.mult)\
                    .then_inc(S["kd"], 1)
            dve.wait_ge(S["ab"], 2)
            dve.wait_ge(S["zeroed"], 2)
            for s_ in range(B - 1):
                rest, w_ = B - 1 - s_, s_ + 1
                part = prodb[:, 0:rest * w_].rearrange("p (t c) -> p t c", t=rest)
                link(V.tensor_tensor(part, Ab[:, s_ + 1:B, s_:s_ + 1].to_broadcast([P, rest, w_]),
                                     Xb[:, s_:s_ + 1, 0:w_].to_broadcast([P, rest, w_]), ALU.mult))
                signal(V.tensor_tensor(Xb[:, s_ + 1:B, 0:w_], Xb[:, s_ + 1:B, 0:w_], part, ALU.subtract), "xrow", s_ + 1)
            dve.wait_ge(S["zeroed"], 4)
            dve.wait_ge(S["xd_ps"], 2)
            for q in range(NB):
                V.tensor_copy(*diagonal_block(q, 1)).then_inc(S["xd"], 1)
            dve.wait_ge(S["xf_ps"], 1)
            for q in (0, 2):
                V.tensor_copy(*inverse_block(q, 0)).then_inc(S["xf"], 1)
            for g_ in range(2):
                dve.wait_ge(S["t32_ps"], g_ + 1)
                V.tensor_scalar(*t32_block(2, g_), -1.0, None, ALU.mult).then_inc(S["t32_dve"], 1)
            for g_ in range(2):
                dve.wait_ge(S["x32_ps"], g_ + 1)
                for qe in (0, 2):
                    re, ro = slice(qe * B, (qe + 1) * B), slice((qe + 1) * B, (qe + 2) * B)
                    V.tensor_copy(XT[re, g_ * HC // 2:(g_ + 1) * HC // 2, ro],
                                  bank[2 + g_][re, :].rearrange("p (n s) -> p n s", s=B)).then_inc(S["xt32"], 1)
            for c in range(PC):
                dve.wait_ge(S["x64_ps"], c + 1)
                V.tensor_copy(XT[0:2 * B, c * HEADS:(c + 1) * HEADS, 2 * B:P],
                              bank[4 + c % 2][0:2 * B, :].rearrange("p (n s) -> p n s", n=HEADS)).then_inc(S["xt64"], 1)
            dve.wait_ge(S["zeroed"], 3)
            dve.wait_ge(S["cend"], 2)

            def output_low(c):
                dve.wait_ge(S["o_hi"], c + 1)
                V.scalar_tensor_tensor(out=oparts[:, 1, c % 2, :], in0=bank[6 + c % 2][:, :], scalar=pv[:, c, 16:17],
                                       in1=oparts[:, 0, c % 2, :].bitcast(F32), op0=ALU.mult, op1=ALU.subtract)\
                    .then_inc(S["o_lo"], 1)

            dve.wait_ge(S["silu"], 8)
            for c in range(NC):
                link(V.tensor_tensor(tm(T_d)[:, c, :], tm(T_d)[:, c, :], row(R_ON), ALU.mult))
            for c in range(PC):
                if c:
                    dve.wait_ge(S["ks_ps"], c)
                    V.tensor_tensor(vp[:, c, :], vp[:, c, :], bank[0][:, :], ALU.subtract).then_inc(S["rhs"], 1)
                if c == PC - 1:
                    break
                new = St[:, (c + 1) % 2, :, :]
                if c:
                    if c >= 2:
                        dve.wait_ge(S["qs_ps"], c - 1)
                    link(V.tensor_tensor(new, St[:, c % 2, :, :],
                                         cend[:, c, :].rearrange("p (j o) -> p j o", o=1).to_broadcast([P, PAIR_HEADS, P]),
                                         ALU.mult))
                    output_low(c - 1)
                dve.wait_ge(S["ku_ps"], c + 1)
                for hh in range(2):
                    r = slice(hh * DH, (hh + 1) * DH)
                    add = bank[4][r, :].rearrange("p (j v) -> p j v", j=PAIR_HEADS)[:, :, r]
                    ins = V.tensor_tensor(new[r, :, r], new[r, :, r], add, ALU.add)
                signal(ins, "st", c + 1)
            output_low(PC - 2)
            output_low(PC - 1)

            for c in range(NC):
                dve.wait_ge(S["core_sq"], c + 1)
                link(V.tensor_reduce(hsum[:, c * HEADS:(c + 1) * HEADS], heads(F_b[:, c * D:(c + 1) * D]), AX, ALU.add))
            signal(V.tensor_scalar(hsum[:, :], hsum[:, :], 1.0 / DH, EPS, ALU.mult, ALU.add), "squares", 3)
            for c in range(NC):
                link(V.tensor_tensor(tm(T_a)[:, c, :], bank[2 + c][:, :], tm(T_d)[:, c, :], ALU.mult))
            dve.wait_ge(S["roots"], 3)
            link(V.reciprocal(hsum[:, :], hsum[:, :]))
            for c in range(NC):
                V.tensor_tensor(heads(tm(T_a)[:, c, :]), heads(tm(T_a)[:, c, :]), per_head(hsum, c), ALU.mult)\
                    .then_inc(S["core"], 1)
            for c in range(NC):
                dve.wait_ge(S["fin_ps"], c + 1)
                V.tensor_tensor(xs[:, c, :], xs[:, c, :], bank[4 + c][:, :], ALU.add).then_inc(S["fin"], 1)


def kernel(**inputs):
    import numpy as np
    import concourse.bacc as bacc
    from concourse import mybir as mb
    from concourse.bass_utils import run_bass_kernel_spmd

    g = {k: np.asarray(v) for k, v in inputs.items()}

    def unit(w):
        return w.reshape(FC, P, D).transpose(1, 0, 2).reshape(P, UNIT)

    q0, k0, v0 = (g["L0_mix_w_qkv"][i * D:(i + 1) * D].T for i in range(3))
    q1, k1, v1 = (g["L1_mix_Wqkv"][i * D:(i + 1) * D].T for i in range(3))
    weights = [q0, k0, v0, g["L0_mix_w_out"].T, g["L0_gnn_W_gcn"][0], g["L0_gnn_W_mlp"][0], g["L0_gnn_W_gcn"][1],
               g["L0_gnn_W_mlp"][1], g["L0_ffn_W1"].transpose(1, 0, 2).reshape(D, D), g["L0_ffn_W2"].reshape(D, D),
               q1, k1, v1, g["L1_gnn_W"].T, g["L1_mix_Wout"].T, g["L1_ffn_Wq"], g["L1_ffn_Wk"], g["L1_ffn_Wv"],
               g["L1_ffn_Wg"], g["L1_ffn_Wo"]]
    rows = np.concatenate([g["L0_gnn_b_mlp"][0], g["L0_gnn_b_mlp"][1], g["L0_mix_out_gamma"], g["L1_gnn_b"],
                           g["L1_mix_bout"], np.tile(g["L1_ffn_o_norm_weight"], HEADS), g["L0_ffn_bg"],
                           g["L1_ffn_A_log"], g["L1_ffn_dt_bias"]])[None]
    cols = np.concatenate([g["L0_gnn_b_gcn"].reshape(8, P).T, g["L0_mix_norm_gamma"].reshape(4, P).T,
                           g["L0_ffn_b1"].reshape(4, P).T, np.tile(g["L0_ffn_bs1"], 2).reshape(P, 1)], axis=1)
    gw = np.concatenate([g["L0_ffn_Wg"], g["L0_ffn_Ws1"], g["L1_ffn_Wgate"], g["L1_ffn_Wb"], g["L1_ffn_Wa"]], axis=1)
    arrays = {
        "x": g["x"].reshape(NC, P, D).transpose(1, 0, 2),
        "edges": np.stack([g["src"], g["dst"]]).reshape(2, ET, P).transpose(2, 0, 1),
        "edge_weights": np.stack([g["edge_weight"], g["edge_weight1"][:, 0]]).reshape(2, ET, P).transpose(2, 0, 1),
        "weights": np.stack([unit(w) for w in weights]),
        "rows": rows,
        "cols": cols,
        "gw": gw.reshape(FC, P, GW).transpose(1, 0, 2),
        "b29": np.concatenate([g["L0_ffn_b2"], g["L0_ffn_bs2"][None]]),
        "ws2": g["L0_ffn_Ws2"],
    }
    nc = bacc.Bacc("TRN2", target_bir_lowering=False, num_devices=1)
    arrays = {"in_" + k: np.ascontiguousarray(v) for k, v in arrays.items()}
    args = [nc.dram_tensor(k, v.shape, mb.dt.from_np(v.dtype), kind="ExternalInput").ap() for k, v in arrays.items()]
    out = nc.dram_tensor("out", (P, NC, D), mb.dt.float32, kind="ExternalOutput").ap()
    build(nc, *args, out)
    r = run_bass_kernel_spmd(nc, [arrays], core_ids=[0])
    return np.asarray(r.results[0]["out"]).transpose(1, 0, 2).reshape(N, D)
```
